# Optimizing a Trainium2 kernel written in Bass

```python
import numpy as np
import jax
import jax.numpy as jnp

def _softmax(x, axis=-1):
    return jax.nn.softmax(x, axis=axis)

def _gelu(x):
    return jax.nn.gelu(x, approximate=True)

def _silu(x):
    return jax.nn.silu(x)

def _sigmoid(x):
    return jax.nn.sigmoid(x)

def _layernorm(x, axis=-1, eps=1e-05):
    m = jnp.mean(x, axis=axis, keepdims=True)
    v = jnp.var(x, axis=axis, keepdims=True)
    return (x - m) / jnp.sqrt(v + eps)

def _scatter_add(tgt, idx, src, axis=0):
    return tgt.at[idx].add(src)

def _segment_sum(src, seg, n):
    return jax.ops.segment_sum(src, seg, n)
kernel_name = 'mk_gnn_preln_d2_gnn_r64_0d249e'

def setup_inputs(seed: int=0):
    np.random.seed(seed)
    _w = jnp.asarray

    def _rec_inputs():
        import jax
        import jax.numpy as jnp
        _gk = jax.random.key(seed)
        x = -0.000202 + 1 * jax.random.normal(jax.random.fold_in(_gk, 1), (50000, 64), jnp.float32)
        src = jax.random.randint(jax.random.fold_in(_gk, 2), (25000,), 0, 50000, jnp.int32)
        dst = jax.random.randint(jax.random.fold_in(_gk, 3), (25000,), 0, 50000, jnp.int32)
        _o = jnp.argsort(dst, stable=True)
        src = src[_o]
        dst = dst[_o]
        edge_attr_64 = 0.000268479 + 0.999861 * jax.random.normal(jax.random.fold_in(_gk, 11), (25000, 64), jnp.float32)
        edge_weight = jax.random.uniform(jax.random.fold_in(_gk, 13), (25000,), jnp.float32, 0.0, 0.999995)
        return (x, src, dst, edge_attr_64, edge_weight)
    x, src, dst, edge_attr_64, edge_weight = _rec_inputs()

    def _L0_gnn_setup():
        import jax, jax.numpy as jnp
        import numpy as np
        N_NODES = 100000
        N_EDGES = 25000
        DIM = 64
        key = jax.random.key(seed)
        ks = jax.random.split(key, 5)
        x = jax.random.normal(ks[0], (N_NODES, DIM), dtype=jnp.float32)
        edge_index = jax.random.randint(ks[1], (2, N_EDGES), 0, N_NODES, dtype=jnp.int64)
        scale = 1.0 / np.sqrt(DIM)
        W1 = jax.random.normal(ks[2], (DIM, DIM), dtype=jnp.float32) * scale
        b1 = jnp.zeros((DIM,), dtype=jnp.float32)
        W2 = jax.random.normal(ks[3], (DIM, DIM), dtype=jnp.float32) * scale
        b2 = jnp.zeros((DIM,), dtype=jnp.float32)
        return {'x': x, 'edge_index': edge_index, 'W1': W1, 'b1': b1, 'W2': W2, 'b2': b2}
    _L0_gnn_all = _L0_gnn_setup()
    _L0_gnn_in = {k: v for k, v in _L0_gnn_all.items() if k in ('W1', 'b1', 'W2', 'b2')}
    del _L0_gnn_all

    def _L1_gnn_setup():
        import jax, jax.numpy as jnp
        import numpy as np
        N, E, HID, HEADS, KHOPS = (10000, 2500, 64, 8, 3)
        D = HID // HEADS
        key = jax.random.key(seed)
        ks = jax.random.split(key, 8)
        s = 1.0 / np.sqrt(HID)
        return {'x': jax.random.normal(ks[0], (N, HID), jnp.float32), 'edge_index': jax.random.randint(ks[1], (2, E), 0, N), 'edge_feature': jax.random.normal(ks[2], (E, HID), jnp.float32), 'edge_weight': jax.random.uniform(ks[3], (E,), jnp.float32), 'Wq': jax.random.normal(ks[4], (HID, HID), jnp.float32) * s, 'bq': jnp.zeros((HID,), jnp.float32), 'Wk': jax.random.normal(ks[5], (HID, HID), jnp.float32) * s, 'bk': jnp.zeros((HID,), jnp.float32), 'Wv': jax.random.normal(ks[6], (HID, HID), jnp.float32) * s, 'bv': jnp.zeros((HID,), jnp.float32), 'hopwise': jnp.ones((KHOPS + 1,), jnp.float32)}
    _L1_gnn_all = _L1_gnn_setup()
    _L1_gnn_in = {k: v for k, v in _L1_gnn_all.items() if k in ('Wq', 'bq', 'Wk', 'bk', 'Wv', 'bv', 'hopwise')}
    del _L1_gnn_all
    return {'x': x, 'src': src, 'dst': dst, 'edge_attr_64': edge_attr_64, 'edge_weight': edge_weight, 'L0_gnn_W1': _L0_gnn_in['W1'], 'L0_gnn_b1': _L0_gnn_in['b1'], 'L0_gnn_W2': _L0_gnn_in['W2'], 'L0_gnn_b2': _L0_gnn_in['b2'], 'L1_gnn_Wq': _L1_gnn_in['Wq'], 'L1_gnn_bq': _L1_gnn_in['bq'], 'L1_gnn_Wk': _L1_gnn_in['Wk'], 'L1_gnn_bk': _L1_gnn_in['bk'], 'L1_gnn_Wv': _L1_gnn_in['Wv'], 'L1_gnn_bv': _L1_gnn_in['bv'], 'L1_gnn_hopwise': _L1_gnn_in['hopwise']}

def reference(x, src, dst, edge_attr_64, edge_weight, L0_gnn_W1, L0_gnn_b1, L0_gnn_W2, L0_gnn_b2, L1_gnn_Wq, L1_gnn_bq, L1_gnn_Wk, L1_gnn_bk, L1_gnn_Wv, L1_gnn_bv, L1_gnn_hopwise):
    import jax
    import jax.numpy as jnp

    def _L0_gnn_ref(x, edge_index, W1, b1, W2, b2):
        import jax, jax.numpy as jnp
        import numpy as np
        N_NODES = 100000
        N_EDGES = 25000
        DIM = 64
        src, dst = (edge_index[0], edge_index[1])
        msg = jax.nn.relu(x[src])
        agg = jax.ops.segment_sum(msg, dst, num_segments=x.shape[0])
        h = (1.0 + 0.0) * x + agg
        h = jax.nn.relu(h @ W1 + b1) @ W2 + b2
        return jax.nn.relu(h)

    def _L1_gnn_ref(x, edge_index, edge_feature, edge_weight, Wq, bq, Wk, bk, Wv, bv, hopwise):
        import jax, jax.numpy as jnp
        import numpy as np
        N, E, HID, HEADS, KHOPS = (10000, 2500, 64, 8, 3)
        D = HID // HEADS
        n = x.shape[0]
        row, col = (edge_index[0], edge_index[1])
        deg = jax.ops.segment_sum(jnp.ones_like(edge_weight), col, num_segments=n)
        deg_inv = jnp.where(deg > 0, deg ** (-0.5), 0.0)
        norm = deg_inv[row] * deg_inv[col] * edge_weight
        Q = jax.nn.relu(x @ Wq + bq).reshape(n, HEADS, D)
        K = (x @ Wk + bk).reshape(n, HEADS, D)
        V = (x @ Wv + bv).reshape(n, HEADS, D)
        ef = edge_feature.reshape(-1, HEADS, D)
        hidden = V * hopwise[0]
        sqrt_d = jnp.sqrt(jnp.asarray(D, x.dtype))
        for hop in range(KHOPS):
            if hop == 0:
                Kj = jax.nn.relu(K[row] + ef)
                msg = norm[:, None, None, None] * jnp.einsum('ehi,ehj->ehij', Kj, V[row])
                M = jax.ops.segment_sum(msg, col, num_segments=n)
                K = jax.ops.segment_sum(norm[:, None, None] * Kj, col, num_segments=n)
            else:
                M = jax.ops.segment_sum(norm[:, None, None, None] * M[row], col, num_segments=n)
                K = jax.ops.segment_sum(norm[:, None, None] * K[row], col, num_segments=n)
            H = jnp.einsum('nhi,nhij->nhj', Q, M)
            nrm = jnp.sqrt(jnp.sum((H / sqrt_d) ** 2, axis=-1))
            H = H / jnp.maximum(jnp.ones_like(nrm), nrm)[..., None]
            hidden = hidden + hopwise[hop + 1] * H
        return hidden.reshape(n, HEADS * D)
    edge_index = jnp.stack([src, dst])
    h = jnp.maximum(_layernorm(x, axis=-1), 0.0)
    x = x + _L0_gnn_ref(h, edge_index, L0_gnn_W1, L0_gnn_b1, L0_gnn_W2, L0_gnn_b2)
    h = jnp.maximum(_layernorm(x, axis=-1), 0.0)
    x = x + _L1_gnn_ref(h, edge_index, edge_attr_64, edge_weight, L1_gnn_Wq, L1_gnn_bq, L1_gnn_Wk, L1_gnn_bk, L1_gnn_Wv, L1_gnn_bv, L1_gnn_hopwise)
    return x

_drawn_inputs = setup_inputs


def setup_inputs(seed=0):
    import zlib

    import numpy as np

    out = dict(_drawn_inputs(seed))
    spreads = {'L0_gnn_b1': (0.0, 0.1),
     'L0_gnn_b2': (0.0, 0.1),
     'L1_gnn_bq': (0.0, 0.549),
     'L1_gnn_bk': (0.0, 0.8),
     'L1_gnn_bv': (0.0, 0.1),
     'L1_gnn_hopwise': (1.0, 0.582)}
    factors = {}
    for name, (base, spread) in spreads.items():
        noise = np.random.default_rng([zlib.crc32(name.encode()), seed]).standard_normal(out[name].shape)
        drawn = base * np.exp(spread * noise) if base else spread * noise
        out[name] = jnp.asarray(drawn.astype(out[name].dtype))
    for name, factor in factors.items():
        out[name] = (out[name] * factor).astype(out[name].dtype)
    return out
```

```python
from contextlib import ExitStack

import numpy as np

import concourse.bass as bass
from concourse import mybir

F32 = mybir.dt.float32
I32 = mybir.dt.int32
U32 = mybir.dt.uint32
ALU = mybir.AluOpType
ACT = mybir.ActivationFunctionType
AX = mybir.AxisListType

P = 128
N = 50000
E = 25000
D = 64
HEADS, HD = 8, 8
MW = HEADS * HD * HD
HOPS = 3
EPS = 1e-5

EP = 125
T = E // EP
XT = T
SLOTS = T * P
AW = D + 1
TW = D + 2
NO_ROW = 1 << 20

NT = 16
NG = 25
GSTEP = (N - NT * P) // (NG - 1)
HT = NT // 2
ET = T // NG
EH = ET // 2

MG, MT = 5, 4
MTURN = MG * MT
POST = 3
PT_ = (T + 1) // POST


def passed(eng, sem, value, note):
    eng.wait_ge(sem, value)
    eng.sem_inc(note, 1)


class Chain:

    def __init__(self, eng, sem, base):
        self.eng, self.sem, self.base, self.n = eng, sem, base, 0

    def step(self, ins):
        ins.then_inc(self.sem, 1)
        self.n += 1

    def wait(self):
        self.eng.wait_ge(self.sem, self.base + self.n)


def gnn(nc, x, src, dst, edge_attr, edge_weight, W1, b1, W2, b2, Wq, bq, Wk, bk, Wv, bv, hopwise,
        mats, slots, out):
    dram = {
        "table": nc.dram_tensor("node_table", (N, TW), F32, kind="Internal").ap(),
        "M0": nc.dram_tensor("state_hop0", (SLOTS, MW), F32, kind="Internal").ap(),
        "M1": nc.dram_tensor("state_hop1", (SLOTS, MW), F32, kind="Internal").ap(),
    }
    with ExitStack() as ctx:
        def sb(name, shape, dt=F32):
            return ctx.enter_context(nc.sbuf_tensor(name, shape, dt))

        s = {}
        s["ident"] = sb("ident", [P, P])
        s["W1"] = sb("W1_two", [P, P])
        s["W2"] = sb("W2_two", [P, P])
        s["Wv"] = sb("Wv_two", [P, P])
        s["Wvq"] = sb("Wvq_two", [P, 2 * P])
        s["Wkv"] = sb("Wkv", [P, P])
        s["b1"] = sb("b1_col", [P, 1])
        s["b2"] = sb("b2_row", [1, P])
        s["bv"] = sb("bv_row", [1, P])
        s["bvq"] = sb("bvq_row", [1, P])
        s["bkv"] = sb("bkv_row", [1, P])
        s["ones"] = sb("ones_row", [1, P])
        s["hop"] = sb("hop_factors", [P, HOPS + 1])
        s["carry"] = sb("carry", [P, P])
        s["carryT"] = sb("carryT", [P, P])
        s["same"] = sb("same_as_before", [P, T])
        s["notlast"] = sb("not_last_here", [P, T])
        s["islast"] = sb("last_here", [P, T])
        s["fix"] = sb("carried_sums", [P, 2, AW])
        s["acc_end"] = sb("state_of_last_column", [P, MW])
        s["first"] = sb("in_first_segment", [P, T])
        s["trail"] = sb("in_last_segment", [P, T])
        s["src"] = sb("src_index", [P, T + ET], I32)
        s["dst"] = sb("dst_index", [P, T + ET], I32)
        s["dst_end"] = sb("dst_at_segment_end", [P, T], I32)
        s["dst_out"] = sb("dst_for_output", [P, T], I32)
        s["dst_x"] = sb("dst_for_extra_column", [P, 1], I32)
        s["slot_x"] = sb("slot_of_first_segment", [P, 1], I32)
        s["w"] = sb("edge_weight_cols", [P, T])
        s["wn"] = sb("norm_hop12", [P, T])
        s["sidx"] = sb("state_slot_of_src", [P, T + ET], I32)
        s["slots"] = sb("slot_ids", [P, T])
        s["AG"] = sb("sums", [P, T + 2, AW])
        s["HID"] = sb("hidden", [P, T + 1, D])

        prepare(nc, s, src, dst, edge_weight, W1, b1, W2, b2, Wq, bq, Wk, bk, Wv, bv, hopwise,
                mats, slots)
        nodes_and_gathers(nc, s, dram, x, out)
        complete_sums(nc, s)
        s["Q"] = sb("queries", [P, T, D])
        edge_mlp(nc, s, dram)
        hop_zero(nc, s, dram, edge_attr)
        hop_end(nc, s, dram, 0)
        hop_next(nc, s, dram, 1)
        hop_end(nc, s, dram, 1)
        hop_next(nc, s, dram, 2)
        hop_end(nc, s, dram, 2)
        write_out(nc, s, out)


def repeated(row, n):
    return row[:, :].unsqueeze(1).to_broadcast([1, n, P])


def running_sum(vec, s, t, width):
    now = s["AG"][:, bass.ds(t + 1, 1), 0:width]
    return vec.scalar_tensor_tensor(now, s["AG"][:, bass.ds(t, 1), 0:width],
                                    s["same"][:, bass.ds(t, 1)], now, ALU.mult, ALU.add)


def prepare(nc, s, src, dst, edge_weight, W1, b1, W2, b2, Wq, bq, Wk, bk, Wv, bv, hopwise, mats,
            slots):
    with ExitStack() as ctx:
        def sb(name, shape, dt=F32):
            return ctx.enter_context(nc.sbuf_tensor(name, shape, dt))

        def sem(name):
            return ctx.enter_context(nc.semaphore(name))

        later = sb("col_after_row", [P, P])
        shift = sb("row_after_col", [P, P])
        dstf = sb("dst_float", [P, T])
        nextf = sb("dst_of_next_partition", [P, 1])
        dif = sb("dst_differs", [P, T])
        lastf = sb("is_segment_end", [P, T])
        tmp = sb("prep_tmp", [P, T])
        tmp2 = sb("prep_tmp2", [P, T])
        len1 = sb("first_segment_length", [P, 1])
        ends = sb("first_segment_ends_here", [P, 1])
        col = sb("prep_col", [P, 2])
        pfirst = ctx.enter_context(nc.psum_tensor("p_first_row", [P, 512], F32))
        pnext = ctx.enter_context(nc.psum_tensor("p_next", [P, 512], F32))
        loaded, cleared, v, pe, rows = (sem("prep_loaded"), sem("prep_cleared"), sem("prep_vec"),
                                        sem("prep_pe"), sem("prep_rows"))
        block = ctx.enter_context(nc.Block())
        n_loads = 0

        @block.sync
        def _(sync):
            nonlocal n_loads
            sync.wait_ge(cleared, 1)
            loads = [(s["src"][0:EP, 0:T], src.rearrange("(p t) -> p t", t=T)),
                     (s["dst"][0:EP, 0:T], dst.rearrange("(p t) -> p t", t=T)),
                     (s["w"][0:EP, :], edge_weight.rearrange("(p t) -> p t", t=T)),
                     (s["ident"][:, :], mats[:, 0:P]), (later[:, :], mats[:, P:2 * P]),
                     (shift[:, :], mats[:, 2 * P:3 * P]), (s["slots"][:, :], slots),
                     (s["hop"][:, :], hopwise.unsqueeze(0).to_broadcast([P, HOPS + 1]))]
            loads += [(s["Wkv"][0:D, 0:D], Wk), (s["Wkv"][0:D, D:2 * D], Wv)]
            for k in range(2):
                r, c = slice(k * D, k * D + D), k * D
                loads += [(s["W1"][r, c:c + D], W1), (s["W2"][r, c:c + D], W2),
                          (s["Wv"][r, c:c + D], Wv),
                          (s["Wvq"][r, 2 * c:2 * c + D], Wv), (s["Wvq"][r, 2 * c + D:2 * c + 2 * D], Wq),
                          (s["b1"][r, :], b1.unsqueeze(1))]
            for j in range(2):
                r = slice(j * D, j * D + D)
                even = j % 2 == 0
                loads += [(s["b2"][:, r], b2.unsqueeze(0)), (s["bv"][:, r], bv.unsqueeze(0)),
                          (s["bvq"][:, r], (bv if even else bq).unsqueeze(0)),
                          (s["bkv"][:, r], (bk if even else bv).unsqueeze(0))]
            for to, what in loads:
                sync.dma_start(to, what).then_inc(loaded, 16)
            n_loads = len(loads)
            sync.wait_ge(loaded, 16 * n_loads)
            sync.sem_inc(rows, 1)

        @block.tensor
        def _(ten):
            ten.wait_ge(v, 2)
            ten.matmul(pfirst[:, 0:P], dstf[:, 0:1].to_broadcast([P, P]), s["ident"][:, :],
                       start=True, stop=True).then_inc(pe, 1)
            ten.matmul(pnext[:, 0:1], shift[:, :], dstf[:, 0:1], start=True, stop=True).then_inc(pe, 1)
            ten.wait_ge(v, 6)
            ten.transpose(pfirst[:, P:2 * P], s["carry"][:, :], s["ident"][:, :]).then_inc(pe, 1)

        @block.vector
        def _(vec):
            for k in ("W1", "W2", "Wv", "Wvq", "Wkv", "w"):
                vec.memset(s[k][:, :], 0.0)
            vec.memset(s["src"][:, :], 0)
            vec.memset(s["dst"][:, :], -1)
            vec.memset(s["sidx"][:, :], 0)
            vec.memset(s["ones"][:, :], 1.0)
            vec.memset(s["AG"][:, :, :], 1.0)
            vec.memset(s["HID"][:, :, :], 0.0).then_inc(cleared, 1)
            vec.wait_ge(cleared, 1)
            vec.wait_ge(rows, 1)
            n = [0]

            def step(ins):
                ins.then_inc(v, 1)
                n[0] += 1
                vec.wait_ge(v, n[0])

            dstt = dstf
            step(vec.tensor_copy(dstt[:, :], s["dst"][:, 0:T]))
            step(vec.tensor_scalar(s["wn"][:, :], s["w"][:, :], 0.0, None, ALU.mult))
            vec.wait_ge(pe, 2)
            step(vec.tensor_copy(nextf[:, :], pnext[:, 0:1]))
            step(vec.tensor_tensor(dif[:, 0:T - 1], dstt[:, 0:T - 1], dstt[:, 1:T], ALU.not_equal))
            step(vec.tensor_scalar(s["carry"][:, :], pfirst[:, 0:P], dstt[:, T - 1:T], None, ALU.is_equal))
            step(vec.tensor_tensor(s["carry"][:, :], s["carry"][:, :], later[:, :], ALU.mult))
            vec.wait_ge(pe, 3)
            step(vec.tensor_copy(s["carryT"][:, :], pfirst[:, P:2 * P]))
            step(vec.tensor_copy(lastf[:, 0:T - 1], dif[:, 0:T - 1]))
            step(vec.tensor_tensor(lastf[:, T - 1:T], dstt[:, T - 1:T], nextf[:, :], ALU.not_equal))
            step(vec.memset(s["same"][:, 0:1], 0.0))
            step(vec.tensor_scalar(s["same"][:, 1:T], dif[:, 0:T - 1], -1.0, 1.0, ALU.mult, ALU.add))
            step(vec.memset(s["notlast"][:, T - 1:T], 0.0))
            step(vec.tensor_scalar(s["notlast"][:, 0:T - 1], dif[:, 0:T - 1], -1.0, 1.0, ALU.mult, ALU.add))
            step(vec.tensor_scalar(s["islast"][:, :], s["notlast"][:, :], -1.0, 1.0, ALU.mult, ALU.add))
            step(vec.tensor_scalar(s["first"][:, :], dstt[:, :], dstt[:, 0:1], None, ALU.is_equal))
            step(vec.tensor_scalar(s["trail"][:, :], dstt[:, :], dstt[:, T - 1:T], None, ALU.is_equal))
            step(vec.tensor_reduce(len1[:, :], s["first"][:, :], AX.X, ALU.add))
            step(vec.tensor_scalar(col[:, 0:1], len1[:, :], float(P), float(-P), ALU.mult, ALU.add))
            step(vec.tensor_tensor(col[:, 1:2], col[:, 0:1], s["slots"][:, 0:1], ALU.add))
            step(vec.tensor_copy(s["slot_x"][:, :], col[:, 1:2]))
            step(vec.tensor_scalar(tmp[:, :], lastf[:, :], -float(NO_ROW), float(NO_ROW), ALU.mult, ALU.add))
            step(vec.tensor_tensor(tmp2[:, :], tmp[:, :], dstt[:, :], ALU.add))
            step(vec.tensor_copy(s["dst_end"][:, :], tmp2[:, :]))
            step(vec.tensor_scalar(tmp[:, :], s["first"][:, :], float(NO_ROW), None, ALU.mult))
            step(vec.tensor_tensor(tmp[:, :], tmp[:, :], tmp2[:, :], ALU.add))
            step(vec.tensor_copy(s["dst_out"][:, :], tmp[:, :]))
            step(vec.tensor_tensor(tmp[:, :], s["first"][:, :], lastf[:, :], ALU.mult))
            step(vec.tensor_reduce(ends[:, :], tmp[:, :], AX.X, ALU.add))
            step(vec.tensor_scalar(ends[:, :], ends[:, :], -float(NO_ROW), float(NO_ROW), ALU.mult, ALU.add))
            step(vec.tensor_tensor(ends[:, :], ends[:, :], dstt[:, 0:1], ALU.add))
            step(vec.tensor_copy(s["dst_x"][:, :], ends[:, :]))
            step(vec.tensor_scalar(s["Wv"][:, :], s["Wv"][:, :], s["hop"][:, 0:1], None, ALU.mult))
            for k in range(2):
                c = slice(2 * k * D, 2 * k * D + D)
                step(vec.tensor_scalar(s["Wvq"][:, c], s["Wvq"][:, c], s["hop"][:, 0:1], None, ALU.mult))
            step(vec.tensor_scalar(s["bv"][:, :], s["bv"][:, :], s["hop"][0:1, 0:1], None, ALU.mult))
            for c in (slice(0, D),):
                step(vec.tensor_scalar(s["bvq"][:, c], s["bvq"][:, c], s["hop"][0:1, 0:1], None, ALU.mult))


def nodes_and_gathers(nc, s, dram, x, out):
    with ExitStack() as ctx:
        def sb(name, shape, dt=F32):
            return ctx.enter_context(nc.sbuf_tensor(name, shape, dt))

        def ps(name):
            return ctx.enter_context(nc.psum_tensor(name, [P, HT * D], F32))

        def sem(name):
            return ctx.enter_context(nc.semaphore(name))

        H2 = range(2)
        C = HT + EH
        xn = [sb(f"x_nodes{h}", [P, HT, D]) for h in H2]
        gs = [sb(f"x_src{h}", [P, EH, D]) for h in H2]
        gd = [sb(f"x_dst{h}", [P, EH, D]) for h in H2]
        sq = [sb(f"squares{h}", [P, C, D]) for h in H2]
        h0 = [sb(f"h0_{h}", [P, HT, D]) for h in H2]
        hT = [sb(f"hT_{h}", [P, HT * D]) for h in H2]
        a1 = [sb(f"a1_{h}", [P, HT * D]) for h in H2]
        x1 = [sb(f"x1_{h}", [P, HT, D]) for h in H2]
        tab = [sb(f"table_rows{h}", [P, HT, TW]) for h in H2]
        res = [sb(f"out_rows{h}", [P, HT, D]) for h in H2]
        st = [sb(f"stats{h}", [P, 6, C]) for h in H2]
        st2 = [sb(f"stats_b{h}", [P, 6, HT]) for h in H2]
        isrc = [sb(f"src_now{h}", [P, EH], I32) for h in H2]
        idst = [sb(f"dst_now{h}", [P, EH], I32) for h in H2]
        pt = [ps(f"p_turned{h}") for h in H2]
        pa = [ps(f"p_mlp1_{h}") for h in H2]
        pb = [ps(f"p_mlp2_{h}") for h in H2]
        x_in = [sem(f"x_in{h}") for h in H2]
        stored = [sem(f"stored{h}") for h in H2]
        src_in = [sem(f"src_in{h}") for h in H2]
        dst_in = [sem(f"dst_in{h}") for h in H2]
        warm = sb("root_of_one", [1, 1])
        idx_set = sem("idx_set")
        dst_kept = sem("dst_kept")
        squared = sem("squared")
        rooted = sem("rooted")
        normed = sem("normed")
        normed2 = sem("normed2")
        act_copy = sem("act_copy")
        varred = sem("varred")
        scaled = sem("scaled")
        x1_done = sem("x1_done")
        res_done = sem("res_done")
        tab_done = sem("tab_done")
        turned = sem("turned")
        mm1 = sem("mm1")
        mm2 = sem("mm2")
        mm3 = sem("mm3")
        v = sem("vec_steps")
        note_p, note_s = sem("note_pool"), sem("note_sync")
        zeroed = sem("zeroed")
        block = ctx.enter_context(nc.Block())
        VSTEPS = 2 * (6 + 1 + EH) + 2 * (5 + 1)

        def rows(dram_t, i, h, w):
            a = dram_t[bass.ds(i * GSTEP, NT * P), :].rearrange("(p j) f -> p j f", j=NT)
            return a[:, h * HT:(h + 1) * HT, :]

        @block.sync
        def _(sync):
            for h in H2:
                sync.dma_start(xn[h][:, :, :], rows(x, 0, h, D)).then_inc(x_in[h], 16)

            def store(i, h):
                passed(sync, res_done, 2 * i + h + 1, note_s)
                passed(sync, tab_done, 2 * i + h + 1, note_s)
                passed(sync, stored[0], i * 32, note_s)
                passed(sync, stored[1], i * 32, note_s)
                sync.dma_start(rows(out, i, h, D), res[h][:, :, :]).then_inc(stored[h], 16)
                sync.dma_start(rows(dram["table"], i, h, TW), tab[h][:, :, :]).then_inc(stored[h], 16)

            with sync.Fori(0, NG - 1) as i:
                for h in H2:
                    passed(sync, x1_done, 2 * i + h + 1, note_s)
                    sync.dma_start(xn[h][:, :, :], rows(x, i + 1, h, D)).then_inc(x_in[h], 16)
                for h in H2:
                    store(i, h)
            for h in H2:
                store(NG - 1, h)
            for h in H2:
                sync.wait_ge(stored[h], 32 * NG)

        @block.gpsimd
        def _(pool):
            top = pool.to_reg(N - 1)
            with pool.Fori(0, NG) as i:
                for h in H2:
                    passed(pool, idx_set, 4 * i + 2 * h + 2, note_p)
                    for k in range(EH):
                        pool.indirect_dma_start(
                            out=gs[h][0:EP, k, :], out_offset=None, in_=x,
                            in_offset=bass.IndirectOffsetOnAxis(ap=isrc[h][0:EP, k:k + 1], axis=0),
                            bounds_check=top, oob_is_err=False).then_inc(src_in[h], 16)
                    for k in range(EH):
                        pool.indirect_dma_start(
                            out=gd[h][0:EP, k, :], out_offset=None, in_=x,
                            in_offset=bass.IndirectOffsetOnAxis(ap=idst[h][0:EP, k:k + 1], axis=0),
                            bounds_check=top, oob_is_err=False).then_inc(dst_in[h], 16)

        @block.scalar
        def _(act):
            act.wait_ge(zeroed, 1)
            act.activation(warm[:, :], s["ones"][:, 0:1], ACT.Sqrt)
            with act.Fori(0, NG) as i:
                act.wait_ge(tab_done, 2 * i)
                for h in H2:
                    act.wait_ge(x_in[h], 16 * i + 16)
                    act.activation(sq[h][:, 0:HT, :], xn[h][:, :, :], ACT.Square).then_inc(squared, 1)
                    act.wait_ge(src_in[h], 16 * EH * (i + 1))
                    act.activation(sq[h][:, HT:C, :], gs[h][:, :, :], ACT.Square).then_inc(squared, 1)
                for h in H2:
                    act.wait_ge(varred, 4 * i + h + 1)
                    act.activation(st[h][:, 3, :], st[h][:, 2, :], ACT.Sqrt).then_inc(rooted, 1)
                for h in H2:
                    act.wait_ge(scaled, 4 * i + h + 1)
                    for k in range(HT):
                        ins = act.activation(h0[h][:, k, :], xn[h][:, k, :], ACT.Relu,
                                             bias=st[h][:, 5, k:k + 1], scale=st[h][:, 4, k:k + 1])
                    ins.then_inc(normed, 1)
                    for k in range(EH):
                        t = i * ET + h * EH + k
                        ins = act.activation(s["AG"][:, bass.ds(t + 1, 1), 0:D], gs[h][:, k:k + 1, :], ACT.Relu,
                                             bias=st[h][:, 5, HT + k:HT + k + 1],
                                             scale=st[h][:, 4, HT + k:HT + k + 1])
                    ins.then_inc(normed, 1)
                act.wait_ge(mm3, 2 * i)
                for h in H2:
                    act.wait_ge(turned, 4 * i + h + 1)
                    act.activation(hT[h][:, :], pt[h][:, :], ACT.Copy).then_inc(act_copy, 1)
                for h in H2:
                    act.wait_ge(mm1, 2 * i + h + 1)
                    act.activation(a1[h][:, :], pa[h][:, :], ACT.Relu, bias=s["b1"][:, 0:1]).then_inc(act_copy, 1)
                for h in H2:
                    act.wait_ge(x1_done, 2 * i + h + 1)
                    act.activation(sq[h][:, 0:HT, :], x1[h][:, :, :], ACT.Square).then_inc(squared, 1)
                for h in H2:
                    act.wait_ge(varred, 4 * i + 2 + h + 1)
                    act.activation(st2[h][:, 3, :], st2[h][:, 2, :], ACT.Sqrt).then_inc(rooted, 1)
                for h in H2:
                    act.wait_ge(scaled, 4 * i + 2 + h + 1)
                    for k in range(HT):
                        ins = act.activation(h0[h][:, k, :], x1[h][:, k, :], ACT.Relu,
                                             bias=st2[h][:, 5, k:k + 1], scale=st2[h][:, 4, k:k + 1])
                    ins.then_inc(normed2, 1)
                for h in H2:
                    act.wait_ge(turned, 4 * i + 2 + h + 1)
                    act.activation(hT[h][:, :], pt[h][:, :], ACT.Copy).then_inc(act_copy, 1)

        @block.tensor
        def _(ten):
            def turn(h, what):
                for k in range(HT // 2):
                    ins = ten.transpose(pt[h][:, k * P:(k + 1) * P], what[:, 2 * k:2 * k + 2, :],
                                        s["ident"][:, :])
                ins.then_inc(turned, 1)

            def rows_out(h, lhs, w, bias, done):
                ten.matmul(pb[h][:, :], s["ones"][:, :], repeated(bias, HT // 2), start=True, stop=False,
                           skip_group_check=True)
                for k in range(HT // 2):
                    ins = ten.matmul(pb[h][:, k * P:(k + 1) * P], lhs[:, k * P:(k + 1) * P], w[:, :],
                                     start=False, stop=(k == HT // 2 - 1), skip_group_check=True)
                ins.then_inc(done, 1)

            with ten.Fori(0, NG) as i:
                for h in H2:
                    ten.wait_ge(normed, 4 * i + 2 * h + 1)
                    ten.wait_ge(act_copy, 6 * i)
                    turn(h, h0[h])
                for h in H2:
                    ten.wait_ge(act_copy, 6 * i + h + 1)
                    ten.matmul(pa[h][:, :], s["W1"][:, :], hT[h][:, :], start=True, stop=True).then_inc(mm1, 1)
                for h in H2:
                    ten.wait_ge(act_copy, 6 * i + 2 + h + 1)
                    ten.wait_ge(res_done, 2 * i)
                    rows_out(h, a1[h], s["W2"], s["b2"], mm2)
                for h in H2:
                    ten.wait_ge(normed2, 2 * i + h + 1)
                    turn(h, h0[h])
                for h in H2:
                    ten.wait_ge(act_copy, 6 * i + 4 + h + 1)
                    ten.wait_ge(x1_done, 2 * i + 2)
                    rows_out(h, hT[h], s["Wv"], s["bv"], mm3)

        @block.vector
        def _(vec):
            def set_index(h, i):
                cols = bass.ds(i * ET + h * EH, EH)
                vec.tensor_copy(isrc[h][:, :], s["src"][:, cols]).then_inc(idx_set, 1)
                vec.tensor_copy(idst[h][:, :], s["dst"][:, cols]).then_inc(idx_set, 1)

            for h in H2:
                vec.memset(gs[h][:, :, :], 0.0)
                vec.memset(gd[h][:, :, :], 0.0)
                vec.memset(tab[h][:, :, D:D + 1], 0.0)
                vec.memset(tab[h][:, :, D + 1:TW], float(NO_ROW))
            for h in H2:
                set_index(h, 0)
            vec.drain().then_inc(zeroed, 1)
            vec.wait_ge(zeroed, 1)
            with vec.Fori(0, NG) as i:
                ch = Chain(vec, v, i * VSTEPS)

                def stats(h, q, sqs, parts):
                    for a, b, what in parts:
                        ch.step(vec.tensor_reduce(q[h][:, 0, a:b], what, AX.X, ALU.add))
                    ch.step(vec.tensor_reduce(q[h][:, 1, :], sqs, AX.X, ALU.add))
                    ch.wait()
                    ch.step(vec.tensor_scalar(q[h][:, 0, :], q[h][:, 0, :], 1.0 / D, None, ALU.mult))
                    ch.wait()
                    ch.step(vec.tensor_tensor(q[h][:, 2, :], q[h][:, 0, :], q[h][:, 0, :], ALU.mult))
                    ch.wait()
                    ch.step(vec.scalar_tensor_tensor(q[h][:, 1, :], q[h][:, 1, :], 1.0 / D, q[h][:, 2, :],
                                                     ALU.mult, ALU.subtract))
                    ch.wait()
                    vec.tensor_scalar(q[h][:, 2, :], q[h][:, 1, :], 0.0, EPS, ALU.max, ALU.add).then_inc(varred, 1)

                def scales(h, q, k):
                    vec.wait_ge(rooted, 4 * i + k + h + 1)
                    ch.step(vec.reciprocal(q[h][:, 4, :], q[h][:, 3, :]))
                    ch.wait()
                    vec.scalar_tensor_tensor(q[h][:, 5, :], q[h][:, 0, :], -1.0, q[h][:, 4, :],
                                             ALU.mult, ALU.mult).then_inc(scaled, 1)

                for h in H2:
                    vec.wait_ge(x_in[h], 16 * i + 16)
                    vec.wait_ge(src_in[h], 16 * EH * (i + 1))
                    vec.wait_ge(squared, 6 * i + 2 * h + 2)
                    stats(h, st, sq[h][:, :, :], [(0, HT, xn[h][:, :, :]), (HT, C, gs[h][:, :, :])])
                for h in H2:
                    scales(h, st, 0)
                for h in H2:
                    vec.wait_ge(dst_in[h], 16 * EH * (i + 1))
                    vec.tensor_copy(s["HID"][:, bass.ds(i * ET + h * EH, EH), :], gd[h][:, :, :]).then_inc(dst_kept, 1)
                    vec.wait_ge(normed, 4 * i + 2 * h + 2)
                    vec.wait_ge(dst_kept, 2 * i + h + 1)
                    set_index(h, i + 1)
                    for k in range(EH):
                        ch.wait()
                        ch.step(running_sum(vec, s, i * ET + h * EH + k, AW))
                for h in H2:
                    vec.wait_ge(mm2, 2 * i + h + 1)
                    vec.scalar_tensor_tensor(x1[h][:, :, :].rearrange("p j f -> p (j f)"), pb[h][:, :], 0.0,
                                             xn[h][:, :, :].rearrange("p j f -> p (j f)"),
                                             ALU.max, ALU.add).then_inc(x1_done, 1)
                for h in H2:
                    vec.wait_ge(x1_done, 2 * i + h + 1)
                    vec.wait_ge(squared, 6 * i + 4 + h + 1)
                    stats(h, st2, sq[h][:, 0:HT, :], [(0, HT, x1[h][:, :, :])])
                for h in H2:
                    scales(h, st2, 2)
                for h in H2:
                    vec.wait_ge(stored[h], 32 * i)
                    vec.wait_ge(normed2, 2 * i + h + 1)
                    vec.tensor_copy(tab[h][:, :, 0:D], h0[h][:, :, :]).then_inc(tab_done, 1)
                for h in H2:
                    vec.wait_ge(mm3, 2 * i + h + 1)
                    vec.tensor_tensor(res[h][:, :, :].rearrange("p j f -> p (j f)"), pb[h][:, :],
                                      x1[h][:, :, :].rearrange("p j f -> p (j f)"),
                                      ALU.add).then_inc(res_done, 1)
                assert ch.n == VSTEPS, ch.n


def complete_sums(nc, s):
    with ExitStack() as ctx:
        pc = ctx.enter_context(nc.psum_tensor("p_carry", [P, 512], F32))
        pe = ctx.enter_context(nc.semaphore("carry_ready"))
        v = ctx.enter_context(nc.semaphore("back_steps"))
        note = ctx.enter_context(nc.semaphore("back_note"))
        block = ctx.enter_context(nc.Block())

        @block.tensor
        def _(ten):
            ten.matmul(pc[:, 0:AW], s["carry"][:, :], s["AG"][:, T, :], start=True, stop=True).then_inc(pe, 1)
            ten.wait_ge(v, 2 + T)
            ten.matmul(pc[:, P:P + AW], s["carryT"][:, :], s["AG"][:, 1, :], start=True, stop=True).then_inc(pe, 1)

        @block.vector
        def _(vec):
            vec.wait_ge(pe, 1)
            vec.tensor_copy(s["fix"][:, 0, :], pc[:, 0:AW]).then_inc(v, 1)
            vec.tensor_tensor(s["AG"][:, 1:T + 1, :], s["AG"][:, 1:T + 1, :],
                              s["islast"][:, :].unsqueeze(2).to_broadcast([P, T, AW]), ALU.mult).then_inc(v, 1)
            with vec.Fori(0, NG) as i:
                for k in range(ET):
                    t = (T - 1 - k) - i * ET
                    now = s["AG"][:, bass.ds(t + 1, 1), :]
                    passed(vec, v, i * ET + 2 + k, note)
                    vec.scalar_tensor_tensor(now, s["AG"][:, bass.ds(t + 2, 1), :], s["notlast"][:, bass.ds(t, 1)],
                                             now, ALU.mult, ALU.add).then_inc(v, 1)
            vec.wait_ge(pe, 2)
            vec.tensor_copy(s["fix"][:, 1, :], pc[:, P:P + AW]).then_inc(v, 1)


def edge_mlp(nc, s, dram):
    with ExitStack() as ctx:
        def sb(name, shape, dt=F32):
            return ctx.enter_context(nc.sbuf_tensor(name, shape, dt))

        def sem(name):
            return ctx.enter_context(nc.semaphore(name))

        G = range(MG)
        W = MT * D
        sq = [sb(f"m_squares{g}", [P, MT, D]) for g in G]
        h0 = [sb(f"m_h0_{g}", [P, MT, D]) for g in G]
        hT = [sb(f"m_hT_{g}", [P, W]) for g in G]
        a1 = [q[:, :, :].rearrange("p j f -> p (j f)") for q in sq]
        x1 = [sb(f"m_x1_{g}", [P, MT, D]) for g in G]
        tab = [sb(f"m_table_rows{g}", [P, MT, TW]) for g in G]
        st = [sb(f"m_stats{g}", [P, 6, 2 * MT]) for g in G]
        st2 = [sb(f"m_stats_b{g}", [P, 6, MT]) for g in G]
        ix = [sb(f"m_dst_now{g}", [P, MT], I32) for g in G]
        bank = [ctx.enter_context(nc.psum_tensor(f"m_bank{g}", [P, 512], F32)) for g in G]
        squared, rooted, varred, scaled = sem("m_squared"), sem("m_rooted"), sem("m_varred"), sem("m_scaled")
        normed, normed2, summed, copied = sem("m_normed"), sem("m_normed2"), sem("m_summed"), sem("m_copied")
        turned, mm1, mm2, mm3 = sem("m_turned"), sem("m_mm1"), sem("m_mm2"), sem("m_mm3")
        x1_done, hid_done, q_done, v = sem("m_x1"), sem("m_hid"), sem("m_q"), sem("m_vec_steps")
        tab_set = sem("m_tab_set")
        scattered = [sem(f"m_scattered{g}") for g in G]
        note, note_a = sem("m_note"), sem("m_note_a")
        block = ctx.enter_context(nc.Block())
        VS = MG * (2 * MT + 1 + 2 + 4 + 1 - 1 + 2 + 4)

        @block.gpsimd
        def _(pool):
            top = pool.to_reg(N - 1)
            with pool.Fori(0, T // MTURN) as i:
                for g in G:
                    passed(pool, tab_set, MG * 4 * i + 4 * g + 4, note)
                    for k in range(MT):
                        pool.indirect_dma_start(
                            out=dram["table"],
                            out_offset=bass.IndirectOffsetOnAxis(ap=ix[g][0:EP, k:k + 1], axis=0),
                            in_=tab[g][0:EP, k, :], in_offset=None,
                            bounds_check=top, oob_is_err=False).then_inc(scattered[g], 16)
            for g in G:
                pool.wait_ge(scattered[g], 16 * T // MG)

        @block.scalar
        def _(act):
            with act.Fori(0, T // MTURN) as i:
                def cols(g):
                    return bass.ds(i * MTURN + g * MT, MT)

                act.wait_ge(tab_set, 4 * MG * i)
                for g in G:
                    act.activation(sq[g][:, :, :], s["HID"][:, cols(g), :], ACT.Square).then_inc(squared, 1)
                for g in G:
                    act.wait_ge(varred, 2 * MG * i + g + 1)
                    act.activation(st[g][:, 3, :], st[g][:, 2, :], ACT.Sqrt).then_inc(rooted, 1)
                for g in G:
                    passed(act, scaled, 2 * MG * i + g + 1, note_a)
                    for k in range(MT):
                        ins = act.activation(h0[g][:, k:k + 1, :], s["HID"][:, bass.ds(i * MTURN + g * MT + k, 1), :],
                                             ACT.Relu, bias=st[g][:, 5, k:k + 1], scale=st[g][:, 4, k:k + 1])
                    ins.then_inc(normed, 1)
                for g in G:
                    act.wait_ge(turned, 2 * MG * i + g + 1)
                    act.activation(hT[g][:, :], bank[g][:, 0:W], ACT.Copy).then_inc(copied, 1)
                for g in G:
                    act.wait_ge(mm1, MG * i + g + 1)
                    act.activation(a1[g], bank[g][:, W:2 * W], ACT.Relu, bias=s["b1"][:, 0:1]).then_inc(copied, 1)
                for g in G:
                    act.wait_ge(x1_done, MG * i + g + 1)
                    act.activation(sq[g][:, :, :], x1[g][:, :, :], ACT.Square).then_inc(squared, 1)
                for g in G:
                    act.wait_ge(varred, 2 * MG * i + MG + g + 1)
                    act.activation(st2[g][:, 3, :], st2[g][:, 2, :], ACT.Sqrt).then_inc(rooted, 1)
                for g in G:
                    act.wait_ge(scaled, 2 * MG * i + MG + g + 1)
                    for k in range(MT):
                        ins = act.activation(h0[g][:, k, :], x1[g][:, k, :], ACT.Relu,
                                             bias=st2[g][:, 5, k:k + 1], scale=st2[g][:, 4, k:k + 1])
                    ins.then_inc(normed2, 1)
                for g in G:
                    act.wait_ge(turned, 2 * MG * i + MG + g + 1)
                    act.activation(hT[g][:, :], bank[g][:, 0:W], ACT.Copy).then_inc(copied, 1)
                for g in G:
                    act.wait_ge(mm3, MG * i + g + 1)
                    for k in range(MT):
                        ins = act.activation(s["Q"][:, bass.ds(i * MTURN + g * MT + k, 1), :],
                                             bank[g][:, k * 2 * D + D:(k + 1) * 2 * D].unsqueeze(1), ACT.Relu,
                                             scale=st[g][:, 4, MT + k:MT + k + 1])
                    ins.then_inc(q_done, 1)

        @block.tensor
        def _(ten):
            with ten.Fori(0, T // MTURN) as i:
                def turn(g, what):
                    for k in range(MT // 2):
                        ins = ten.transpose(bank[g][:, k * P:(k + 1) * P], what[:, 2 * k:2 * k + 2, :],
                                            s["ident"][:, :])
                    ins.then_inc(turned, 1)
                for g in G:
                    ten.wait_ge(summed, MG * i + g + 1)
                    ten.wait_ge(q_done, MG * i)
                    ten.wait_ge(hid_done, MG * i)
                    turn(g, h0[g])
                for g in G:
                    ten.wait_ge(copied, 3 * MG * i + g + 1)
                    ten.matmul(bank[g][:, W:2 * W], s["W1"][:, :], hT[g][:, :], start=True, stop=True).then_inc(mm1, 1)
                for g in G:
                    ten.wait_ge(copied, 3 * MG * i + MG + g + 1)
                    ten.matmul(bank[g][:, W:2 * W], s["ones"][:, :], repeated(s["b2"], MT // 2), start=True, stop=False,
                               skip_group_check=True)
                    for k in range(MT // 2):
                        ins = ten.matmul(bank[g][:, W + k * P:W + (k + 1) * P], a1[g][:, k * P:(k + 1) * P],
                                         s["W2"][:, :], start=False, stop=(k == MT // 2 - 1), skip_group_check=True)
                    ins.then_inc(mm2, 1)
                for g in G:
                    ten.wait_ge(normed2, MG * i + g + 1)
                    turn(g, h0[g])
                for g in G:
                    ten.wait_ge(copied, 3 * MG * i + 2 * MG + g + 1)
                    ten.matmul(bank[g][:, :], s["ones"][:, :], repeated(s["bvq"], MT), start=True, stop=False,
                               skip_group_check=True)
                    for k in range(MT // 2):
                        ins = ten.matmul(bank[g][:, k * 4 * D:(k + 1) * 4 * D], hT[g][:, k * P:(k + 1) * P],
                                         s["Wvq"][:, :], start=False, stop=(k == MT // 2 - 1), skip_group_check=True)
                    ins.then_inc(mm3, 1)

        @block.vector
        def _(vec):
            with vec.Fori(0, T // MTURN) as i:
                ch = Chain(vec, v, i * VS)

                def cols(g):
                    return bass.ds(i * MTURN + g * MT, MT)

                def stats(g, q, n, sqs, rows):
                    ch.step(vec.tensor_reduce(q[g][:, 0, 0:n], rows, AX.X, ALU.add))
                    ch.step(vec.tensor_reduce(q[g][:, 1, 0:n], sqs, AX.X, ALU.add))
                    ch.wait()
                    ch.step(vec.tensor_scalar(q[g][:, 0, 0:n], q[g][:, 0, 0:n], 1.0 / D, None, ALU.mult))
                    ch.wait()
                    ch.step(vec.tensor_tensor(q[g][:, 2, 0:n], q[g][:, 0, 0:n], q[g][:, 0, 0:n], ALU.mult))
                    ch.wait()
                    ch.step(vec.scalar_tensor_tensor(q[g][:, 1, 0:n], q[g][:, 1, 0:n], 1.0 / D, q[g][:, 2, 0:n],
                                                     ALU.mult, ALU.subtract))
                    ch.wait()
                    vec.tensor_scalar(q[g][:, 2, 0:n], q[g][:, 1, 0:n], 0.0, EPS, ALU.max, ALU.add).then_inc(varred, 1)

                def scales(g, q, n, m):
                    vec.wait_ge(rooted, 2 * MG * i + m + g + 1)
                    ch.step(vec.reciprocal(q[g][:, 4, :], q[g][:, 3, :]))
                    ch.wait()
                    vec.scalar_tensor_tensor(q[g][:, 5, 0:n], q[g][:, 0, 0:n], -1.0, q[g][:, 4, 0:n],
                                             ALU.mult, ALU.mult).then_inc(scaled, 1)

                for g in G:
                    for which, flags in ((0, "first"), (1, "trail")):
                        for k in range(MT):
                            t = i * MTURN + g * MT + k
                            now = s["AG"][:, bass.ds(t + 1, 1), :]
                            ch.step(vec.scalar_tensor_tensor(now, s["fix"][:, which:which + 1, :],
                                                             s[flags][:, bass.ds(t, 1)], now, ALU.mult, ALU.add))
                        ch.wait()
                    ch.step(vec.tensor_copy(st[g][:, 2, MT:2 * MT],
                                            s["AG"][:, bass.ds(i * MTURN + g * MT + 1, MT), D]))
                    vec.wait_ge(squared, 2 * MG * i + g + 1)
                    stats(g, st, MT, sq[g][:, :, :], s["HID"][:, cols(g), :])
                for g in G:
                    scales(g, st, MT, 0)
                for g in G:
                    vec.wait_ge(normed, MG * i + g + 1)
                    vec.tensor_tensor(h0[g][:, :, :], h0[g][:, :, :],
                                      s["AG"][:, bass.ds(i * MTURN + g * MT + 1, MT), 0:D], ALU.add).then_inc(summed, 1)
                for g in G:
                    vec.wait_ge(mm2, MG * i + g + 1)
                    vec.scalar_tensor_tensor(x1[g][:, :, :], bank[g][:, W:2 * W].rearrange("p (j f) -> p j f", f=D),
                                             0.0, s["HID"][:, cols(g), :], ALU.max, ALU.add).then_inc(x1_done, 1)
                for g in G:
                    vec.wait_ge(x1_done, MG * i + g + 1)
                    vec.wait_ge(squared, 2 * MG * i + MG + g + 1)
                    stats(g, st2, MT, sq[g][:, :, :], x1[g][:, :, :])
                for g in G:
                    scales(g, st2, MT, MG)
                for g in G:
                    vec.wait_ge(scattered[g], 16 * MT * i)
                    vec.wait_ge(normed2, MG * i + g + 1)
                    vec.tensor_copy(tab[g][:, :, 0:D], h0[g][:, :, :]).then_inc(tab_set, 1)
                    vec.tensor_copy(tab[g][:, :, D], st[g][:, 4, MT:2 * MT]).then_inc(tab_set, 1)
                    vec.tensor_copy(tab[g][:, :, D + 1], s["slots"][:, cols(g)]).then_inc(tab_set, 1)
                    vec.tensor_copy(ix[g][:, :], s["dst_end"][:, cols(g)]).then_inc(tab_set, 1)
                for g in G:
                    vec.wait_ge(q_done, MG * i + g + 1)
                    vec.tensor_tensor(s["HID"][:, cols(g), :],
                                      bank[g][:, :].rearrange("p (j f) -> p j f", f=2 * D)[:, :, 0:D],
                                      x1[g][:, :, :], ALU.add).then_inc(hid_done, 1)
                assert VS == ch.n, ch.n
            vec.wait_ge(hid_done, MG * (T // MTURN))
            vec.tensor_copy(s["HID"][:, T, :], s["HID"][:, 0, :]).then_inc(hid_done, 1)


def ihj(ap):
    return ap.rearrange("p (h i j) -> p h i j", h=HEADS, i=HD)


def state_rows(dram_t, t0):
    return dram_t[bass.ds(t0 * P, EH * P), :].rearrange("(j p) f -> p j f", p=P)


def hop_zero(nc, s, dram, edge_attr):
    with ExitStack() as ctx:
        def sb(name, shape, dt=F32):
            return ctx.enter_context(nc.sbuf_tensor(name, shape, dt))

        def sem(name):
            return ctx.enter_context(nc.semaphore(name))

        H2 = range(2)
        W = EH * D
        tg = [sb(f"z_table{h}", [P, EH, TW]) for h in H2]
        ef = [sb(f"z_edge{h}", [P, EH, D]) for h in H2]
        hT = [sb(f"z_hT{h}", [TW, EH * P]) for h in H2]
        kj = [sb(f"z_kj{h}", [P, EH, D]) for h in H2]
        vs = [sb(f"z_v{h}", [P, EH, D]) for h in H2]
        kq = [sb(f"z_kq{h}", [P, EH, D]) for h in H2]
        sc = [sb(f"z_s{h}", [P, EH * HEADS]) for h in H2]
        wn = [sb(f"z_wn{h}", [P, EH]) for h in H2]
        ix = [sb(f"z_src_now{h}", [P, EH], I32) for h in H2]
        pr = [sb(f"z_outer{k}", [P, MW]) for k in range(2)]
        acc = [sb(f"z_acc{h}", [P, EH, MW]) for h in H2]
        pt = [ctx.enter_context(nc.psum_tensor(f"z_turned{h}", [P, 512], F32)) for h in H2]
        pk = [ctx.enter_context(nc.psum_tensor(f"z_kv{h}", [P, 512], F32)) for h in H2]
        row_in = [sem(f"z_row_in{h}") for h in H2]
        ef_in = [sem(f"z_ef_in{h}") for h in H2]
        stored = [sem(f"z_stored{h}") for h in H2]
        idx_set, turned, copied, kv = sem("z_idx_set"), sem("z_turned_"), sem("z_copied"), sem("z_kv_")
        wn_set, k_sum, v_done, k_done = sem("z_wn_set"), sem("z_k_sum"), sem("z_v_done"), sem("z_k_done")
        acc_done, v, zeroed, note_p, note_s = (sem("z_acc_done"), sem("z_steps"), sem("z_zeroed"),
                                               sem("z_note_p"), sem("z_note_s"))
        block = ctx.enter_context(nc.Block())
        VS = 2 * (2 + 3 + EH + 2 * EH - EH)
        ef_rows = edge_attr.rearrange("(p t) f -> p t f", t=T)

        @block.sync
        def _(sync):
            def load(i, h):
                for a, b in ((0, 112), (112, EP)):
                    sync.dma_start(ef[h][a:b, :, :], ef_rows[a:b, bass.ds(i * ET + h * EH, EH), :]).then_inc(ef_in[h], 16)

            def store(i, h):
                passed(sync, acc_done, EH * (2 * i + h + 1), note_s)
                sync.dma_start(state_rows(dram["M0"], i * ET + h * EH), acc[h][:, :, :]).then_inc(stored[h], 16)

            sync.wait_ge(zeroed, 1)
            for h in H2:
                load(0, h)
            with sync.Fori(0, NG - 1) as i:
                for h in H2:
                    passed(sync, k_sum, 2 * i + h + 1, note_s)
                    load(i + 1, h)
                for h in H2:
                    store(i, h)
            for h in H2:
                store(NG - 1, h)
            for h in H2:
                sync.wait_ge(stored[h], 16 * NG)

        @block.gpsimd
        def _(pool):
            top = pool.to_reg(N - 1)
            with pool.Fori(0, NG) as i:
                for h in H2:
                    passed(pool, idx_set, 2 * i + h + 1, note_p)
                    for k in range(EH):
                        pool.indirect_dma_start(
                            out=tg[h][0:EP, k, :], out_offset=None, in_=dram["table"],
                            in_offset=bass.IndirectOffsetOnAxis(ap=ix[h][0:EP, k:k + 1], axis=0),
                            bounds_check=top, oob_is_err=False).then_inc(row_in[h], 16)

        @block.tensor
        def _(ten):
            ten.wait_ge(zeroed, 1)
            with ten.Fori(0, NG) as i:
                for h in H2:
                    ten.wait_ge(row_in[h], 16 * EH * (i + 1))
                    ten.wait_ge(copied, 2 * i)
                    for k in range(EH):
                        ins = ten.transpose(pt[h][0:TW, k * P:(k + 1) * P], tg[h][:, k, :], s["ident"][:, :])
                    ins.then_inc(turned, 1)
                for h in H2:
                    ten.wait_ge(copied, 2 * i + h + 1)
                    ten.wait_ge(k_sum, 2 * i)
                    ten.wait_ge(v_done, 2 * i)
                    ten.matmul(pk[h][:, :], s["ones"][:, :], repeated(s["bkv"], EH), start=True, stop=False,
                               skip_group_check=True)
                    for k in range(EH):
                        ins = ten.matmul(pk[h][:, k * P:(k + 1) * P], hT[h][:, k * P:(k + 1) * P],
                                         s["Wkv"][0:TW, :], start=False, stop=(k == EH - 1), skip_group_check=True)
                    ins.then_inc(kv, 1)

        @block.scalar
        def _(act):
            with act.Fori(0, NG) as i:
                for h in H2:
                    act.wait_ge(turned, 2 * i + h + 1)
                    act.activation(hT[h][:, :], pt[h][0:TW, :], ACT.Copy).then_inc(copied, 1)
                for h in H2:
                    act.wait_ge(kv, 2 * i + h + 1)
                    act.wait_ge(wn_set, 2 * i + h + 1)
                    act.wait_ge(acc_done, 2 * EH * i)
                    act.wait_ge(k_sum, 2 * i + h + 1)
                    for k in range(EH):
                        ins = act.activation(vs[h][:, k, :], pk[h][:, (2 * k + 1) * D:(2 * k + 2) * D], ACT.Copy,
                                             scale=wn[h][:, k:k + 1])
                    ins.then_inc(v_done, 1)
                    act.activation(kj[h][:, :, :], kj[h][:, :, :], ACT.Relu).then_inc(k_done, 1)

        @block.vector
        def _(vec):
            def set_index(h, i):
                vec.tensor_copy(ix[h][:, :], s["src"][:, bass.ds(i * ET + h * EH, EH)]).then_inc(idx_set, 1)

            for h in H2:
                vec.memset(tg[h][:, :, :], 0.0)
                vec.memset(ef[h][:, :, :], 0.0)
                vec.memset(acc[h][:, :, :], 0.0)
            vec.drain().then_inc(zeroed, 1)
            vec.wait_ge(zeroed, 1)
            for h in H2:
                set_index(h, 0)
            with vec.Fori(0, NG) as i:
                ch = Chain(vec, v, i * VS)
                for h in H2:
                    cols = bass.ds(i * ET + h * EH, EH)
                    vec.wait_ge(row_in[h], 16 * EH * (i + 1))
                    vec.tensor_tensor(wn[h][:, :], s["w"][:, cols], tg[h][:, :, D], ALU.mult).then_inc(wn_set, 1)
                    vec.wait_ge(wn_set, 2 * i + h + 1)
                    ch.step(vec.tensor_tensor(s["wn"][:, cols], wn[h][:, :], tg[h][:, :, D], ALU.mult))
                    ch.step(vec.tensor_copy(s["sidx"][:, cols], tg[h][:, :, D + 1]))
                    vec.wait_ge(kv, 2 * i + h + 1)
                    vec.wait_ge(ef_in[h], 32 * (i + 1))
                    ch.wait()
                    set_index(h, i + 1)
                    vec.tensor_tensor(kj[h][:, :, :], pk[h][:, :].rearrange("p (j f) -> p j f", f=2 * D)[:, :, 0:D],
                                      ef[h][:, :, :], ALU.add).then_inc(k_sum, 1)
                for h in H2:
                    cols = bass.ds(i * ET + h * EH, EH)
                    gcols = bass.ds(i * ET + h * EH + 1, EH)
                    vec.wait_ge(v_done, 2 * i + h + 1)
                    vec.wait_ge(k_done, 2 * i + h + 1)
                    vec.wait_ge(stored[h], 16 * i)
                    ch.step(vec.tensor_tensor(kq[h][:, :, :], kj[h][:, :, :], s["Q"][:, cols, :], ALU.mult))
                    ch.wait()
                    ch.step(vec.tensor_reduce(sc[h][:, :], kq[h][:, :, :].rearrange("p t (h i) -> p (t h) i", i=HD),
                                              AX.X, ALU.add))
                    ch.wait()
                    ch.step(vec.tensor_tensor(
                        s["AG"][:, gcols, 0:D].rearrange("p t (h j) -> p t h j", j=HD),
                        vs[h][:, :, :].rearrange("p t (h j) -> p t h j", j=HD),
                        sc[h][:, :].rearrange("p (t h) -> p t h", h=HEADS).unsqueeze(3).to_broadcast([P, EH, HEADS, HD]),
                        ALU.mult))
                    for k in range(EH):
                        t = i * ET + h * EH + k
                        ch.wait()
                        ch.step(running_sum(vec, s, t, D))
                        o = pr[k % 2]
                        ch.step(vec.tensor_tensor(
                            ihj(o[:, :]),
                            kj[h][:, k, :].rearrange("p (h i) -> p h i", i=HD).unsqueeze(3).to_broadcast([P, HEADS, HD, HD]),
                            vs[h][:, k, :].rearrange("p (h j) -> p h j", j=HD).unsqueeze(2).to_broadcast([P, HEADS, HD, HD]),
                            ALU.mult))
                        ch.wait()
                        before = acc[h][:, k - 1, :] if k else acc[1 - h][:, EH - 1, :]
                        vec.wait_ge(acc_done, EH * (2 * i + h) + k)
                        vec.scalar_tensor_tensor(acc[h][:, k, :], before, s["same"][:, bass.ds(t, 1)], o[:, :],
                                                 ALU.mult, ALU.add).then_inc(acc_done, 1)
                assert ch.n == VS, ch.n
            vec.wait_ge(acc_done, T)
            vec.tensor_copy(s["acc_end"][:, :], acc[1][:, EH - 1, :]).then_inc(acc_done, 1)


def hop_next(nc, s, dram, hop):
    keep = hop < HOPS - 1
    with ExitStack() as ctx:
        def sb(name, shape, dt=F32):
            return ctx.enter_context(nc.sbuf_tensor(f"n{hop}_{name}", shape, dt))

        def sem(name):
            return ctx.enter_context(nc.semaphore(f"n{hop}_{name}"))

        H2 = range(2)
        mg = [sb(f"state{h}", [P, EH, MW]) for h in H2]
        pr = [sb(f"product{k}", [P, MW]) for k in range(2)]
        acc = [sb(f"acc{h}", [P, EH, MW]) for h in H2] if keep else None
        ix = [sb(f"slot_now{h}", [P, EH], I32) for h in H2]
        pg = [ctx.enter_context(nc.psum_tensor(f"n{hop}_heads{h}", [P, 512], F32)) for h in H2]
        row_in = [sem(f"row_in{h}") for h in H2]
        stored = [sem(f"stored{h}") for h in H2]
        idx_set, weighted, multiplied, headed = sem("idx_set"), sem("weighted"), sem("multiplied"), sem("headed")
        acc_done, v, zeroed, note_p, note_s = sem("acc_done"), sem("steps"), sem("zeroed"), sem("note_p"), sem("note_s")
        block = ctx.enter_context(nc.Block())
        VS = 2 * EH * (1 if keep else 2)

        if keep:
            @block.sync
            def _(sync):
                with sync.Fori(0, NG) as i:
                    for h in H2:
                        passed(sync, acc_done, EH * (2 * i + h + 1), note_s)
                        sync.dma_start(state_rows(dram[f"M{hop}"], i * ET + h * EH), acc[h][:, :, :]).then_inc(stored[h], 16)
                for h in H2:
                    sync.wait_ge(stored[h], 16 * NG)

        @block.gpsimd
        def _(pool):
            top = pool.to_reg(SLOTS - 1)
            with pool.Fori(0, NG) as i:
                for h in H2:
                    passed(pool, idx_set, 2 * i + h + 1, note_p)
                    for k in range(EH):
                        pool.indirect_dma_start(
                            out=mg[h][0:EP, k, :], out_offset=None, in_=dram[f"M{hop - 1}"],
                            in_offset=bass.IndirectOffsetOnAxis(ap=ix[h][0:EP, k:k + 1], axis=0),
                            bounds_check=top, oob_is_err=False).then_inc(row_in[h], 16)

        @block.scalar
        def _(act):
            with act.Fori(0, NG) as i:
                for h in H2:
                    act.wait_ge(row_in[h], 16 * EH * (i + 1))
                    for k in range(EH):
                        t = i * ET + h * EH + k
                        act.activation(mg[h][:, k:k + 1, :], mg[h][:, k:k + 1, :], ACT.Copy,
                                       scale=s["wn"][:, bass.ds(t, 1)]).then_inc(weighted, 1)

        @block.tensor
        def _(ten):
            with ten.Fori(0, NG) as i:
                for h in H2:
                    for k in range(EH):
                        ten.wait_ge(multiplied, EH * (2 * i + h) + k + 1)
                        if k == 0:
                            ten.wait_ge(v, VS * i)
                        for r in range(HD):
                            ins = ten.matmul(pg[h][:, k * D:(k + 1) * D].rearrange("p (h j) -> p h j", j=HD),
                                             s["ident"][:, :], ihj(pr[k % 2][:, :])[:, :, r, :],
                                             start=(r == 0), stop=(r == HD - 1))
                        ins.then_inc(headed, 1)

        @block.vector
        def _(vec):
            def set_index(h, i):
                vec.tensor_copy(ix[h][:, :], s["sidx"][:, bass.ds(i * ET + h * EH, EH)]).then_inc(idx_set, 1)

            for h in H2:
                vec.memset(mg[h][:, :, :], 0.0)
                if keep:
                    vec.memset(acc[h][:, :, :], 0.0)
            vec.memset(s["AG"][:, T + 1, :], 0.0)
            vec.drain().then_inc(zeroed, 1)
            vec.wait_ge(zeroed, 1)
            for h in H2:
                set_index(h, 0)
            with vec.Fori(0, NG) as i:
                ch = Chain(vec, v, i * VS)
                for h in H2:
                    for k in range(EH):
                        t = i * ET + h * EH + k
                        vec.wait_ge(weighted, EH * (2 * i + h) + k + 1)
                        vec.wait_ge(headed, 2 * EH * i + max(EH * h + k - 1, 0))
                        vec.tensor_tensor(
                            ihj(pr[k % 2][:, :]), ihj(mg[h][:, k, :]),
                            s["Q"][:, bass.ds(t, 1), :].rearrange("p t (h i) -> p (t h) i", i=HD).unsqueeze(3)
                            .to_broadcast([P, HEADS, HD, HD]), ALU.mult).then_inc(multiplied, 1)
                        if keep:
                            before = acc[h][:, k - 1, :] if k else acc[1 - h][:, EH - 1, :]
                            if k == 0:
                                vec.wait_ge(stored[h], 16 * i)
                            vec.wait_ge(acc_done, EH * (2 * i + h) + k)
                            vec.scalar_tensor_tensor(acc[h][:, k, :], before, s["same"][:, bass.ds(t, 1)],
                                                     mg[h][:, k, :], ALU.mult, ALU.add).then_inc(acc_done, 1)
                    vec.wait_ge(multiplied, EH * (2 * i + h + 1))
                    if keep:
                        vec.wait_ge(acc_done, EH * (2 * i + h + 1))
                    set_index(h, i + 1)
                    for k in range(EH):
                        t = i * ET + h * EH + k
                        if k == 0:
                            vec.wait_ge(headed, EH * (2 * i + h + 1))
                        ch.wait()
                        g = pg[h][:, k * D:(k + 1) * D]
                        ch.step(vec.scalar_tensor_tensor(
                            s["AG"][:, bass.ds(t + 1, 1), 0:D].rearrange("p t f -> p (t f)"),
                            s["AG"][:, bass.ds(t, 1), 0:D].rearrange("p t f -> p (t f)"),
                            s["same"][:, bass.ds(t, 1)], g, ALU.mult, ALU.add))
                        if not keep:
                            x = s["AG"][:, T + 1, 0:D]
                            ch.step(vec.scalar_tensor_tensor(x, g, s["first"][:, bass.ds(t, 1)], x, ALU.mult, ALU.add))
                assert ch.n == VS, ch.n
            if keep:
                vec.wait_ge(acc_done, T)
                vec.tensor_copy(s["acc_end"][:, :], acc[1][:, EH - 1, :]).then_inc(acc_done, 1)


def hop_end(nc, s, dram, hop):
    keep = hop < HOPS - 1
    with ExitStack() as ctx:
        def sb(name, shape, dt=F32):
            return ctx.enter_context(nc.sbuf_tensor(f"e{hop}_{name}", shape, dt))

        def sem(name):
            return ctx.enter_context(nc.semaphore(f"e{hop}_{name}"))

        row = sb("first_state", [P, MW])
        prod = sb("first_product", [P, MW])
        sq = sb("squares", [P, PT_, D])
        ss = sb("head_norms", [P, 3, PT_ * HEADS])
        pc = ctx.enter_context(nc.psum_tensor(f"e{hop}_carry", [P, 512], F32))
        carried, got, fixed, put, v = sem("carried"), sem("got"), sem("fixed"), sem("put"), sem("steps")
        squared, clamped, rooted, zeroed = sem("squared"), sem("clamped"), sem("rooted"), sem("zeroed")
        block = ctx.enter_context(nc.Block())

        @block.tensor
        def _(ten):
            if keep:
                ten.matmul(pc[:, :], s["carry"][:, :], s["acc_end"][:, :], start=True, stop=True).then_inc(carried, 1)
            else:
                ten.matmul(pc[:, 0:D], s["carry"][:, :], s["AG"][:, T, 0:D], start=True, stop=True).then_inc(carried, 1)

        if keep:
            @block.gpsimd
            def _(pool):
                top = pool.to_reg(SLOTS - 1)
                slot = bass.IndirectOffsetOnAxis(ap=s["slot_x"][0:EP, 0:1], axis=0)
                pool.wait_ge(zeroed, 1)
                pool.indirect_dma_start(out=row[0:EP, :], out_offset=None, in_=dram[f"M{hop}"], in_offset=slot,
                                        bounds_check=top, oob_is_err=False).then_inc(got, 16)
                pool.wait_ge(fixed, 1)
                pool.indirect_dma_start(out=dram[f"M{hop}"], out_offset=slot, in_=row[0:EP, :], in_offset=None,
                                        bounds_check=top, oob_is_err=False).then_inc(put, 16)
                pool.wait_ge(put, 16)

        @block.scalar
        def _(act):
            act.wait_ge(fixed, 1 if keep else 0)
            for c in range(POST):
                if c:
                    act.wait_ge(v, 6 * c)
                if c == POST - 1:
                    act.wait_ge(fixed, 2)
                act.activation(sq[:, :, :], s["AG"][:, 1 + c * PT_:1 + (c + 1) * PT_, 0:D], ACT.Square).then_inc(squared, 1)
                act.wait_ge(clamped, c + 1)
                act.activation(ss[:, 1, :], ss[:, 0, :], ACT.Sqrt).then_inc(rooted, 1)

        @block.vector
        def _(vec):
            extra = s["AG"][:, T + 1, 0:D]
            if keep:
                vec.memset(row[:, :], 0.0).then_inc(zeroed, 1)
                vec.wait_ge(carried, 1)
                vec.wait_ge(got, 16)
                vec.wait_ge(zeroed, 1)
                vec.tensor_tensor(row[:, :], row[:, :], pc[:, :], ALU.add).then_inc(fixed, 1)
                vec.wait_ge(fixed, 1)
                q = s["Q"][:, 0, :].rearrange("p (h i) -> p h i", i=HD).unsqueeze(3).to_broadcast([P, HEADS, HD, HD])
                vec.tensor_tensor(ihj(prod[:, :]), ihj(row[:, :]), q, ALU.mult).then_inc(zeroed, 1)
                vec.wait_ge(zeroed, 2)
                vec.tensor_reduce(extra, prod[:, :].rearrange("p (h i j) -> p h j i", h=HEADS, i=HD),
                                  AX.X, ALU.add).then_inc(fixed, 1)
            else:
                vec.wait_ge(carried, 1)
                vec.tensor_tensor(extra, extra, pc[:, 0:D], ALU.add).then_inc(fixed, 2)
            n = 0
            for c in range(POST):
                def step(ins):
                    nonlocal n
                    ins.then_inc(v, 1)
                    n += 1
                    vec.wait_ge(v, n)

                a, b = c * PT_, (c + 1) * PT_
                vec.wait_ge(squared, c + 1)
                step(vec.tensor_reduce(ss[:, 2, :], sq[:, :, :].rearrange("p t (h j) -> p (t h) j", j=HD), AX.X, ALU.add))
                vec.tensor_scalar(ss[:, 0, :], ss[:, 2, :], 1.0 / HD, 1.0, ALU.mult, ALU.max).then_inc(clamped, 1)
                vec.wait_ge(rooted, c + 1)
                step(vec.reciprocal(ss[:, 2, :], ss[:, 1, :]))
                step(vec.tensor_scalar(ss[:, 2, :], ss[:, 2, :], s["hop"][:, hop + 1:hop + 2], None, ALU.mult))
                step(vec.tensor_tensor(
                    sq[:, :, :].rearrange("p t (h j) -> p t h j", j=HD),
                    s["AG"][:, 1 + a:1 + b, 0:D].rearrange("p t (h j) -> p t h j", j=HD),
                    ss[:, 2, :].rearrange("p (t h) -> p t h", h=HEADS).unsqueeze(3).to_broadcast([P, PT_, HEADS, HD]),
                    ALU.mult))
                step(vec.tensor_tensor(s["HID"][:, a:b, :], s["HID"][:, a:b, :], sq[:, :, :], ALU.add))
                step(vec.memset(ss[:, 2, 0:1], 0.0))


def write_out(nc, s, out):
    with ExitStack() as ctx:
        H2 = range(2)
        row = [ctx.enter_context(nc.sbuf_tensor(f"o_rows{h}", [P, EH, D], F32)) for h in H2]
        ix = [ctx.enter_context(nc.sbuf_tensor(f"o_dst{h}", [P, EH], I32)) for h in H2]
        put = [ctx.enter_context(nc.semaphore(f"o_put{h}")) for h in H2]
        rows_set, idx_set, note, last = (ctx.enter_context(nc.semaphore(n)) for n in
                                         ("o_rows_set", "o_idx_set", "o_note", "o_last"))
        block = ctx.enter_context(nc.Block())

        @block.scalar
        def _(act):
            with act.Fori(0, NG) as i:
                for h in H2:
                    act.wait_ge(put[h], 16 * EH * i)
                    act.activation(row[h][:, :, :], s["HID"][:, bass.ds(i * ET + h * EH, EH), :], ACT.Copy).then_inc(rows_set, 1)

        @block.vector
        def _(vec):
            with vec.Fori(0, NG) as i:
                for h in H2:
                    vec.wait_ge(put[h], 16 * EH * i)
                    vec.tensor_copy(ix[h][:, :], s["dst_out"][:, bass.ds(i * ET + h * EH, EH)]).then_inc(idx_set, 1)

        @block.gpsimd
        def _(pool):
            top = pool.to_reg(N - 1)
            pool.indirect_dma_start(out=out, out_offset=bass.IndirectOffsetOnAxis(ap=s["dst_x"][0:EP, 0:1], axis=0),
                                    in_=s["HID"][0:EP, T, :], in_offset=None,
                                    bounds_check=top, oob_is_err=False).then_inc(last, 16)
            with pool.Fori(0, NG) as i:
                for h in H2:
                    passed(pool, rows_set, 2 * i + h + 1, note)
                    passed(pool, idx_set, 2 * i + h + 1, note)
                    for k in range(EH):
                        pool.indirect_dma_start(
                            out=out, out_offset=bass.IndirectOffsetOnAxis(ap=ix[h][0:EP, k:k + 1], axis=0),
                            in_=row[h][0:EP, k, :], in_offset=None,
                            bounds_check=top, oob_is_err=False).then_inc(put[h], 16)
            for h in H2:
                pool.wait_ge(put[h], 16 * EH * NG)
            pool.wait_ge(last, 16)


INPUTS = ["x", "src", "dst", "edge_attr_64", "edge_weight", "L0_gnn_W1", "L0_gnn_b1", "L0_gnn_W2", "L0_gnn_b2",
          "L1_gnn_Wq", "L1_gnn_bq", "L1_gnn_Wk", "L1_gnn_bk", "L1_gnn_Wv", "L1_gnn_bv", "L1_gnn_hopwise"]


def kernel(**inputs):
    import concourse.bacc as bacc
    from concourse.bass_utils import run_bass_kernel_spmd

    nc = bacc.Bacc("TRN2", target_bir_lowering=False, num_devices=1)
    r, c = np.arange(P)[:, None], np.arange(P)[None, :]
    constants = {
        "mats": np.concatenate([r == c, c > r, r == c + 1], axis=1).astype(np.float32),
        "slots": (np.arange(T)[None, :] * P + r).astype(np.float32),
    }
    arrays, args = {}, []
    for name, a in [(n, inputs[n]) for n in INPUTS] + list(constants.items()):
        a = np.ascontiguousarray(a)
        arrays[f"in_{name}"] = a
        args.append(nc.dram_tensor(f"in_{name}", a.shape, mybir.dt.from_np(a.dtype), kind="ExternalInput").ap())
    args.append(nc.dram_tensor("out", (N, D), F32, kind="ExternalOutput").ap())
    gnn(nc, *args)
    r = run_bass_kernel_spmd(nc, [arrays], core_ids=[0])
    return r.results[0]["out"]
```

```python
from contextlib import ExitStack

import numpy as np

import concourse.bass as bass
from concourse import mybir

F32 = mybir.dt.float32
I32 = mybir.dt.int32
U32 = mybir.dt.uint32
ALU = mybir.AluOpType
ACT = mybir.ActivationFunctionType
AX = mybir.AxisListType

P = 128
N = 50000
E = 25000
D = 64
HEADS, HD = 8, 8
MW = HEADS * HD * HD
HOPS = 3
EPS = 1e-5

EP = 125
T = E // EP
XT = T
SLOTS = T * P
AW = D + 1
TW = D + 2
NO_ROW = 1 << 20

NT = 16
NG = 25
GSTEP = (N - NT * P) // (NG - 1)
HT = NT // 2
ET = T // NG
EH = ET // 2

UNITS = 2 * NG
W = EH * D
X_STEPS = 10


def passed(eng, sem, value, note):
    eng.wait_ge(sem, value)
    eng.sem_inc(note, 1)


def here(m):
    return not isinstance(m, int) or 0 <= m < UNITS


def wait(eng, sem, value):
    if not isinstance(value, int) or value > 0:
        eng.wait_ge(sem, value)


def passed(eng, sem, value, note):
    if not isinstance(value, int) or value > 0:
        eng.wait_ge(sem, value)
        eng.sem_inc(note, 1)


def turns(eng, body, behind):
    lead = (behind + 2) // 2
    for i in range(lead):
        for b in range(2):
            body(2 * i + b, b)
    with eng.Fori(lead, NG) as i:
        for b in range(2):
            body(2 * i + b, b)
    for m in range(UNITS, UNITS + behind):
        body(m, m % 2)


class Chain:

    def __init__(self, eng, sem, m, steps):
        self.eng, self.sem, self.base, self.steps, self.n = eng, sem, m * steps, steps, 0

    def step(self, ins):
        ins.then_inc(self.sem, 1)
        self.n += 1
        assert self.n <= self.steps

    def wait(self):
        wait(self.eng, self.sem, self.base + self.n)


def edge_cols(m):
    return bass.ds(m * EH, EH)


def norm_stats(ch, varred, q, n, rows, squares):
    vec = ch.eng
    for a, b, what in rows:
        ch.step(vec.tensor_reduce(q[:, 0, a:b], what, AX.X, ALU.add))
    ch.step(vec.tensor_reduce(q[:, 1, 0:n], squares, AX.X, ALU.add))
    ch.wait()
    ch.step(vec.tensor_scalar(q[:, 0, 0:n], q[:, 0, 0:n], 1.0 / D, None, ALU.mult))
    ch.wait()
    ch.step(vec.tensor_tensor(q[:, 2, 0:n], q[:, 0, 0:n], q[:, 0, 0:n], ALU.mult))
    ch.wait()
    ch.step(vec.scalar_tensor_tensor(q[:, 1, 0:n], q[:, 1, 0:n], 1.0 / D, q[:, 2, 0:n],
                                     ALU.mult, ALU.subtract))
    ch.wait()
    vec.tensor_scalar(q[:, 2, 0:n], q[:, 1, 0:n], 0.0, EPS, ALU.max, ALU.add).then_inc(varred, 1)


def norm_scales(ch, scaled, q, n):
    vec = ch.eng
    ch.step(vec.reciprocal(q[:, 4, :], q[:, 3, :]))
    ch.wait()
    vec.scalar_tensor_tensor(q[:, 5, 0:n], q[:, 0, 0:n], -1.0, q[:, 4, 0:n],
                             ALU.mult, ALU.mult).then_inc(scaled, 1)


def gnn(nc, x, src, dst, edge_attr, edge_weight, W1, b1, W2, b2, Wq, bq, Wk, bk, Wv, bv, hopwise,
        mats, slots, out):
    dram = {
        "table": nc.dram_tensor("node_table", (N, TW), F32, kind="Internal").ap(),
        "M0": nc.dram_tensor("state_hop0", (SLOTS, MW), F32, kind="Internal").ap(),
        "M1": nc.dram_tensor("state_hop1", (SLOTS, MW), F32, kind="Internal").ap(),
        "xd": nc.dram_tensor("x_of_dst", (P, T, D), F32, kind="Internal").ap(),
        "base": nc.dram_tensor("out_before_hops", (P, T, D), F32, kind="Internal").ap(),
        "g": [nc.dram_tensor(f"head_sums{k}", (P, T, D), F32, kind="Internal").ap() for k in range(HOPS)],
    }
    with ExitStack() as ctx:
        def sb(name, shape, dt=F32):
            return ctx.enter_context(nc.sbuf_tensor(name, shape, dt))

        s = {"used_semaphores": []}
        s["ident"] = sb("ident", [P, P])
        s["W1"] = sb("W1_two", [P, P])
        s["W2"] = sb("W2_two", [P, P])
        s["Wv"] = sb("Wv_two", [P, P])
        s["Wvq"] = sb("Wvq_two", [P, 2 * P])
        s["Wkv"] = sb("Wkv", [P, P])
        s["b1"] = sb("b1_col", [P, 1])
        s["b2"] = sb("b2_row", [1, P])
        s["bv"] = sb("bv_row", [1, P])
        s["bvq"] = sb("bvq_row", [1, P])
        s["bkv"] = sb("bkv_row", [1, P])
        s["ones"] = sb("ones_row", [1, P])
        s["hop"] = sb("hop_factors", [P, HOPS + 1])
        s["carry"] = sb("carry", [P, P])
        s["carryT"] = sb("carryT", [P, P])
        s["same"] = sb("same_as_before", [P, T])
        s["notlast"] = sb("not_last_here", [P, T])
        s["islast"] = sb("last_here", [P, T])
        s["fix"] = sb("carried_sums", [P, 2, AW])
        s["acc_end"] = sb("state_of_last_column", [P, MW])
        s["first"] = sb("in_first_segment", [P, T])
        s["trail"] = sb("in_last_segment", [P, T])
        s["src"] = sb("src_index", [P, T + ET], I32)
        s["dst"] = sb("dst_index", [P, T + ET], I32)
        s["dst_end"] = sb("dst_at_segment_end", [P, T], I32)
        s["dst_out"] = sb("dst_for_output", [P, T], I32)
        s["dst_x"] = sb("dst_for_extra_column", [P, 1], I32)
        s["slot_x"] = sb("slot_of_first_segment", [P, 1], I32)
        s["w"] = sb("edge_weight_cols", [P, T])
        s["wn"] = sb("norm_hop12", [P, T])
        s["sidx"] = sb("state_slot_of_src", [P, T + ET], I32)
        s["slots"] = sb("slot_ids", [P, T])
        s["AG"] = sb("sums", [P, T + 1, AW])
        s["xbase"] = sb("extra_base", [P, D])
        s["gx"] = sb("extra_head_sums", [P, HOPS, D])

        prepare(nc, s, src, dst, edge_weight, W1, b1, W2, b2, Wq, bq, Wk, bk, Wv, bv, hopwise,
                mats, slots)
        nodes_and_gathers(nc, s, dram, x, out)
        complete_sums(nc, s)
        s["Q"] = sb("queries", [P, T, D])
        edge_mlp(nc, s, dram)
        hop_zero(nc, s, dram, edge_attr, s["used_semaphores"])
        hop_end(nc, s, dram, 0)
        hop_next(nc, s, dram, 1)
        hop_end(nc, s, dram, 1)
        hop_next(nc, s, dram, 2)
        write_out(nc, s, dram, out)


def repeated(row, n):
    return row[:, :].unsqueeze(1).to_broadcast([1, n, P])


def prepare(nc, s, src, dst, edge_weight, W1, b1, W2, b2, Wq, bq, Wk, bk, Wv, bv, hopwise, mats,
            slots):
    with ExitStack() as ctx:
        def sb(name, shape, dt=F32):
            return ctx.enter_context(nc.sbuf_tensor(name, shape, dt))

        def sem(name):
            return used(s, ctx.enter_context(nc.semaphore(name)))

        later = sb("col_after_row", [P, P])
        shift = sb("row_after_col", [P, P])
        dstf = sb("dst_float", [P, T])
        nextf = sb("dst_of_next_partition", [P, 1])
        dif = sb("dst_differs", [P, T])
        lastf = sb("is_segment_end", [P, T])
        tmp = sb("prep_tmp", [P, T])
        tmp2 = sb("prep_tmp2", [P, T])
        len1 = sb("first_segment_length", [P, 1])
        ends = sb("first_segment_ends_here", [P, 1])
        col = sb("prep_col", [P, 2])
        pfirst = ctx.enter_context(nc.psum_tensor("p_first_row", [P, 512], F32))
        pnext = ctx.enter_context(nc.psum_tensor("p_next", [P, 512], F32))
        loaded, cleared, v, pe, rows = (sem("prep_loaded"), sem("prep_cleared"), sem("prep_vec"),
                                        sem("prep_pe"), sem("prep_rows"))
        block = ctx.enter_context(nc.Block())
        n_loads = 0

        @block.sync
        def _(sync):
            nonlocal n_loads
            sync.wait_ge(cleared, 1)
            loads = [(s["src"][0:EP, 0:T], src.rearrange("(p t) -> p t", t=T)),
                     (s["dst"][0:EP, 0:T], dst.rearrange("(p t) -> p t", t=T)),
                     (s["w"][0:EP, :], edge_weight.rearrange("(p t) -> p t", t=T)),
                     (s["ident"][:, :], mats[:, 0:P]), (later[:, :], mats[:, P:2 * P]),
                     (shift[:, :], mats[:, 2 * P:3 * P]), (s["slots"][:, :], slots),
                     (s["hop"][:, :], hopwise.unsqueeze(0).to_broadcast([P, HOPS + 1]))]
            loads += [(s["Wkv"][0:D, 0:D], Wk), (s["Wkv"][0:D, D:2 * D], Wv)]
            for k in range(2):
                r, c = slice(k * D, k * D + D), k * D
                loads += [(s["W1"][r, c:c + D], W1), (s["W2"][r, c:c + D], W2),
                          (s["Wv"][r, c:c + D], Wv),
                          (s["Wvq"][r, 2 * c:2 * c + D], Wv), (s["Wvq"][r, 2 * c + D:2 * c + 2 * D], Wq),
                          (s["b1"][r, :], b1.unsqueeze(1))]
            for j in range(2):
                r = slice(j * D, j * D + D)
                even = j % 2 == 0
                loads += [(s["b2"][:, r], b2.unsqueeze(0)), (s["bv"][:, r], bv.unsqueeze(0)),
                          (s["bvq"][:, r], (bv if even else bq).unsqueeze(0)),
                          (s["bkv"][:, r], (bk if even else bv).unsqueeze(0))]
            for to, what in loads:
                sync.dma_start(to, what).then_inc(loaded, 16)
            n_loads = len(loads)
            sync.wait_ge(loaded, 16 * n_loads)
            sync.sem_inc(rows, 1)

        @block.tensor
        def _(ten):
            ten.wait_ge(v, 2)
            ten.matmul(pfirst[:, 0:P], dstf[:, 0:1].to_broadcast([P, P]), s["ident"][:, :],
                       start=True, stop=True).then_inc(pe, 1)
            ten.matmul(pnext[:, 0:1], shift[:, :], dstf[:, 0:1], start=True, stop=True).then_inc(pe, 1)
            ten.wait_ge(v, 6)
            ten.transpose(pfirst[:, P:2 * P], s["carry"][:, :], s["ident"][:, :]).then_inc(pe, 1)

        @block.vector
        def _(vec):
            for k in ("W1", "W2", "Wv", "Wvq", "Wkv", "w"):
                vec.memset(s[k][:, :], 0.0)
            vec.memset(s["src"][:, :], 0)
            vec.memset(s["dst"][:, :], -1)
            vec.memset(s["sidx"][:, :], 0)
            vec.memset(s["ones"][:, :], 1.0)
            vec.memset(s["AG"][:, :, :], 1.0)
            vec.memset(s["gx"][:, :, :], 0.0)
            vec.memset(s["dst_out"][:, :], 0).then_inc(cleared, 1)
            vec.wait_ge(cleared, 1)
            vec.wait_ge(rows, 1)
            n = [0]

            def step(ins):
                ins.then_inc(v, 1)
                n[0] += 1
                vec.wait_ge(v, n[0])

            dstt = dstf
            step(vec.tensor_copy(dstt[:, :], s["dst"][:, 0:T]))
            step(vec.tensor_scalar(s["wn"][:, :], s["w"][:, :], 0.0, None, ALU.mult))
            vec.wait_ge(pe, 2)
            step(vec.tensor_copy(nextf[:, :], pnext[:, 0:1]))
            step(vec.tensor_tensor(dif[:, 0:T - 1], dstt[:, 0:T - 1], dstt[:, 1:T], ALU.not_equal))
            step(vec.tensor_scalar(s["carry"][:, :], pfirst[:, 0:P], dstt[:, T - 1:T], None, ALU.is_equal))
            step(vec.tensor_tensor(s["carry"][:, :], s["carry"][:, :], later[:, :], ALU.mult))
            vec.wait_ge(pe, 3)
            step(vec.tensor_copy(s["carryT"][:, :], pfirst[:, P:2 * P]))
            step(vec.tensor_copy(lastf[:, 0:T - 1], dif[:, 0:T - 1]))
            step(vec.tensor_tensor(lastf[:, T - 1:T], dstt[:, T - 1:T], nextf[:, :], ALU.not_equal))
            step(vec.memset(s["same"][:, 0:1], 0.0))
            step(vec.tensor_scalar(s["same"][:, 1:T], dif[:, 0:T - 1], -1.0, 1.0, ALU.mult, ALU.add))
            step(vec.memset(s["notlast"][:, T - 1:T], 0.0))
            step(vec.tensor_scalar(s["notlast"][:, 0:T - 1], dif[:, 0:T - 1], -1.0, 1.0, ALU.mult, ALU.add))
            step(vec.tensor_scalar(s["islast"][:, :], s["notlast"][:, :], -1.0, 1.0, ALU.mult, ALU.add))
            step(vec.tensor_scalar(s["first"][:, :], dstt[:, :], dstt[:, 0:1], None, ALU.is_equal))
            step(vec.tensor_scalar(s["trail"][:, :], dstt[:, :], dstt[:, T - 1:T], None, ALU.is_equal))
            step(vec.tensor_reduce(len1[:, :], s["first"][:, :], AX.X, ALU.add))
            step(vec.tensor_scalar(col[:, 0:1], len1[:, :], float(P), float(-P), ALU.mult, ALU.add))
            step(vec.tensor_tensor(col[:, 1:2], col[:, 0:1], s["slots"][:, 0:1], ALU.add))
            step(vec.tensor_copy(s["slot_x"][:, :], col[:, 1:2]))
            step(vec.tensor_scalar(tmp[:, :], lastf[:, :], -float(NO_ROW), float(NO_ROW), ALU.mult, ALU.add))
            step(vec.tensor_tensor(tmp2[:, :], tmp[:, :], dstt[:, :], ALU.add))
            step(vec.tensor_copy(s["dst_end"][:, :], tmp2[:, :]))
            step(vec.tensor_scalar(tmp[:, :], s["first"][:, :], float(NO_ROW), None, ALU.mult))
            step(vec.tensor_tensor(tmp[:, :], tmp[:, :], tmp2[:, :], ALU.add))
            step(vec.tensor_copy(s["dst_out"][:, :], tmp[:, :]))
            step(vec.tensor_tensor(tmp[:, :], s["first"][:, :], lastf[:, :], ALU.mult))
            step(vec.tensor_reduce(ends[:, :], tmp[:, :], AX.X, ALU.add))
            step(vec.tensor_scalar(ends[:, :], ends[:, :], -float(NO_ROW), float(NO_ROW), ALU.mult, ALU.add))
            step(vec.tensor_tensor(ends[:, :], ends[:, :], dstt[:, 0:1], ALU.add))
            step(vec.tensor_copy(s["dst_x"][:, :], ends[:, :]))
            step(vec.tensor_scalar(s["Wv"][:, :], s["Wv"][:, :], s["hop"][:, 0:1], None, ALU.mult))
            for k in range(2):
                c = slice(2 * k * D, 2 * k * D + D)
                step(vec.tensor_scalar(s["Wvq"][:, c], s["Wvq"][:, c], s["hop"][:, 0:1], None, ALU.mult))
            step(vec.tensor_scalar(s["bv"][:, :], s["bv"][:, :], s["hop"][0:1, 0:1], None, ALU.mult))
            for c in (slice(0, D),):
                step(vec.tensor_scalar(s["bvq"][:, c], s["bvq"][:, c], s["hop"][0:1, 0:1], None, ALU.mult))


def used(s, sem):
    s["used_semaphores"].append(sem)
    return sem


def nodes_and_gathers(nc, s, dram, x, out):
    with ExitStack() as ctx:
        def sb(name, shape, dt=F32):
            return ctx.enter_context(nc.sbuf_tensor(name, shape, dt))

        def ps(name):
            return ctx.enter_context(nc.psum_tensor(name, [P, HT * D], F32))

        def sem(name):
            return used(s, ctx.enter_context(nc.semaphore(name)))

        def two(name, shape, dt=F32):
            return [sb(f"{name}{b}", shape, dt) for b in range(2)]

        C = HT + EH
        xn, gs, gd = two("x_nodes", [P, HT, D]), two("x_src", [P, EH, D]), two("x_dst", [P, EH, D])
        sq, sq2 = two("squares", [P, C, D]), two("squares_b", [P, HT, D])
        h0, h1 = two("h0_", [P, HT, D]), two("h1_", [P, HT, D])
        hT1, hT2, a1 = sb("h0_turned", [P, HT * D]), sb("h1_turned", [P, HT * D]), sb("mlp1", [P, HT * D])
        x1, tab, res = two("x1_", [P, HT, D]), two("table_rows", [P, HT, TW]), two("out_rows", [P, HT, D])
        st, st2 = two("stats", [P, 6, C]), two("stats_b", [P, 6, HT])
        isrc, idst = two("src_now", [P, EH], I32), two("dst_now", [P, EH], I32)
        warm = sb("root_of_one", [1, 1])
        pt1, pt2, pa, pb1, pb2 = ps("p_turned1"), ps("p_turned2"), ps("p_mlp1"), ps("p_mlp2"), ps("p_value")
        x_in, stored = [sem("x_in0"), sem("x_in1")], [sem("stored0"), sem("stored1")]
        src_in, dst_in = [sem("src_in0"), sem("src_in1")], [sem("dst_in0"), sem("dst_in1")]
        dst_kept = [sem("dst_kept0"), sem("dst_kept1")]
        isrc_set, idst_set = sem("isrc_set"), sem("idst_set")
        squared, squared2 = sem("squared"), sem("squared2")
        varred, varred2 = sem("varred"), sem("varred2")
        rooted, rooted2 = sem("rooted"), sem("rooted2")
        scaled, scaled2 = sem("scaled"), sem("scaled2")
        normed, src_normed, normed2 = sem("normed"), sem("src_normed"), sem("normed2")
        turned1, turned2, mm1, mm2, mm3 = sem("turned1"), sem("turned2"), sem("mm1"), sem("mm2"), sem("mm3")
        copied1, copied2, relued = sem("copied1"), sem("copied2"), sem("relued")
        x1_done, tab_done, res_done = sem("x1_done"), sem("tab_done"), sem("res_done")
        v1, v2, v3, v4, v5 = (sem(f"vec_steps{k}") for k in range(5))
        note_p, note_s, zeroed = sem("note_pool"), sem("note_sync"), sem("zeroed")
        block = ctx.enter_context(nc.Block())

        def rows(dram_t, m, b, w):
            i = m // 2 if isinstance(m, int) else (m - b) * (GSTEP // 2)
            start = i * GSTEP if isinstance(m, int) else i
            a = dram_t[bass.ds(start, NT * P), :].rearrange("(p j) f -> p j f", j=NT)
            return a[:, b * HT:(b + 1) * HT, :]

        @block.sync
        def _(sync):
            def body(n, b):
                if here(n):
                    passed(sync, x1_done, n - 1, note_s)
                    sync.dma_start(xn[b][:, :, :], rows(x, n, b, D)).then_inc(x_in[b], 16)
                m = n - 4
                if here(m):
                    passed(sync, res_done, m + 1, note_s)
                    passed(sync, tab_done, m + 1, note_s)
                    for h in range(2):
                        passed(sync, stored[h], 16 * (m - b), note_s)
                    sync.dma_start(rows(out, m, b, D), res[b][:, :, :]).then_inc(stored[b], 16)
                    sync.dma_start(rows(dram["table"], m, b, TW), tab[b][:, :, :]).then_inc(stored[b], 16)
                m = n - 2
                if here(m):
                    passed(sync, dst_in[b], 8 * EH * (m - b + 2), note_s)
                    sync.dma_start(dram["xd"][:, edge_cols(m), :], gd[b][:, :, :]).then_inc(dst_kept[b], 16)

            sync.wait_ge(zeroed, 1)
            turns(sync, body, 4)
            for b in range(2):
                sync.wait_ge(stored[b], 32 * NG)
                sync.wait_ge(dst_kept[b], 16 * NG)

        @block.gpsimd
        def _(pool):
            top = pool.to_reg(N - 1)

            def body(n, b):
                passed(pool, isrc_set, n + 1, note_p)
                for k in range(EH):
                    pool.indirect_dma_start(
                        out=gs[b][0:EP, k, :], out_offset=None, in_=x,
                        in_offset=bass.IndirectOffsetOnAxis(ap=isrc[b][0:EP, k:k + 1], axis=0),
                        bounds_check=top, oob_is_err=False).then_inc(src_in[b], 16)
                passed(pool, idst_set, n + 1, note_p)
                passed(pool, dst_kept[b], 8 * (n - b), note_p)
                for k in range(EH):
                    pool.indirect_dma_start(
                        out=gd[b][0:EP, k, :], out_offset=None, in_=x,
                        in_offset=bass.IndirectOffsetOnAxis(ap=idst[b][0:EP, k:k + 1], axis=0),
                        bounds_check=top, oob_is_err=False).then_inc(dst_in[b], 16)

            turns(pool, body, 0)

        @block.scalar
        def _(act):
            def body(n, b):
                o = 1 - b
                if here(n - 1):
                    act.wait_ge(turned1, n)
                    act.activation(hT1[:, :], pt1[:, :], ACT.Copy).then_inc(copied1, 1)
                if here(n - 3):
                    act.wait_ge(turned2, n - 2)
                    act.activation(hT2[:, :], pt2[:, :], ACT.Copy).then_inc(copied2, 1)
                if here(n - 2):
                    act.wait_ge(x1_done, n - 1)
                    act.activation(sq2[b][:, :, :], x1[b][:, :, :], ACT.Square).then_inc(squared2, 1)
                if here(n - 1):
                    act.wait_ge(mm1, n)
                    act.activation(a1[:, :], pa[:, :], ACT.Relu, bias=s["b1"][:, 0:1]).then_inc(relued, 1)
                if here(n):
                    act.wait_ge(x_in[b], 8 * (n - b + 2))
                    act.activation(sq[b][:, 0:HT, :], xn[b][:, :, :], ACT.Square)
                    act.wait_ge(src_in[b], 8 * EH * (n - b + 2))
                    act.activation(sq[b][:, HT:C, :], gs[b][:, :, :], ACT.Square).then_inc(squared, 1)
                if here(n - 2):
                    act.wait_ge(varred2, n - 1)
                    act.activation(st2[b][:, 3, :], st2[b][:, 2, :], ACT.Sqrt).then_inc(rooted2, 1)
                    act.wait_ge(scaled2, n - 1)
                    for k in range(HT):
                        ins = act.activation(h1[b][:, k, :], x1[b][:, k, :], ACT.Relu,
                                             bias=st2[b][:, 5, k:k + 1], scale=st2[b][:, 4, k:k + 1])
                    ins.then_inc(normed2, 1)
                if here(n):
                    act.wait_ge(varred, n + 1)
                    act.activation(st[b][:, 3, :], st[b][:, 2, :], ACT.Sqrt).then_inc(rooted, 1)
                    act.wait_ge(scaled, n + 1)
                    for k in range(EH):
                        ins = act.activation(s["AG"][:, bass.ds(n * EH + k + 1, 1), 0:D], gs[b][:, k:k + 1, :],
                                             ACT.Relu, bias=st[b][:, 5, HT + k:HT + k + 1],
                                             scale=st[b][:, 4, HT + k:HT + k + 1])
                    ins.then_inc(src_normed, 1)
                    for k in range(HT):
                        ins = act.activation(h0[b][:, k, :], xn[b][:, k, :], ACT.Relu,
                                             bias=st[b][:, 5, k:k + 1], scale=st[b][:, 4, k:k + 1])
                    ins.then_inc(normed, 1)

            act.wait_ge(zeroed, 1)
            act.activation(warm[:, :], s["ones"][:, 0:1], ACT.Sqrt)
            turns(act, body, 3)

        @block.tensor
        def _(ten):
            def turn(pt, what, done):
                for k in range(HT // 2):
                    ins = ten.transpose(pt[:, k * P:(k + 1) * P], what[:, 2 * k:2 * k + 2, :], s["ident"][:, :])
                ins.then_inc(done, 1)

            def rows_out(pb, lhs, w, bias, done):
                ten.matmul(pb[:, :], s["ones"][:, :], repeated(bias, HT // 2), start=True, stop=False,
                           skip_group_check=True)
                for k in range(HT // 2):
                    ins = ten.matmul(pb[:, k * P:(k + 1) * P], lhs[:, k * P:(k + 1) * P], w[:, :],
                                     start=False, stop=(k == HT // 2 - 1), skip_group_check=True)
                ins.then_inc(done, 1)

            def body(n, b):
                if here(n - 1):
                    ten.wait_ge(normed, n)
                    wait(ten, copied1, n - 1)
                    turn(pt1, h0[1 - b], turned1)
                if here(n - 3):
                    ten.wait_ge(normed2, n - 2)
                    wait(ten, copied2, n - 3)
                    turn(pt2, h1[1 - b], turned2)
                if here(n - 1):
                    ten.wait_ge(copied1, n)
                    wait(ten, relued, n - 1)
                    ten.matmul(pa[:, :], s["W1"][:, :], hT1[:, :], start=True, stop=True).then_inc(mm1, 1)
                if here(n - 3):
                    ten.wait_ge(copied2, n - 2)
                    wait(ten, res_done, n - 3)
                    rows_out(pb2, hT2, s["Wv"], s["bv"], mm3)
                if here(n - 1):
                    ten.wait_ge(relued, n)
                    wait(ten, x1_done, n - 1)
                    rows_out(pb1, a1, s["W2"], s["b2"], mm2)

            turns(ten, body, 3)

        @block.vector
        def _(vec):
            def set_isrc(m, b):
                vec.tensor_copy(isrc[b][:, :], s["src"][:, edge_cols(m)]).then_inc(isrc_set, 1)

            def set_idst(m, b):
                vec.tensor_copy(idst[b][:, :], s["dst"][:, edge_cols(m)]).then_inc(idst_set, 1)

            def flat(t):
                return t[:, :, :].rearrange("p j f -> p (j f)")

            def body(n, b):
                o = 1 - b
                if here(n - 3):
                    m = n - 3
                    wait(vec, stored[o], 16 * (m - o))
                    vec.wait_ge(normed2, m + 1)
                    vec.tensor_copy(tab[o][:, :, 0:D], h1[o][:, :, :]).then_inc(tab_done, 1)
                if here(n - 2):
                    vec.wait_ge(squared2, n - 1)
                    norm_stats(Chain(vec, v2, n - 2, 5), varred2, st2[b], HT,
                               [(0, HT, x1[b][:, :, :])], sq2[b][:, :, :])
                if here(n - 3):
                    vec.wait_ge(mm3, n - 2)
                    vec.tensor_tensor(flat(res[o]), pb2[:, :], flat(x1[o]), ALU.add).then_inc(res_done, 1)
                if here(n - 2):
                    vec.wait_ge(rooted2, n - 1)
                    norm_scales(Chain(vec, v3, n - 2, 1), scaled2, st2[b], HT)
                if here(n - 1):
                    m = n - 1
                    vec.wait_ge(src_normed, m + 1)
                    ch = Chain(vec, v4, m, EH)
                    for k in range(EH):
                        t = m * EH + k
                        now = s["AG"][:, bass.ds(t + 1, 1), :]
                        ch.wait()
                        ch.step(vec.scalar_tensor_tensor(now, s["AG"][:, bass.ds(t, 1), :],
                                                         s["same"][:, bass.ds(t, 1)], now, ALU.mult, ALU.add))
                    if here(m + 2):
                        set_isrc(m + 2, o)
                if here(n - 1):
                    m = n - 1
                    vec.wait_ge(mm2, m + 1)
                    vec.scalar_tensor_tensor(flat(x1[o]), pb1[:, :], 0.0, flat(xn[o]),
                                             ALU.max, ALU.add).then_inc(x1_done, 1)
                if here(n):
                    vec.wait_ge(x_in[b], 8 * (n - b + 2))
                    vec.wait_ge(squared, n + 1)
                    norm_stats(Chain(vec, v1, n, 6), varred, st[b], C,
                               [(0, HT, xn[b][:, :, :]), (HT, C, gs[b][:, :, :])], sq[b][:, :, :])
                if here(n - 1) and here(n + 1):
                    vec.wait_ge(dst_in[o], 8 * EH * (n - 1 - o + 2))
                    set_idst(n + 1, o)
                if here(n):
                    vec.wait_ge(rooted, n + 1)
                    norm_scales(Chain(vec, v5, n, 1), scaled, st[b], C)

            for b in range(2):
                vec.memset(gs[b][:, :, :], 0.0)
                vec.memset(gd[b][:, :, :], 0.0)
                vec.memset(tab[b][:, :, D:D + 1], 0.0)
                vec.memset(tab[b][:, :, D + 1:TW], float(NO_ROW))
                set_isrc(b, b)
                set_idst(b, b)
            vec.drain().then_inc(zeroed, 1)
            vec.wait_ge(zeroed, 1)
            turns(vec, body, 3)


def complete_sums(nc, s):
    with ExitStack() as ctx:
        pc = ctx.enter_context(nc.psum_tensor("p_carry", [P, 512], F32))
        pe = used(s, ctx.enter_context(nc.semaphore("carry_ready")))
        v = used(s, ctx.enter_context(nc.semaphore("back_steps")))
        block = ctx.enter_context(nc.Block())

        @block.tensor
        def _(ten):
            ten.matmul(pc[:, 0:AW], s["carry"][:, :], s["AG"][:, T, :], start=True, stop=True).then_inc(pe, 1)
            ten.wait_ge(v, 2 + AW)
            ten.matmul(pc[:, P:P + AW], s["carryT"][:, :], s["AG"][:, 1, :], start=True, stop=True).then_inc(pe, 1)

        @block.vector
        def _(vec):
            vec.wait_ge(pe, 1)
            vec.tensor_copy(s["fix"][:, 0, :], pc[:, 0:AW]).then_inc(v, 1)
            vec.tensor_tensor(s["AG"][:, 1:T + 1, :], s["AG"][:, 1:T + 1, :],
                              s["islast"][:, :].unsqueeze(2).to_broadcast([P, T, AW]), ALU.mult).then_inc(v, 1)
            vec.wait_ge(v, 2)
            for f in range(AW):
                col = s["AG"][:, T:0:-1, f]
                vec.tensor_tensor_scan(col, s["notlast"][:, ::-1], col, 0.0, ALU.mult, ALU.add).then_inc(v, 1)
            vec.wait_ge(pe, 2)
            vec.tensor_copy(s["fix"][:, 1, :], pc[:, P:P + AW]).then_inc(v, 1)


def edge_mlp(nc, s, dram):
    with ExitStack() as ctx:
        def sb(name, shape, dt=F32):
            return ctx.enter_context(nc.sbuf_tensor(f"m_{name}", shape, dt))

        def two(name, shape, dt=F32):
            return [sb(f"{name}{b}", shape, dt) for b in range(2)]

        def sem(name):
            return used(s, ctx.enter_context(nc.semaphore(f"m_{name}")))

        def ps(name):
            return ctx.enter_context(nc.psum_tensor(f"mp_{name}", [P, 512], F32))

        S2 = 2 * EH
        xd, h0, h1, x1 = (two(n, [P, EH, D]) for n in ("x", "h0_", "h1_", "x1_"))
        sq, sq2, hid = two("squares", [P, EH, D]), two("squares_b", [P, EH, D]), two("base", [P, EH, D])
        hT1, hT2, a1 = sb("h0_turned", [P, W]), sb("h1_turned", [P, W]), sb("mlp1", [P, W])
        tab, st, st2 = two("table_rows", [P, EH, TW]), two("stats", [P, 6, S2]), two("stats_b", [P, 6, EH])
        deg = [sb(f"deg{b}", [P, 2, EH]) for b in range(2)]
        ix = two("dst_now", [P, EH], I32)
        pt1, pt2, pa, pb1, pb2 = ps("turned1"), ps("turned2"), ps("mlp1p"), ps("mlp2p"), ps("vq")
        x_in, kept, scattered = ([sem(f"{n}{b}") for b in range(2)] for n in ("x_in", "kept", "scattered"))
        squared, squared2, varred, varred2 = sem("squared"), sem("squared2"), sem("varred"), sem("varred2")
        rooted, rooted2, scaled, scaled2 = sem("rooted"), sem("rooted2"), sem("scaled"), sem("scaled2")
        normed, normed2, summed = sem("normed"), sem("normed2"), sem("summed")
        turned1, turned2, mm1, mm2, mm3 = sem("turned1_"), sem("turned2_"), sem("mm1"), sem("mm2"), sem("mm3")
        copied1, copied2, relued = sem("copied1"), sem("copied2"), sem("relued")
        x1_done, tab_set, hid_done, q_done = sem("x1_done"), sem("tab_set"), sem("hid_done"), sem("q_done")
        v1, v2, v3, v5, v6 = (sem(f"steps{k}") for k in range(5))
        note_p, note_s, note_a = sem("note_p"), sem("note_s"), sem("note_a")
        extra, deg_moved = sem("extra"), sem("deg_moved")
        block = ctx.enter_context(nc.Block())

        @block.sync
        def _(sync):
            def body(n, b):
                if here(n):
                    passed(sync, x1_done, n - 1, note_s)
                    sync.dma_start(xd[b][:, :, :], dram["xd"][:, edge_cols(n), :]).then_inc(x_in[b], 16)
                m, o = n - 4, b
                if here(m):
                    passed(sync, hid_done, m + 1, note_s)
                    sync.dma_start(dram["base"][:, edge_cols(m), :], hid[o][:, :, :]).then_inc(kept[o], 16)

            turns(sync, body, 4)
            for b in range(2):
                sync.wait_ge(kept[b], 16 * NG)

        @block.gpsimd
        def _(pool):
            top = pool.to_reg(N - 1)

            def body(m, b):
                passed(pool, tab_set, 4 * m + 4, note_p)
                for k in range(EH):
                    pool.indirect_dma_start(
                        out=dram["table"],
                        out_offset=bass.IndirectOffsetOnAxis(ap=ix[b][0:EP, k:k + 1], axis=0),
                        in_=tab[b][0:EP, k, :], in_offset=None,
                        bounds_check=top, oob_is_err=False).then_inc(scattered[b], 16)

            turns(pool, body, 0)
            for b in range(2):
                pool.wait_ge(scattered[b], 16 * EH * NG)

        @block.scalar
        def _(act):
            def body(n, b):
                o = 1 - b
                if here(n - 1):
                    act.wait_ge(turned1, n)
                    act.activation(hT1[:, :], pt1[:, 0:W], ACT.Copy).then_inc(copied1, 1)
                if here(n - 3):
                    act.wait_ge(turned2, n - 2)
                    act.activation(hT2[:, :], pt2[:, 0:W], ACT.Copy).then_inc(copied2, 1)
                if here(n - 2):
                    act.wait_ge(x1_done, n - 1)
                    act.activation(sq2[b][:, :, :], x1[b][:, :, :], ACT.Square).then_inc(squared2, 1)
                if here(n - 1):
                    act.wait_ge(mm1, n)
                    act.activation(a1[:, :], pa[:, 0:W], ACT.Relu, bias=s["b1"][:, 0:1]).then_inc(relued, 1)
                if here(n):
                    act.wait_ge(x_in[b], 8 * (n - b + 2))
                    act.activation(sq[b][:, :, :], xd[b][:, :, :], ACT.Square).then_inc(squared, 1)
                if here(n - 2):
                    act.wait_ge(varred2, n - 1)
                    act.activation(st2[b][:, 3, :], st2[b][:, 2, :], ACT.Sqrt).then_inc(rooted2, 1)
                if here(n - 3):
                    act.wait_ge(deg_moved, n - 2)
                    passed(act, mm3, n - 2, note_a)
                    for k in range(EH):
                        ins = act.activation(s["Q"][:, bass.ds((n - 3) * EH + k, 1), :],
                                             pb2[:, k * 2 * D + D:(k + 1) * 2 * D].unsqueeze(1), ACT.Relu,
                                             scale=deg[o][:, 1, k:k + 1])
                    ins.then_inc(q_done, 1)
                if here(n - 2):
                    act.wait_ge(scaled2, n - 1)
                    for k in range(EH):
                        ins = act.activation(h1[b][:, k, :], x1[b][:, k, :], ACT.Relu,
                                             bias=st2[b][:, 5, k:k + 1], scale=st2[b][:, 4, k:k + 1])
                    ins.then_inc(normed2, 1)
                if here(n):
                    act.wait_ge(varred, n + 1)
                    act.activation(st[b][:, 3, :], st[b][:, 2, :], ACT.Sqrt).then_inc(rooted, 1)
                    act.wait_ge(scaled, n + 1)
                    for k in range(EH):
                        ins = act.activation(h0[b][:, k, :], xd[b][:, k, :], ACT.Relu,
                                             bias=st[b][:, 5, k:k + 1], scale=st[b][:, 4, k:k + 1])
                    ins.then_inc(normed, 1)

            turns(act, body, 3)

        @block.tensor
        def _(ten):
            def turn(pt, what, done):
                for k in range(EH // 2):
                    ins = ten.transpose(pt[:, k * P:(k + 1) * P], what[:, 2 * k:2 * k + 2, :], s["ident"][:, :])
                ins.then_inc(done, 1)

            def rows_out(pb, lhs, w, width, bias, n, done):
                ten.matmul(pb[:, 0:n * P], s["ones"][:, :], repeated(bias, n), start=True, stop=False,
                           skip_group_check=True)
                for k in range(EH // 2):
                    ins = ten.matmul(pb[:, k * width:(k + 1) * width], lhs[:, k * P:(k + 1) * P], w[:, :],
                                     start=False, stop=(k == EH // 2 - 1), skip_group_check=True)
                ins.then_inc(done, 1)

            def body(n, b):
                if here(n - 1):
                    ten.wait_ge(summed, n)
                    wait(ten, copied1, n - 1)
                    turn(pt1, h0[1 - b], turned1)
                if here(n - 3):
                    ten.wait_ge(normed2, n - 2)
                    wait(ten, copied2, n - 3)
                    turn(pt2, h1[1 - b], turned2)
                if here(n - 1):
                    ten.wait_ge(copied1, n)
                    wait(ten, relued, n - 1)
                    ten.matmul(pa[:, 0:W], s["W1"][:, :], hT1[:, :], start=True, stop=True).then_inc(mm1, 1)
                if here(n - 3):
                    ten.wait_ge(copied2, n - 2)
                    wait(ten, hid_done, n - 3)
                    rows_out(pb2, hT2, s["Wvq"], 4 * D, s["bvq"], EH, mm3)
                if here(n - 1):
                    ten.wait_ge(relued, n)
                    wait(ten, x1_done, n - 1)
                    rows_out(pb1, a1, s["W2"], P, s["b2"], EH // 2, mm2)

            turns(ten, body, 3)

        @block.vector
        def _(vec):
            def flat(t):
                return t[:, :, :].rearrange("p j f -> p (j f)")

            def body(n, b):
                o = 1 - b
                if here(n - 1):
                    vec.wait_ge(normed, n)
                    vec.tensor_tensor(h0[o][:, :, :], h0[o][:, :, :], s["AG"][:, bass.ds((n - 1) * EH + 1, EH), 0:D],
                                      ALU.add).then_inc(summed, 1)
                if here(n - 2):
                    vec.wait_ge(squared2, n - 1)
                    norm_stats(Chain(vec, v2, n - 2, 5), varred2, st2[b], EH,
                               [(0, EH, x1[b][:, :, :])], sq2[b][:, :, :])
                if here(n - 3):
                    m = n - 3
                    wait(vec, scattered[o], 8 * EH * (m - o))
                    vec.wait_ge(deg_moved, m + 1)
                    vec.tensor_copy(tab[o][:, :, D], deg[o][:, 1, :]).then_inc(tab_set, 1)
                    vec.tensor_copy(tab[o][:, :, D + 1], s["slots"][:, edge_cols(m)]).then_inc(tab_set, 1)
                    vec.tensor_copy(ix[o][:, :], s["dst_end"][:, edge_cols(m)]).then_inc(tab_set, 1)
                    vec.wait_ge(normed2, m + 1)
                    vec.tensor_copy(tab[o][:, :, 0:D], h1[o][:, :, :]).then_inc(tab_set, 1)
                if here(n):
                    ch = Chain(vec, v1, n, 2 * EH)
                    for which, flags in ((0, "first"), (1, "trail")):
                        for k in range(EH):
                            now = s["AG"][:, bass.ds(n * EH + k + 1, 1), :]
                            ch.step(vec.scalar_tensor_tensor(now, s["fix"][:, which:which + 1, :],
                                                             s[flags][:, bass.ds(n * EH + k, 1)], now,
                                                             ALU.mult, ALU.add))
                        ch.wait()
                if here(n - 2):
                    vec.wait_ge(rooted2, n - 1)
                    norm_scales(Chain(vec, v3, n - 2, 1), scaled2, st2[b], EH)
                if here(n):
                    vec.wait_ge(x_in[b], 8 * (n - b + 2))
                    vec.wait_ge(squared, n + 1)
                    ch = Chain(vec, v5, n, 6)
                    ch.step(vec.tensor_copy(st[b][:, 2, EH:S2], s["AG"][:, bass.ds(n * EH + 1, EH), D]))
                    norm_stats(ch, varred, st[b], EH, [(0, EH, xd[b][:, :, :])], sq[b][:, :, :])
                if here(n - 3):
                    m = n - 3
                    vec.wait_ge(q_done, m + 1)
                    wait(vec, kept[o], 8 * (m - o))
                    vec.tensor_tensor(hid[o][:, :, :], pb2[:, :].rearrange("p (j f) -> p j f", f=2 * D)[:, :, 0:D],
                                      x1[o][:, :, :], ALU.add).then_inc(hid_done, 1)
                    if isinstance(m, int) and m == 0:
                        vec.wait_ge(hid_done, 1)
                        vec.tensor_copy(s["xbase"][:, :], hid[0][:, 0, :]).then_inc(extra, 1)
                if here(n - 1):
                    vec.wait_ge(mm2, n)
                    wait(vec, hid_done, n - 2)
                    vec.scalar_tensor_tensor(flat(x1[o]), pb1[:, 0:W], 0.0, flat(xd[o]),
                                             ALU.max, ALU.add).then_inc(x1_done, 1)
                if here(n - 2):
                    vec.tensor_copy(deg[b][:, 1, :], deg[b][:, 0, :]).then_inc(deg_moved, 1)
                if here(n):
                    vec.wait_ge(rooted, n + 1)
                    ch = Chain(vec, v6, n, 2)
                    norm_scales(ch, scaled, st[b], EH)
                    ch.step(vec.tensor_copy(deg[b][:, 0, :], st[b][:, 4, EH:S2]))

            turns(vec, body, 3)


def ihj(ap):
    return ap.rearrange("p (h i j) -> p h i j", h=HEADS, i=HD)


def over_j(ap):
    return ap.rearrange("p (h i) -> p h i", i=HD).unsqueeze(3).to_broadcast([P, HEADS, HD, HD])


def over_i(ap):
    return ap.rearrange("p (h j) -> p h j", j=HD).unsqueeze(2).to_broadcast([P, HEADS, HD, HD])


def state_rows(dram_t, m):
    return dram_t[bass.ds(m * (EH * P), EH * P), :].rearrange("(j p) f -> p j f", p=P)


def hop_zero(nc, s, dram, edge_attr, retired):
    with ExitStack() as ctx:
        def sb(name, shape, dt=F32):
            return ctx.enter_context(nc.sbuf_tensor(f"z_{name}", shape, dt))

        def two(name, shape, dt=F32):
            return [sb(f"{name}{b}", shape, dt) for b in range(2)]

        def sem(name):
            return ctx.enter_context(nc.semaphore(f"z_{name}"))

        tg, ef = two("table", [P, EH, TW]), two("edge", [P, EH, D])
        hT = sb("turned", [TW, EH * P])
        kj, vs, kq, g = (two(n, [P, EH, D]) for n in ("kj", "v", "kq", "g"))
        sc, wn, ix = two("s", [P, EH * HEADS]), two("wn", [P, EH]), two("src_now", [P, EH], I32)
        pr, acc = two("outer", [P, MW]), two("acc", [P, EH, MW])
        pt = ctx.enter_context(nc.psum_tensor("z_p_turned", [P, 512], F32))
        pk = [ctx.enter_context(nc.psum_tensor(f"z_p_kv{b}", [P, 512], F32)) for b in range(2)]
        row_in, ef_in, stored, g_kept = ([sem(f"{n}{b}") for b in range(2)]
                                         for n in ("row_in", "ef_in", "stored", "g_kept"))
        idx_set, turned, copied, kv = sem("idx_set"), sem("turned_"), sem("copied"), sem("kv")
        wn_set, k_sum, v_done, k_done = sem("wn_set"), sem("k_sum"), sem("v_done"), sem("k_done")
        acc_done, g_done, v, v2, zeroed = sem("acc_done"), sem("g_done"), sem("steps"), sem("steps2"), sem("zeroed")
        note_p, note_s = sem("note_p"), sem("note_s")
        ended = sem("ended")
        block = ctx.enter_context(nc.Block())
        ef_rows = edge_attr.rearrange("(p t) f -> p t f", t=T)

        @block.sync
        def _(sync):
            def body(n, b):
                if here(n):
                    passed(sync, k_sum, n - 1, note_s)
                    for p0, p1 in ((0, 112), (112, EP)):
                        sync.dma_start(ef[b][p0:p1, :, :], ef_rows[p0:p1, edge_cols(n), :]).then_inc(ef_in[b], 16)
                m, o = n - 2, b
                if here(m):
                    passed(sync, g_done, m + 1, note_s)
                    sync.dma_start(dram["g"][0][:, edge_cols(m), :], g[o][:, :, :]).then_inc(g_kept[o], 16)
                    passed(sync, acc_done, EH * (m + 1), note_s)
                    sync.dma_start(state_rows(dram["M0"], m), acc[o][:, :, :]).then_inc(stored[o], 16)

            sync.wait_ge(zeroed, 1)
            turns(sync, body, 2)
            for b in range(2):
                sync.wait_ge(stored[b], 16 * NG)
                sync.wait_ge(g_kept[b], 16 * NG)

        @block.gpsimd
        def _(pool):
            for old in retired:
                pool.sem_clear(old)
            top = pool.to_reg(N - 1)

            def body(n, b):
                passed(pool, idx_set, n + 1, note_p)
                for k in range(EH):
                    pool.indirect_dma_start(
                        out=tg[b][0:EP, k, :], out_offset=None, in_=dram["table"],
                        in_offset=bass.IndirectOffsetOnAxis(ap=ix[b][0:EP, k:k + 1], axis=0),
                        bounds_check=top, oob_is_err=False).then_inc(row_in[b], 16)

            turns(pool, body, 0)

        @block.tensor
        def _(ten):
            def body(n, b):
                ten.wait_ge(row_in[b], 8 * EH * (n - b + 2))
                wait(ten, copied, n)
                for k in range(EH):
                    ins = ten.transpose(pt[0:TW, k * P:(k + 1) * P], tg[b][:, k, :], s["ident"][:, :])
                ins.then_inc(turned, 1)
                wait(ten, v_done, n - 1)
                ten.matmul(pk[b][:, :], s["ones"][:, :], repeated(s["bkv"], EH), start=True, stop=False,
                           skip_group_check=True)
                ten.wait_ge(copied, n + 1)
                for k in range(EH):
                    ins = ten.matmul(pk[b][:, k * P:(k + 1) * P], hT[:, k * P:(k + 1) * P],
                                     s["Wkv"][0:TW, :], start=False, stop=(k == EH - 1), skip_group_check=True)
                ins.then_inc(kv, 1)

            ten.wait_ge(zeroed, 1)
            turns(ten, body, 0)

        @block.scalar
        def _(act):
            def body(n, b):
                act.wait_ge(turned, n + 1)
                act.activation(hT[:, :], pt[0:TW, :], ACT.Copy).then_inc(copied, 1)
                act.wait_ge(k_sum, n + 1)
                wait(act, acc_done, EH * (n - 1))
                act.activation(kj[b][:, :, :], kj[b][:, :, :], ACT.Relu).then_inc(k_done, 1)
                for k in range(EH):
                    ins = act.activation(vs[b][:, k, :], pk[b][:, (2 * k + 1) * D:(2 * k + 2) * D], ACT.Copy,
                                         scale=wn[b][:, k:k + 1])
                ins.then_inc(v_done, 1)

            turns(act, body, 0)

        @block.vector
        def _(vec):
            def set_index(m, b):
                vec.tensor_copy(ix[b][:, :], s["src"][:, edge_cols(m)]).then_inc(idx_set, 1)

            def heavy(m, o, ch, k):
                t = m * EH + k
                out_ = pr[k % 2]
                ch.step(vec.tensor_tensor(ihj(out_[:, :]), over_j(kj[o][:, k, :]), over_i(vs[o][:, k, :]), ALU.mult))
                ch.wait()
                before = acc[o][:, k - 1, :] if k else acc[1 - o][:, EH - 1, :]
                wait(vec, acc_done, EH * m + k)
                vec.scalar_tensor_tensor(acc[o][:, k, :], before, s["same"][:, bass.ds(t, 1)], out_[:, :],
                                         ALU.mult, ALU.add).then_inc(acc_done, 1)

            def body(n, b):
                o = 1 - b
                m = n - 1
                if here(m):
                    ch = Chain(vec, v, m, 2 + EH)
                    vec.wait_ge(k_done, m + 1)
                    ch.step(vec.tensor_tensor(kq[o][:, :, :], kj[o][:, :, :], s["Q"][:, edge_cols(m), :], ALU.mult))
                    ch.wait()
                    ch.step(vec.tensor_reduce(sc[o][:, :], kq[o][:, :, :].rearrange("p t (h i) -> p (t h) i", i=HD),
                                              AX.X, ALU.add))
                    vec.wait_ge(v_done, m + 1)
                    wait(vec, stored[o], 8 * (m - o))
                    wait(vec, g_kept[o], 8 * (m - o))
                    heavy(m, o, ch, 0)
                    vec.tensor_tensor(
                        g[o][:, :, :].rearrange("p t (h j) -> p t h j", j=HD),
                        vs[o][:, :, :].rearrange("p t (h j) -> p t h j", j=HD),
                        sc[o][:, :].rearrange("p (t h) -> p t h", h=HEADS).unsqueeze(3).to_broadcast([P, EH, HEADS, HD]),
                        ALU.mult).then_inc(g_done, 1)
                    heavy(m, o, ch, 1)
                if here(n):
                    ch2 = Chain(vec, v2, n, 2)
                    vec.wait_ge(row_in[b], 8 * EH * (n - b + 2))
                    vec.tensor_tensor(wn[b][:, :], s["w"][:, edge_cols(n)], tg[b][:, :, D], ALU.mult).then_inc(wn_set, 1)
                    ch2.step(vec.tensor_copy(s["sidx"][:, edge_cols(n)], tg[b][:, :, D + 1]))
                    vec.wait_ge(wn_set, n + 1)
                    ch2.step(vec.tensor_tensor(s["wn"][:, edge_cols(n)], wn[b][:, :], tg[b][:, :, D], ALU.mult))
                    vec.wait_ge(kv, n + 1)
                    if here(n + 2):
                        ch2.wait()
                        set_index(n + 2, b)
                    vec.wait_ge(ef_in[b], 16 * (n - b + 2))
                    vec.tensor_tensor(kj[b][:, :, :], pk[b][:, :].rearrange("p (j f) -> p j f", f=2 * D)[:, :, 0:D],
                                      ef[b][:, :, :], ALU.add).then_inc(k_sum, 1)
                if here(m):
                    heavy(m, o, ch, 2)
                    heavy(m, o, ch, 3)

            for b in range(2):
                vec.memset(tg[b][:, :, :], 0.0)
                vec.memset(ef[b][:, :, :], 0.0)
                vec.memset(acc[b][:, :, :], 0.0)
                set_index(b, b)
            vec.drain().then_inc(zeroed, 1)
            vec.wait_ge(zeroed, 1)
            turns(vec, body, 1)
            vec.wait_ge(acc_done, T)
            vec.tensor_copy(s["acc_end"][:, :], acc[1][:, EH - 1, :]).then_inc(ended, 1)


def hop_next(nc, s, dram, hop):
    keep = hop < HOPS - 1
    with ExitStack() as ctx:
        def sb(name, shape, dt=F32):
            return ctx.enter_context(nc.sbuf_tensor(f"n{hop}_{name}", shape, dt))

        def two(name, shape, dt=F32):
            return [sb(f"{name}{b}", shape, dt) for b in range(2)]

        def sem(name):
            return ctx.enter_context(nc.semaphore(f"n{hop}_{name}"))

        mg = two("state", [P, EH, MW])
        pr = two("product", [P, EH, MW])
        acc = two("acc", [P, EH, MW]) if keep else None
        g, ix = two("g", [P, EH, D]), two("slot_now", [P, EH], I32)
        pg = [ctx.enter_context(nc.psum_tensor(f"n{hop}_heads{b}", [P, 512], F32)) for b in range(2)]
        row_in = [[sem(f"row_in{b}_{k}") for k in range(EH)] for b in range(2)]
        stored, g_kept = ([sem(f"{n}{b}") for b in range(2)] for n in ("stored", "g_kept"))
        idx_set, weighted, multiplied, headed = sem("idx_set"), sem("weighted"), sem("multiplied"), sem("headed")
        acc_done, g_done, zeroed, note_p, note_s = sem("acc_done"), sem("g_done"), sem("zeroed"), sem("note_p"), sem("note_s")
        extra, note_a, ended = sem("extra"), sem("note_a"), sem("ended")
        block = ctx.enter_context(nc.Block())

        @block.sync
        def _(sync):
            def body(n, b):
                if keep and here(n):
                    passed(sync, acc_done, EH * (n + 1), note_s)
                    sync.dma_start(state_rows(dram[f"M{hop}"], n), acc[b][:, :, :]).then_inc(stored[b], 16)
                m, o = n - 1, 1 - b
                if here(m):
                    passed(sync, g_done, m + 1, note_s)
                    sync.dma_start(dram["g"][hop][:, edge_cols(m), :], g[o][:, :, :]).then_inc(g_kept[o], 16)

            turns(sync, body, 1)
            for b in range(2):
                if keep:
                    sync.wait_ge(stored[b], 16 * NG)
                sync.wait_ge(g_kept[b], 16 * NG)

        @block.gpsimd
        def _(pool):
            top = pool.to_reg(SLOTS - 1)

            def body(n, b):
                passed(pool, idx_set, n + 1, note_p)
                for k in range(EH):
                    passed(pool, multiplied, EH * (n - 2) + k + 1, note_p)
                    pool.indirect_dma_start(
                        out=mg[b][0:EP, k, :], out_offset=None, in_=dram[f"M{hop - 1}"],
                        in_offset=bass.IndirectOffsetOnAxis(ap=ix[b][0:EP, k:k + 1], axis=0),
                        bounds_check=top, oob_is_err=False).then_inc(row_in[b][k], 16)

            turns(pool, body, 2)

        @block.scalar
        def _(act):
            def body(n, b):
                if here(n):
                    for k in range(EH):
                        act.wait_ge(row_in[b][k], 8 * (n - b + 2))
                        act.activation(mg[b][:, k:k + 1, :], mg[b][:, k:k + 1, :], ACT.Copy,
                                       scale=s["wn"][:, bass.ds(n * EH + k, 1)]).then_inc(weighted, 1)
                m, o = n - 1, 1 - b
                if here(m):
                    act.wait_ge(headed, m + 1)
                    wait(act, g_kept[o], 8 * (m - o))
                    if not keep:
                        act.wait_ge(extra, EH * (m + 1))
                    act.activation(g[o][:, :, :].rearrange("p t f -> p (t f)"), pg[o][:, 0:W], ACT.Copy).then_inc(g_done, 1)

            turns(act, body, 1)

        @block.tensor
        def _(ten):
            def body(n, b):
                ten.wait_ge(multiplied, EH * (n + 1))
                wait(ten, g_done, n - 1)
                heads = pg[b][:, 0:W].rearrange("p (t f) -> p t f", f=D)
                for r in range(HD):
                    part = pr[b][:, :, :].rearrange("p t (h i j) -> p (t h) i j", h=HEADS, i=HD)[:, :, r, :]
                    ins = ten.matmul(pg[b][:, 0:W].rearrange("p (c j) -> p c j", j=HD), s["ident"][:, :], part,
                                     start=(r == 0), stop=(r == HD - 1))
                ins.then_inc(headed, 1)

            turns(ten, body, 0)

        @block.vector
        def _(vec):
            def set_index(m, b):
                vec.tensor_copy(ix[b][:, :], s["sidx"][:, edge_cols(m)]).then_inc(idx_set, 1)

            def body(n, b):
                if here(n):
                    wait(vec, headed, n - 1)
                    if keep:
                        wait(vec, stored[b], 8 * (n - b))
                    for k in range(EH):
                        t = n * EH + k
                        vec.wait_ge(weighted, EH * n + k + 1)
                        if keep:
                            before = acc[b][:, k - 1, :] if k else acc[1 - b][:, EH - 1, :]
                            wait(vec, acc_done, EH * n + k)
                            vec.scalar_tensor_tensor(acc[b][:, k, :], before, s["same"][:, bass.ds(t, 1)],
                                                     mg[b][:, k, :], ALU.mult, ALU.add).then_inc(acc_done, 1)
                        vec.tensor_tensor(
                            ihj(pr[b][:, k, :]), ihj(mg[b][:, k, :]),
                            over_j(s["Q"][:, bass.ds(t, 1), :].rearrange("p t f -> p (t f)")),
                            ALU.mult).then_inc(multiplied, 1)
                        if k == EH - 1 and here(n + 2):
                            set_index(n + 2, b)
                m, o = n - 1, 1 - b
                if not keep and here(m):
                    vec.wait_ge(headed, m + 1)
                    for k in range(EH):
                        wait(vec, extra, EH * m + k)
                        gx = s["gx"][:, hop, :]
                        vec.scalar_tensor_tensor(gx, pg[o][:, k * D:(k + 1) * D], s["first"][:, bass.ds(m * EH + k, 1)],
                                                 gx, ALU.mult, ALU.add).then_inc(extra, 1)

            for b in range(2):
                vec.memset(mg[b][:, :, :], 0.0)
                if keep:
                    vec.memset(acc[b][:, :, :], 0.0)
            vec.drain().then_inc(zeroed, 1)
            vec.wait_ge(zeroed, 1)
            for b in range(2):
                set_index(b, b)
            turns(vec, body, 1)
            if keep:
                vec.wait_ge(acc_done, T)
                vec.tensor_copy(s["acc_end"][:, :], acc[1][:, EH - 1, :]).then_inc(ended, 1)


def hop_end(nc, s, dram, hop):
    with ExitStack() as ctx:
        def sb(name, shape, dt=F32):
            return ctx.enter_context(nc.sbuf_tensor(f"e{hop}_{name}", shape, dt))

        def sem(name):
            return ctx.enter_context(nc.semaphore(f"e{hop}_{name}"))

        row, prod = sb("first_state", [P, MW]), sb("first_product", [P, MW])
        pc = ctx.enter_context(nc.psum_tensor(f"e{hop}_carry", [P, 512], F32))
        carried, got, fixed, put, v, zeroed = (sem("carried"), sem("got"), sem("fixed"), sem("put"), sem("steps"),
                                               sem("zeroed"))
        block = ctx.enter_context(nc.Block())

        @block.tensor
        def _(ten):
            ten.matmul(pc[:, :], s["carry"][:, :], s["acc_end"][:, :], start=True, stop=True).then_inc(carried, 1)

        @block.gpsimd
        def _(pool):
            top = pool.to_reg(SLOTS - 1)
            slot = bass.IndirectOffsetOnAxis(ap=s["slot_x"][0:EP, 0:1], axis=0)
            pool.wait_ge(zeroed, 1)
            pool.indirect_dma_start(out=row[0:EP, :], out_offset=None, in_=dram[f"M{hop}"], in_offset=slot,
                                    bounds_check=top, oob_is_err=False).then_inc(got, 16)
            pool.wait_ge(fixed, 1)
            pool.indirect_dma_start(out=dram[f"M{hop}"], out_offset=slot, in_=row[0:EP, :], in_offset=None,
                                    bounds_check=top, oob_is_err=False).then_inc(put, 16)
            pool.wait_ge(put, 16)

        @block.vector
        def _(vec):
            vec.memset(row[:, :], 0.0).then_inc(zeroed, 1)
            vec.wait_ge(carried, 1)
            vec.wait_ge(got, 16)
            vec.wait_ge(zeroed, 1)
            vec.tensor_tensor(row[:, :], row[:, :], pc[:, :], ALU.add).then_inc(fixed, 1)
            vec.wait_ge(fixed, 1)
            vec.tensor_tensor(ihj(prod[:, :]), ihj(row[:, :]), over_j(s["Q"][:, 0, :]), ALU.mult).then_inc(v, 1)
            vec.wait_ge(v, 1)
            vec.tensor_reduce(s["gx"][:, hop, :], prod[:, :].rearrange("p (h i j) -> p h j i", h=HEADS, i=HD),
                              AX.X, ALU.add).then_inc(v, 1)


def write_out(nc, s, dram, out):
    with ExitStack() as ctx:
        def sb(name, shape, dt=F32):
            return ctx.enter_context(nc.sbuf_tensor(f"o_{name}", shape, dt))

        def two(name, shape, dt=F32):
            return [sb(f"{name}{b}", shape, dt) for b in range(2)]

        def sem(name):
            return ctx.enter_context(nc.semaphore(f"o_{name}"))

        NH = HOPS * EH * HEADS
        base = two("base", [P, EH, D])
        gg = two("g", [P, HOPS, EH, D])
        sq, q, row, ix = two("squares", [P, NH, HD]), two("norms", [P, 4, NH]), two("rows", [P, EH, D]), two("dst", [P, EH], I32)
        fac = sb("factors", [P, NH])
        psr = [ctx.enter_context(nc.psum_tensor(f"o_p_rows{b}", [P, 512], F32)) for b in range(2)]
        pc = ctx.enter_context(nc.psum_tensor("o_carry", [P, 512], F32))
        loaded, put = ([sem(f"{n}{b}") for b in range(2)] for n in ("loaded", "put"))
        chained, squared, clamped, rooted, scaled, added = (sem("chained"), sem("squared"), sem("clamped"),
                                                            sem("rooted"), sem("scaled"), sem("added"))
        rows_set, idx_set, note_p, note_s, note_c, v, v2 = (sem("rows_set"), sem("idx_set"), sem("note_p"), sem("note_s"), sem("note_c"),
                                                    sem("steps"), sem("steps2"))
        zeroed, prep, x_steps, x_act, x_pe, x_put = sem("zeroed"), sem("prep"), sem("x_steps"), sem("x_act"), sem("x_pe"), sem("x_put")
        block = ctx.enter_context(nc.Block())

        @block.sync
        def _(sync):
            def body(n, b):
                passed(sync, added, n - 1, note_s)
                passed(sync, chained, EH * (n - 1) + 1, note_c)
                sync.dma_start(base[b][:, :, :], dram["base"][:, edge_cols(n), :]).then_inc(loaded[b], 16)
                for k in range(HOPS):
                    sync.dma_start(gg[b][:, k, :, :], dram["g"][k][:, edge_cols(n), :]).then_inc(loaded[b], 16)

            turns(sync, body, 0)

        @block.gpsimd
        def _(pool):
            top = pool.to_reg(N - 1)

            def body(m, b):
                passed(pool, rows_set, m + 1, note_p)
                passed(pool, idx_set, m + 1, note_p)
                for k in range(EH):
                    pool.indirect_dma_start(
                        out=out, out_offset=bass.IndirectOffsetOnAxis(ap=ix[b][0:EP, k:k + 1], axis=0),
                        in_=row[b][0:EP, k, :], in_offset=None,
                        bounds_check=top, oob_is_err=False).then_inc(put[b], 16)

            turns(pool, body, 0)
            pool.wait_ge(x_steps, X_STEPS)
            pool.indirect_dma_start(out=out, out_offset=bass.IndirectOffsetOnAxis(ap=s["dst_x"][0:EP, 0:1], axis=0),
                                    in_=s["xbase"][0:EP, :], in_offset=None,
                                    bounds_check=top, oob_is_err=False).then_inc(x_put, 16)
            for b in range(2):
                pool.wait_ge(put[b], 16 * EH * NG)
            pool.wait_ge(x_put, 16)

        @block.scalar
        def _(act):
            def body(n, b):
                o = 1 - b
                if here(n):
                    act.wait_ge(chained, EH * (n + 1))
                    act.activation(sq[b][:, :, :].rearrange("p c j -> p (c j)"),
                                   gg[b][:, :, :, :].rearrange("p c t f -> p (c t f)"), ACT.Square).then_inc(squared, 1)
                if here(n - 1):
                    act.wait_ge(added, n)
                    wait(act, put[o], 8 * EH * (n - 1 - o))
                    act.activation(row[o][:, :, :].rearrange("p t f -> p (t f)"), psr[o][:, 0:W], ACT.Copy).then_inc(rows_set, 1)
                if here(n):
                    act.wait_ge(clamped, n + 1)
                    act.activation(q[b][:, 1, :], q[b][:, 0, :], ACT.Sqrt).then_inc(rooted, 1)

            turns(act, body, 1)
            act.wait_ge(x_steps, 2)
            act.activation(sq[0][:, 0:HOPS * HEADS, :], s["gx"][:, :, :].rearrange("p k (h j) -> p (k h) j", j=HD),
                           ACT.Square).then_inc(x_act, 1)
            act.wait_ge(x_steps, 4)
            act.activation(q[0][:, 1, 0:HOPS * HEADS], q[0][:, 0, 0:HOPS * HEADS], ACT.Sqrt).then_inc(x_act, 1)

        @block.tensor
        def _(ten):
            def body(m, b):
                ten.wait_ge(scaled, m + 1)
                wait(ten, rows_set, m - 1)
                ten.matmul(psr[b][:, 0:W], s["ident"][:, :], base[b][:, :, :].rearrange("p t f -> p (t f)"),
                           start=True, stop=False)
                for k in range(HOPS):
                    ins = ten.matmul(psr[b][:, 0:W], s["ident"][:, :], gs[b][:, k, :],
                                     start=False, stop=(k == HOPS - 1))
                ins.then_inc(added, 1)

            gs = [x[:, :, :].rearrange("p (k c) j -> p k (c j)", k=HOPS) for x in sq]
            turns(ten, body, 0)
            ten.wait_ge(chained, T)
            ten.matmul(pc[:, 0:D], s["carry"][:, :], gg[1][:, HOPS - 1, EH - 1, :], start=True, stop=True).then_inc(x_pe, 1)

        @block.vector
        def _(vec):
            def body(n, b):
                o = 1 - b
                if here(n):
                    vec.wait_ge(loaded[b], 8 * (HOPS + 1) * (n - b + 2))
                    for k in range(EH):
                        before = gg[b][:, :, k - 1, :] if k else gg[o][:, :, EH - 1, :]
                        wait(vec, chained, EH * n + k)
                        vec.scalar_tensor_tensor(gg[b][:, :, k, :], before, s["same"][:, bass.ds(n * EH + k, 1)],
                                                 gg[b][:, :, k, :], ALU.mult, ALU.add).then_inc(chained, 1)
                    wait(vec, put[b], 8 * EH * (n - b))
                    vec.tensor_copy(ix[b][:, :], s["dst_out"][:, edge_cols(n)]).then_inc(idx_set, 1)
                if here(n - 1):
                    vec.wait_ge(rooted, n)
                    ch = Chain(vec, v, n - 1, 2)
                    ch.step(vec.reciprocal(q[o][:, 2, :], q[o][:, 1, :]))
                    ch.wait()
                    ch.step(vec.tensor_tensor(q[o][:, 3, :], q[o][:, 2, :], fac[:, :], ALU.mult))
                    ch.wait()
                    vec.tensor_tensor(sq[o][:, :, :], gg[o][:, :, :, :].rearrange("p k t (h j) -> p (k t h) j", j=HD),
                                      q[o][:, 3, :].unsqueeze(2).to_broadcast([P, NH, HD]), ALU.mult).then_inc(scaled, 1)
                if here(n):
                    vec.wait_ge(squared, n + 1)
                    ch = Chain(vec, v2, n, 1)
                    ch.step(vec.tensor_reduce(q[b][:, 2, :], sq[b][:, :, :], AX.X, ALU.add))
                    ch.wait()
                    vec.tensor_scalar(q[b][:, 0, :], q[b][:, 2, :], 1.0 / HD, 1.0, ALU.mult, ALU.max).then_inc(clamped, 1)

            vec.memset(gg[1][:, :, EH - 1, :], 0.0).then_inc(zeroed, 1)
            vec.wait_ge(zeroed, 1)
            for k in range(HOPS):
                c = slice(k * EH * HEADS, (k + 1) * EH * HEADS)
                vec.tensor_copy(fac[:, c], s["hop"][:, k + 1:k + 2].to_broadcast([P, EH * HEADS])).then_inc(prep, 1)
            vec.wait_ge(prep, HOPS)
            turns(vec, body, 1)
            n = [0]

            def step(ins):
                ins.then_inc(x_steps, 1)
                n[0] += 1
                vec.wait_ge(x_steps, n[0])

            XH = HOPS * HEADS
            gx = s["gx"][:, HOPS - 1, :]
            vec.wait_ge(x_pe, 1)
            step(vec.tensor_tensor(gx, gx, pc[:, 0:D], ALU.add))
            vec.wait_ge(scaled, UNITS)
            vec.wait_ge(added, UNITS)
            for k in range(HOPS):
                ins = vec.tensor_copy(fac[:, k * HEADS:(k + 1) * HEADS], s["hop"][:, k + 1:k + 2].to_broadcast([P, HEADS]))
            step(ins)
            vec.wait_ge(x_act, 1)
            step(vec.tensor_reduce(q[0][:, 2, 0:XH], sq[0][:, 0:XH, :], AX.X, ALU.add))
            step(vec.tensor_scalar(q[0][:, 0, 0:XH], q[0][:, 2, 0:XH], 1.0 / HD, 1.0, ALU.mult, ALU.max))
            vec.wait_ge(x_act, 2)
            step(vec.reciprocal(q[0][:, 2, 0:XH], q[0][:, 1, 0:XH]))
            step(vec.tensor_tensor(q[0][:, 3, 0:XH], q[0][:, 2, 0:XH], fac[:, 0:XH], ALU.mult))
            step(vec.tensor_tensor(sq[0][:, 0:XH, :], s["gx"][:, :, :].rearrange("p k (h j) -> p (k h) j", j=HD),
                                   q[0][:, 3, 0:XH].unsqueeze(2).to_broadcast([P, XH, HD]), ALU.mult))
            for k in range(HOPS):
                step(vec.tensor_tensor(s["xbase"][:, :], s["xbase"][:, :],
                                       sq[0][:, k * HEADS:(k + 1) * HEADS, :].rearrange("p c j -> p (c j)"), ALU.add))
            assert n[0] == X_STEPS


INPUTS = ["x", "src", "dst", "edge_attr_64", "edge_weight", "L0_gnn_W1", "L0_gnn_b1", "L0_gnn_W2", "L0_gnn_b2",
          "L1_gnn_Wq", "L1_gnn_bq", "L1_gnn_Wk", "L1_gnn_bk", "L1_gnn_Wv", "L1_gnn_bv", "L1_gnn_hopwise"]


def kernel(**inputs):
    import concourse.bacc as bacc
    from concourse.bass_utils import run_bass_kernel_spmd

    nc = bacc.Bacc("TRN2", target_bir_lowering=False, num_devices=1)
    r, c = np.arange(P)[:, None], np.arange(P)[None, :]
    constants = {
        "mats": np.concatenate([r == c, c > r, r == c + 1], axis=1).astype(np.float32),
        "slots": (np.arange(T)[None, :] * P + r).astype(np.float32),
    }
    arrays, args = {}, []
    for name, a in [(n, inputs[n]) for n in INPUTS] + list(constants.items()):
        a = np.ascontiguousarray(a)
        arrays[f"in_{name}"] = a
        args.append(nc.dram_tensor(f"in_{name}", a.shape, mybir.dt.from_np(a.dtype), kind="ExternalInput").ap())
    args.append(nc.dram_tensor("out", (N, D), F32, kind="ExternalOutput").ap())
    gnn(nc, *args)
    r = run_bass_kernel_spmd(nc, [arrays], core_ids=[0])
    return r.results[0]["out"]
```

```python
from contextlib import ExitStack

import numpy as np

import concourse.bass as bass
from concourse import mybir

F32 = mybir.dt.float32
BF16 = mybir.dt.bfloat16
I32 = mybir.dt.int32
ALU = mybir.AluOpType
ACT = mybir.ActivationFunctionType
AX = mybir.AxisListType

P = 128
N = 50000
E = 25000
D = 64
HEADS, HD = 8, 8
MW = HEADS * HD * HD
HOPS = 3
EPS = 1e-5

EP = 125
T = E // EP
SLOTS = T * P
AW = D + 1
TW = D + 2
NO_ROW = 1 << 20

NT = 16
NG = 25
GSTEP = (N - NT * P) // (NG - 1)
HT = NT // 2
ET = T // NG
EH = ET // 2

UNITS = 2 * NG
R = 4
W = EH * D
X_STEPS = 9


def here(m):
    return not isinstance(m, int) or 0 <= m < UNITS


def wait(eng, sem, value):
    if not isinstance(value, int) or value > 0:
        eng.wait_ge(sem, value)


def passed(eng, sem, value, note):
    if not isinstance(value, int) or value > 0:
        eng.wait_ge(sem, value)
        eng.sem_inc(note, 1)


def turns(eng, body, behind, ring=2):
    lead = -(-(behind + ring) // ring)
    for m in range(lead * ring):
        body(m, m % ring)
    with eng.Fori(lead, UNITS // ring) as i:
        for b in range(ring):
            body(ring * i + b, b)
    for m in range(UNITS // ring * ring, UNITS + behind):
        body(m, m % ring)


def before_unit(m, b, count):
    return (m - b) * (count // R)


def with_unit(m, b, count):
    return (m - b + R) * (count // R)


def units_in(b):
    return len(range(b, UNITS, R))


class Chain:

    def __init__(self, eng, sem, m, steps):
        self.eng, self.sem, self.base, self.steps, self.n = eng, sem, m * steps, steps, 0

    def step(self, ins):
        ins.then_inc(self.sem, 1)
        self.n += 1
        assert self.n <= self.steps

    def wait(self, ago=0):
        wait(self.eng, self.sem, self.base + self.n - ago)


def edge_cols(m):
    return bass.ds(m * EH, EH)


def norm_stats(ch, sums, varred, q, n, between):
    vec = ch.eng
    between(0)
    for reduced in sums:
        reduced.wait()
    ch.step(vec.tensor_scalar(q[:, 0, 0:n], q[:, 0, 0:n], 1.0 / D, None, ALU.mult))
    between(1)
    ch.wait()
    ch.step(vec.tensor_tensor(q[:, 2, 0:n], q[:, 0, 0:n], q[:, 0, 0:n], ALU.mult))
    between(2)
    ch.wait()
    ch.step(vec.scalar_tensor_tensor(q[:, 1, 0:n], q[:, 1, 0:n], 1.0 / D, q[:, 2, 0:n],
                                     ALU.mult, ALU.subtract))
    between(3)
    ch.wait()
    vec.tensor_scalar(q[:, 2, 0:n], q[:, 1, 0:n], 0.0, EPS, ALU.max, ALU.add).then_inc(varred, 1)


def norm_scales(ch, scaled, q, n):
    vec = ch.eng
    ch.step(vec.reciprocal(q[:, 4, :], q[:, 3, :]))
    ch.wait()
    vec.scalar_tensor_tensor(q[:, 5, 0:n], q[:, 0, 0:n], -1.0, q[:, 4, 0:n],
                             ALU.mult, ALU.mult).then_inc(scaled, 1)


def gnn(nc, x, src, dst, edge_attr, edge_weight, W1, b1, W2, b2, Wq, bq, Wk, bk, Wv, bv, hopwise,
        mats, slots, out):
    dram = {
        "table": nc.dram_tensor("node_table", (N, TW), F32, kind="Internal").ap(),
        "M0": nc.dram_tensor("state_hop0", (SLOTS, MW), F32, kind="Internal").ap(),
        "M1": nc.dram_tensor("state_hop1", (SLOTS, MW), F32, kind="Internal").ap(),
        "xd": nc.dram_tensor("x_of_dst", (P, T, D), F32, kind="Internal").ap(),
        "base": nc.dram_tensor("out_before_hops", (P, T, D), F32, kind="Internal").ap(),
        "g": [nc.dram_tensor(f"head_sums{k}", (P, T, D), F32, kind="Internal").ap() for k in range(HOPS)],
    }
    with ExitStack() as ctx:
        def sb(name, shape, dt=F32):
            return ctx.enter_context(nc.sbuf_tensor(name, shape, dt))

        s = {"used_semaphores": []}
        s["row_in"] = [ctx.enter_context(nc.semaphore(f"row_in{k}")) for k in range(2 * R)]
        s["ident"] = sb("ident", [P, P])
        s["W1"] = sb("W1_two", [P, P])
        s["W2"] = sb("W2_two", [P, P])
        s["Wv"] = sb("Wv_two", [P, P])
        s["Wvq"] = sb("Wvq_bias", [D + 1, 2 * D])
        s["Wkv"] = sb("Wkv_bias", [D + 1, 2 * D])
        s["b1"] = sb("b1_col", [P, 1])
        s["b23"] = sb("b2_parts", [3, P], BF16)
        s["bv3"] = sb("bv_parts", [3, P], BF16)
        s["ones3"] = sb("ones_parts", [3, P], BF16)
        s["ones"] = sb("ones_row", [1, P])
        s["hop"] = sb("hop_factors", [P, HOPS + 1])
        s["carry"] = sb("carry", [P, P])
        s["carryT"] = sb("carryT", [P, P])
        s["same"] = sb("same_as_before", [P, T])
        s["notlast"] = sb("not_last_here", [P, T])
        s["islast"] = sb("last_here", [P, T])
        s["fix"] = sb("carried_sums", [P, 2, AW])
        s["acc_end"] = sb("state_of_last_column", [P, MW])
        s["first"] = sb("in_first_segment", [P, T])
        s["trail"] = sb("in_last_segment", [P, T])
        s["src"] = sb("src_index", [P, T + ET], I32)
        s["dst"] = sb("dst_index", [P, T + ET], I32)
        s["dst_end"] = sb("dst_at_segment_end", [P, T], I32)
        s["dst_out"] = sb("dst_for_output", [P, T], I32)
        s["dst_x"] = sb("dst_for_extra_column", [P, 1], I32)
        s["slot_x"] = sb("slot_of_first_segment", [P, 1], I32)
        s["w"] = sb("edge_weight_cols", [P, T])
        s["wn"] = sb("norm_hop12", [P, T])
        s["sidx"] = sb("state_slot_of_src", [P, T + ET], I32)
        s["slots"] = sb("slot_ids", [P, T])
        s["AG"] = sb("sums", [P, T + 1, AW])
        s["xbase"] = sb("extra_base", [P, D])
        s["gx"] = sb("extra_head_sums", [P, HOPS, D])

        prepare(nc, s, src, dst, edge_weight, W1, b1, W2, b2, Wq, bq, Wk, bk, Wv, bv, hopwise,
                mats, slots)
        nodes_and_gathers(nc, s, dram, x, out)
        complete_sums(nc, s)
        s["Q"] = sb("queries", [P, T, D])
        edge_mlp(nc, s, dram)
        hop_zero(nc, s, dram, edge_attr, s["used_semaphores"])
        hop_end(nc, s, dram, 0)
        hop_next(nc, s, dram, 1)
        hop_end(nc, s, dram, 1)
        hop_next(nc, s, dram, 2)
        write_out(nc, s, dram, out)


def repeated(row, n):
    return row[:, :].unsqueeze(1).to_broadcast([3, n, P])


def prepare(nc, s, src, dst, edge_weight, W1, b1, W2, b2, Wq, bq, Wk, bk, Wv, bv, hopwise, mats,
            slots):
    with ExitStack() as ctx:
        def sb(name, shape, dt=F32):
            return ctx.enter_context(nc.sbuf_tensor(name, shape, dt))

        def sem(name):
            return used(s, ctx.enter_context(nc.semaphore(name)))

        later = sb("col_after_row", [P, P])
        shift = sb("row_after_col", [P, P])
        dstf = sb("dst_float", [P, T])
        nextf = sb("dst_of_next_partition", [P, 1])
        dif = sb("dst_differs", [P, T])
        lastf = sb("is_segment_end", [P, T])
        tmp = sb("prep_tmp", [P, T])
        tmp2 = sb("prep_tmp2", [P, T])
        len1 = sb("first_segment_length", [P, 1])
        ends = sb("first_segment_ends_here", [P, 1])
        col = sb("prep_col", [P, 2])
        brow, rest = sb("bias_rows", [3, 2, P]), sb("bias_rest", [3, 2, P])
        part, parts = sb("bias_part", [3, 2, P], BF16), sb("bias_parts", [3, 2, P])
        pfirst = ctx.enter_context(nc.psum_tensor("p_first_row", [P, 512], F32))
        pnext = ctx.enter_context(nc.psum_tensor("p_next", [P, 512], F32))
        loaded, cleared, v, pe, rows = (sem("prep_loaded"), sem("prep_cleared"), sem("prep_vec"),
                                        sem("prep_pe"), sem("prep_rows"))
        block = ctx.enter_context(nc.Block())
        n_loads = 0

        @block.sync
        def _(sync):
            nonlocal n_loads
            sync.wait_ge(cleared, 1)
            loads = [(s["src"][0:EP, 0:T], src.rearrange("(p t) -> p t", t=T)),
                     (s["dst"][0:EP, 0:T], dst.rearrange("(p t) -> p t", t=T)),
                     (s["w"][0:EP, :], edge_weight.rearrange("(p t) -> p t", t=T)),
                     (s["ident"][:, :], mats[:, 0:P]), (later[:, :], mats[:, P:2 * P]),
                     (shift[:, :], mats[:, 2 * P:3 * P]), (s["slots"][:, :], slots),
                     (s["hop"][:, :], hopwise.unsqueeze(0).to_broadcast([P, HOPS + 1]))]
            for to, parts in (("Wkv", ((Wk, bk), (Wv, bv))), ("Wvq", ((Wv, bv), (Wq, bq)))):
                for j, (weights, bias) in enumerate(parts):
                    c = slice(j * D, (j + 1) * D)
                    loads += [(s[to][0:D, c], weights), (s[to][D:D + 1, c], bias.unsqueeze(0))]
            for k in range(2):
                r, c = slice(k * D, k * D + D), k * D
                loads += [(s["W1"][r, c:c + D], W1), (s["W2"][r, c:c + D], W2),
                          (s["Wv"][r, c:c + D], Wv),
                          (s["b1"][r, :], b1.unsqueeze(1))]
            for j in range(2):
                r = slice(j * D, j * D + D)
                loads += [(brow[:, 0, r], b2.unsqueeze(0).to_broadcast([3, D])),
                          (brow[:, 1, r], bv.unsqueeze(0).to_broadcast([3, D]))]
            for to, what in loads:
                sync.dma_start(to, what).then_inc(loaded, 16)
            n_loads = len(loads)
            sync.wait_ge(loaded, 16 * n_loads)
            sync.sem_inc(rows, 1)

        @block.tensor
        def _(ten):
            ten.wait_ge(v, 2)
            ten.matmul(pfirst[:, 0:P], dstf[:, 0:1].to_broadcast([P, P]), s["ident"][:, :],
                       start=True, stop=True).then_inc(pe, 1)
            ten.matmul(pnext[:, 0:1], shift[:, :], dstf[:, 0:1], start=True, stop=True).then_inc(pe, 1)
            ten.wait_ge(v, 6)
            ten.transpose(pfirst[:, P:2 * P], s["carry"][:, :], s["ident"][:, :]).then_inc(pe, 1)

        @block.vector
        def _(vec):
            for k in ("W1", "W2", "Wv", "w"):
                vec.memset(s[k][:, :], 0.0)
            vec.memset(s["src"][:, :], 0)
            vec.memset(s["dst"][:, :], -1)
            vec.memset(s["sidx"][:, :], 0)
            vec.memset(s["ones"][:, :], 1.0)
            vec.memset(s["ones3"][:, :], 1.0)
            vec.memset(s["AG"][:, 1:, D:AW], 1.0)
            vec.memset(s["AG"][:, 0, :], 1.0)
            vec.memset(s["gx"][:, :, :], 0.0)
            vec.memset(s["dst_out"][:, :], 0).then_inc(cleared, 1)
            vec.wait_ge(cleared, 1)
            vec.wait_ge(rows, 1)
            n = [0]

            def step(ins):
                ins.then_inc(v, 1)
                n[0] += 1
                vec.wait_ge(v, n[0])

            dstt = dstf
            step(vec.tensor_copy(dstt[:, :], s["dst"][:, 0:T]))
            step(vec.tensor_scalar(s["wn"][:, :], s["w"][:, :], 0.0, None, ALU.mult))
            vec.wait_ge(pe, 2)
            step(vec.tensor_copy(nextf[:, :], pnext[:, 0:1]))
            step(vec.tensor_tensor(dif[:, 0:T - 1], dstt[:, 0:T - 1], dstt[:, 1:T], ALU.not_equal))
            step(vec.tensor_scalar(s["carry"][:, :], pfirst[:, 0:P], dstt[:, T - 1:T], None, ALU.is_equal))
            step(vec.tensor_tensor(s["carry"][:, :], s["carry"][:, :], later[:, :], ALU.mult))
            vec.wait_ge(pe, 3)
            step(vec.tensor_copy(s["carryT"][:, :], pfirst[:, P:2 * P]))
            step(vec.tensor_copy(lastf[:, 0:T - 1], dif[:, 0:T - 1]))
            step(vec.tensor_tensor(lastf[:, T - 1:T], dstt[:, T - 1:T], nextf[:, :], ALU.not_equal))
            step(vec.memset(s["same"][:, 0:1], 0.0))
            step(vec.tensor_scalar(s["same"][:, 1:T], dif[:, 0:T - 1], -1.0, 1.0, ALU.mult, ALU.add))
            step(vec.memset(s["notlast"][:, T - 1:T], 0.0))
            step(vec.tensor_scalar(s["notlast"][:, 0:T - 1], dif[:, 0:T - 1], -1.0, 1.0, ALU.mult, ALU.add))
            step(vec.tensor_scalar(s["islast"][:, :], s["notlast"][:, :], -1.0, 1.0, ALU.mult, ALU.add))
            step(vec.tensor_scalar(s["first"][:, :], dstt[:, :], dstt[:, 0:1], None, ALU.is_equal))
            step(vec.tensor_scalar(s["trail"][:, :], dstt[:, :], dstt[:, T - 1:T], None, ALU.is_equal))
            step(vec.tensor_reduce(len1[:, :], s["first"][:, :], AX.X, ALU.add))
            step(vec.tensor_scalar(col[:, 0:1], len1[:, :], float(P), float(-P), ALU.mult, ALU.add))
            step(vec.tensor_tensor(col[:, 1:2], col[:, 0:1], s["slots"][:, 0:1], ALU.add))
            step(vec.tensor_copy(s["slot_x"][:, :], col[:, 1:2]))
            step(vec.tensor_scalar(tmp[:, :], lastf[:, :], -float(NO_ROW), float(NO_ROW), ALU.mult, ALU.add))
            step(vec.tensor_tensor(tmp2[:, :], tmp[:, :], dstt[:, :], ALU.add))
            step(vec.tensor_copy(s["dst_end"][:, :], tmp2[:, :]))
            step(vec.tensor_scalar(tmp[:, :], s["first"][:, :], float(NO_ROW), None, ALU.mult))
            step(vec.tensor_tensor(tmp[:, :], tmp[:, :], tmp2[:, :], ALU.add))
            step(vec.tensor_copy(s["dst_out"][:, :], tmp[:, :]))
            step(vec.tensor_tensor(tmp[:, :], s["first"][:, :], lastf[:, :], ALU.mult))
            step(vec.tensor_reduce(ends[:, :], tmp[:, :], AX.X, ALU.add))
            step(vec.tensor_scalar(ends[:, :], ends[:, :], -float(NO_ROW), float(NO_ROW), ALU.mult, ALU.add))
            step(vec.tensor_tensor(ends[:, :], ends[:, :], dstt[:, 0:1], ALU.add))
            step(vec.tensor_copy(s["dst_x"][:, :], ends[:, :]))
            step(vec.tensor_scalar(s["Wv"][:, :], s["Wv"][:, :], s["hop"][:, 0:1], None, ALU.mult))
            step(vec.tensor_scalar(s["Wvq"][:, 0:D], s["Wvq"][:, 0:D], s["hop"][0:D + 1, 0:1], None, ALU.mult))
            step(vec.tensor_scalar(brow[:, 1, :], brow[:, 1, :], s["hop"][0:3, 0:1], None, ALU.mult))
            step(vec.tensor_scalar(parts[:, :, :], brow[:, :, :], 0.0, None, ALU.mult))
            for k in range(3):
                step(vec.tensor_copy(part[:, :, :], brow[:, :, :]))
                step(vec.tensor_copy(rest[:, :, :], part[:, :, :]))
                step(vec.scalar_tensor_tensor(parts[:, :, :], rest[:, :, :], s["ident"][0:3, k:k + 1],
                                              parts[:, :, :], ALU.mult, ALU.add))
                step(vec.tensor_tensor(brow[:, :, :], brow[:, :, :], rest[:, :, :], ALU.subtract))
            step(vec.tensor_copy(s["b23"][:, :], parts[:, 0, :]))
            step(vec.tensor_copy(s["bv3"][:, :], parts[:, 1, :]))


def used(s, sem):
    s["used_semaphores"].append(sem)
    return sem


def nodes_and_gathers(nc, s, dram, x, out):
    with ExitStack() as ctx:
        def sb(name, shape, dt=F32):
            return ctx.enter_context(nc.sbuf_tensor(name, shape, dt))

        def ps(name):
            return ctx.enter_context(nc.psum_tensor(name, [P, HT * D], F32))

        def sem(name):
            return used(s, ctx.enter_context(nc.semaphore(name)))

        def ring(name, shape, dt=F32):
            return [sb(f"{name}{b}", shape, dt) for b in range(R)]

        def sems(name):
            return [sem(f"{name}{b}") for b in range(R)]

        C = HT + EH
        xn, gs, gd = ring("x_nodes", [P, HT, D]), ring("x_src", [P, EH, D]), ring("x_dst", [P, EH, D])
        sq, sq2 = ring("squares", [P, C, D]), ring("squares_b", [P, HT, D])
        z, h1 = ring("h0_before_relu", [P, HT, D]), ring("h1_", [P, HT, D])
        hT1, hT2, a1 = sb("h0_turned", [P, HT * D]), sb("h1_turned", [P, HT * D]), sb("mlp1", [P, HT * D])
        x1, tab, res = ring("x1_", [P, HT, D]), ring("table_rows", [P, HT, TW]), ring("out_rows", [P, HT, D])
        st = ring("stats", [P, 6, C + HT])
        isrc, idst = ring("src_now", [P, EH], I32), ring("dst_now", [P, EH], I32)
        warm = sb("root_of_one", [1, 1])
        pt1, pt2, pa, pb1, pb2 = ps("p_turned1"), ps("p_turned2"), ps("p_mlp1"), ps("p_mlp2"), ps("p_value")
        x_in, stored, dst_kept = (sems(n) for n in ("x_in", "stored", "dst_kept"))
        src_in, dst_in = s["row_in"][0:R], s["row_in"][R:2 * R]
        isrc_set, idst_set = sem("isrc_set"), sem("idst_set")
        squared, squared2 = sem("squared"), sem("squared2")
        varred, rooted, scaled = sem("varred"), sem("rooted"), sem("scaled")
        normed, src_normed, normed2 = sem("normed"), sem("src_normed"), sem("normed2")
        turned1, turned2, mm1, mm2, mm3 = sem("turned1"), sem("turned2"), sem("mm1"), sem("mm2"), sem("mm3")
        copied1, copied2, relued = sem("copied1"), sem("copied2"), sem("relued")
        x1_done, tab_done, res_done = sem("x1_done"), sem("tab_done"), sem("res_done")
        v_red, v_red2, v_norm, v_scale, v_sums, v_z = (
            sem(f"vec_{k}") for k in ("red", "red2", "norm", "scale", "sums", "z"))
        note_p, note_s, zeroed = sem("note_pool"), sem("note_sync"), sem("zeroed")
        block = ctx.enter_context(nc.Block())

        def rows(dram_t, m, b, w):
            half = b % 2
            start = m // 2 * GSTEP if isinstance(m, int) else (m - half) * (GSTEP // 2)
            a = dram_t[bass.ds(start, NT * P), :].rearrange("(p j) f -> p j f", j=NT)
            return a[:, half * HT:(half + 1) * HT, :]

        @block.sync
        def _(sync):
            def load(n, b):
                passed(sync, x1_done, n - R + 1, note_s)
                sync.dma_start(xn[b][:, :, :], rows(x, n, b, D)).then_inc(x_in[b], 16)

            def body(n, b):
                if here(n + 1):
                    load(n + 1, (b + 1) % R)
                m, c = n - 2, (b - 2) % R
                if here(m):
                    passed(sync, dst_in[c], with_unit(m, c, 16 * EH), note_s)
                    sync.dma_start(dram["xd"][:, edge_cols(m), :], gd[c][:, :, :]).then_inc(dst_kept[c], 16)
                m, c = n - 5, (b - 5) % R
                if here(m):
                    passed(sync, res_done, m + 1, note_s)
                    passed(sync, tab_done, m + 1, note_s)
                    if c % 2 == 0:
                        for h in range(R):
                            passed(sync, stored[h], before_unit(m, c, 32) + (32 if h < c else 0), note_s)
                    sync.dma_start(rows(out, m, c, D), res[c][:, :, :]).then_inc(stored[c], 16)
                    sync.dma_start(rows(dram["table"], m, c, TW), tab[c][:, :, :]).then_inc(stored[c], 16)

            sync.wait_ge(zeroed, 1)
            load(0, 0)
            turns(sync, body, 5, R)
            for b in range(R):
                sync.wait_ge(stored[b], 32 * units_in(b))
                sync.wait_ge(dst_kept[b], 16 * units_in(b))

        @block.gpsimd
        def _(pool):
            top = pool.to_reg(N - 1)

            def body(n, b):
                passed(pool, isrc_set, n + 1, note_p)
                passed(pool, src_normed, n - R + 1, note_p)
                for k in range(EH):
                    pool.indirect_dma_start(
                        out=gs[b][0:EP, k, :], out_offset=None, in_=x,
                        in_offset=bass.IndirectOffsetOnAxis(ap=isrc[b][0:EP, k:k + 1], axis=0),
                        bounds_check=top, oob_is_err=False).then_inc(src_in[b], 16)
                passed(pool, idst_set, n + 1, note_p)
                passed(pool, dst_kept[b], before_unit(n, b, 16), note_p)
                for k in range(EH):
                    pool.indirect_dma_start(
                        out=gd[b][0:EP, k, :], out_offset=None, in_=x,
                        in_offset=bass.IndirectOffsetOnAxis(ap=idst[b][0:EP, k:k + 1], axis=0),
                        bounds_check=top, oob_is_err=False).then_inc(dst_in[b], 16)

            turns(pool, body, 0, R)

        @block.scalar
        def _(act):
            def norm_rows(c):
                for k in range(HT):
                    ins = act.activation(h1[c][:, k, :], x1[c][:, k, :], ACT.Relu,
                                         bias=st[(c + 2) % R][:, 5, C + k:C + k + 1],
                                         scale=st[(c + 2) % R][:, 4, C + k:C + k + 1])
                return ins

            def body(n, b):
                m, c = n - 2, (b - 2) % R
                if here(m):
                    act.wait_ge(turned1, m + 1)
                    act.activation(hT1[:, :], pt1[:, :], ACT.Relu).then_inc(copied1, 1)
                m = n - 5
                if here(m):
                    act.wait_ge(turned2, m + 1)
                    act.activation(hT2[:, :], pt2[:, :], ACT.Copy).then_inc(copied2, 1)
                if here(n):
                    act.wait_ge(x_in[b], with_unit(n, b, 16))
                    act.activation(sq[b][:, 0:HT, :], xn[b][:, :, :], ACT.Square)
                    act.wait_ge(src_in[b], with_unit(n, b, 16 * EH))
                    act.activation(sq[b][:, HT:C, :], gs[b][:, :, :], ACT.Square).then_inc(squared, 1)
                m = n - 2
                if here(m):
                    act.wait_ge(mm1, m + 1)
                    act.activation(a1[:, :], pa[:, :], ACT.Relu, bias=s["b1"][:, 0:1]).then_inc(relued, 1)
                if here(m):
                    act.wait_ge(scaled, m + 1)
                    for k in range(EH):
                        ins = act.activation(s["AG"][:, bass.ds(m * EH + k + 1, 1), 0:D], gs[c][:, k:k + 1, :],
                                             ACT.Relu, bias=st[c][:, 5, HT + k:HT + k + 1],
                                             scale=st[c][:, 4, HT + k:HT + k + 1])
                    ins.then_inc(src_normed, 1)
                if here(n - 1) or here(n - 3):
                    act.wait_ge(varred, n)
                    q = st[(b - 1) % R]
                    act.activation(q[:, 3, :], q[:, 2, :], ACT.Sqrt).then_inc(rooted, 1)
                m, c = n - 4, (b - 4) % R
                if here(m):
                    act.wait_ge(scaled, m + 3)
                    norm_rows(c).then_inc(normed2, 1)
                m, c = n - 2, (b - 2) % R
                if here(m):
                    act.wait_ge(x1_done, m + 1)
                    act.activation(sq2[c][:, :, :], x1[c][:, :, :], ACT.Square).then_inc(squared2, 1)
                m, c = n - 4, (b - 4) % R
                if here(m):
                    act.wait_ge(normed2, m + 1)
                    wait(act, stored[c], before_unit(m, c, 32))
                    act.activation(tab[c][:, :, 0:D], h1[c][:, :, :], ACT.Copy).then_inc(tab_done, 1)

            act.wait_ge(zeroed, 1)
            act.activation(warm[:, :], s["ones"][:, 0:1], ACT.Sqrt)
            turns(act, body, 5, R)

        @block.tensor
        def _(ten):
            def turn(pt, what, done):
                for k in range(HT // 2):
                    ins = ten.transpose(pt[:, k * P:(k + 1) * P], what[:, 2 * k:2 * k + 2, :], s["ident"][:, :])
                ins.then_inc(done, 1)

            def rows_out(pb, lhs, w, bias, done):
                ten.matmul(pb[:, :], s["ones3"][:, :], repeated(bias, HT // 2), start=True, stop=False,
                           skip_group_check=True)
                for k in range(HT // 2):
                    ins = ten.matmul(pb[:, k * P:(k + 1) * P], lhs[:, k * P:(k + 1) * P], w[:, :],
                                     start=False, stop=(k == HT // 2 - 1), skip_group_check=True)
                ins.then_inc(done, 1)

            def body(n, b):
                m = n - 2
                if here(m):
                    ten.wait_ge(copied1, m + 1)
                    wait(ten, relued, m)
                    ten.matmul(pa[:, :], s["W1"][:, :], hT1[:, :], start=True, stop=True).then_inc(mm1, 1)
                if here(n - 5):
                    ten.wait_ge(copied2, n - 4)
                    wait(ten, res_done, n - 5)
                    rows_out(pb2, hT2, s["Wv"], s["bv3"], mm3)
                if here(m):
                    ten.wait_ge(relued, m + 1)
                    wait(ten, x1_done, m)
                    rows_out(pb1, a1, s["W2"], s["b23"], mm2)
                if here(n - 1):
                    ten.wait_ge(normed, n)
                    wait(ten, copied1, n - 1)
                    turn(pt1, z[(b - 1) % R], turned1)
                if here(n - 4):
                    ten.wait_ge(normed2, n - 3)
                    wait(ten, copied2, n - 4)
                    turn(pt2, h1[(b - 4) % R], turned2)

            turns(ten, body, 5, R)

        @block.vector
        def _(vec):
            def set_index(m, b):
                vec.tensor_copy(isrc[b][:, :], s["src"][:, edge_cols(m)]).then_inc(isrc_set, 1)
                vec.tensor_copy(idst[b][:, :], s["dst"][:, edge_cols(m)]).then_inc(idst_set, 1)

            def flat(t):
                return t[:, :, :].rearrange("p j f -> p (j f)")

            def each_row(q):
                return q.unsqueeze(2).to_broadcast([P, HT, D])

            def body(n, b):
                m, c = n - 1, (b - 1) % R
                both = st[c]
                waits = []
                if here(m):
                    vec.wait_ge(squared, m + 1)
                    vec.wait_ge(x_in[c], with_unit(m, c, 16))
                    red = Chain(vec, v_red, m, 3)
                    red.step(vec.tensor_reduce(both[:, 0, 0:HT], xn[c][:, :, :], AX.X, ALU.add))
                    red.step(vec.tensor_reduce(both[:, 0, HT:C], gs[c][:, :, :], AX.X, ALU.add))
                    red.step(vec.tensor_reduce(both[:, 1, 0:C], sq[c][:, :, :], AX.X, ALU.add))
                    waits.append(red)
                m, c = n - 3, (b - 3) % R
                if here(m):
                    vec.wait_ge(squared2, m + 1)
                    red2 = Chain(vec, v_red2, m, 2)
                    red2.step(vec.tensor_reduce(both[:, 0, C:C + HT], x1[c][:, :, :], AX.X, ALU.add))
                    red2.step(vec.tensor_reduce(both[:, 1, C:C + HT], sq2[c][:, :, :], AX.X, ALU.add))
                    waits.append(red2)
                    vec.wait_ge(src_normed, m + 1)
                    sums = Chain(vec, v_sums, m, EH)

                def join(k):
                    if here(m):
                        t = m * EH + k
                        now = s["AG"][:, bass.ds(t + 1, 1), :]
                        sums.wait()
                        sums.step(vec.scalar_tensor_tensor(now, s["AG"][:, bass.ds(t, 1), :],
                                                           s["same"][:, bass.ds(t, 1)], now, ALU.mult, ALU.add))

                if waits:
                    norm_stats(Chain(vec, v_norm, n - 1, 3), waits, varred, both, C + HT, join)
                m2, c2 = n + 2, (b + 2) % R
                if here(n) and here(m2):
                    wait(vec, src_in[c2], before_unit(m2, c2, 16 * EH))
                    wait(vec, dst_in[c2], before_unit(m2, c2, 16 * EH))
                    set_index(m2, c2)
                m, c = n - 5, (b - 5) % R
                if here(m):
                    vec.wait_ge(mm3, m + 1)
                    wait(vec, stored[c], before_unit(m, c, 32))
                    vec.tensor_tensor(flat(res[c]), pb2[:, :], flat(x1[c]), ALU.add).then_inc(res_done, 1)
                if waits:
                    vec.wait_ge(rooted, n)
                    norm_scales(Chain(vec, v_scale, n - 1, 1), scaled, both, C + HT)
                m, c = n - 1, (b - 1) % R
                if here(m):
                    vec.wait_ge(scaled, m + 1)
                    ch = Chain(vec, v_z, m, 1)
                    ch.step(vec.tensor_tensor(z[c][:, :, :], xn[c][:, :, :], each_row(both[:, 4, 0:HT]), ALU.mult))
                    ch.wait()
                    vec.tensor_tensor(z[c][:, :, :], z[c][:, :, :], each_row(both[:, 5, 0:HT]),
                                      ALU.add).then_inc(normed, 1)
                m, c = n - 2, (b - 2) % R
                if here(m):
                    vec.wait_ge(mm2, m + 1)
                    vec.scalar_tensor_tensor(flat(x1[c]), pb1[:, :], 0.0, flat(xn[c]),
                                             ALU.max, ALU.add).then_inc(x1_done, 1)

            for b in range(R):
                vec.memset(st[b][:, :, :], 1.0)
                vec.memset(gs[b][:, :, :], 0.0)
                vec.memset(gd[b][:, :, :], 0.0)
                vec.memset(tab[b][:, :, D:D + 1], 0.0)
                vec.memset(tab[b][:, :, D + 1:TW], float(NO_ROW))
            for b in range(2):
                set_index(b, b)
            vec.drain().then_inc(zeroed, 1)
            vec.wait_ge(zeroed, 1)
            turns(vec, body, 5, R)


def complete_sums(nc, s):
    with ExitStack() as ctx:
        pc = ctx.enter_context(nc.psum_tensor("p_carry", [P, 512], F32))
        pe = used(s, ctx.enter_context(nc.semaphore("carry_ready")))
        v = used(s, ctx.enter_context(nc.semaphore("back_steps")))
        block = ctx.enter_context(nc.Block())

        @block.tensor
        def _(ten):
            ten.matmul(pc[:, 0:AW], s["carry"][:, :], s["AG"][:, T, :], start=True, stop=True).then_inc(pe, 1)
            ten.wait_ge(v, 2 + AW)
            ten.matmul(pc[:, P:P + AW], s["carryT"][:, :], s["AG"][:, 1, :], start=True, stop=True).then_inc(pe, 1)

        @block.vector
        def _(vec):
            vec.wait_ge(pe, 1)
            vec.tensor_copy(s["fix"][:, 0, :], pc[:, 0:AW]).then_inc(v, 1)
            vec.tensor_tensor(s["AG"][:, 1:T + 1, :], s["AG"][:, 1:T + 1, :],
                              s["islast"][:, :].unsqueeze(2).to_broadcast([P, T, AW]), ALU.mult).then_inc(v, 1)
            vec.wait_ge(v, 2)
            for f in range(AW):
                col = s["AG"][:, T:0:-1, f]
                vec.tensor_tensor_scan(col, s["notlast"][:, ::-1], col, 0.0, ALU.mult, ALU.add).then_inc(v, 1)
            vec.wait_ge(pe, 2)
            vec.tensor_copy(s["fix"][:, 1, :], pc[:, P:P + AW]).then_inc(v, 1)


def edge_mlp(nc, s, dram):
    with ExitStack() as ctx:
        def sb(name, shape, dt=F32):
            return ctx.enter_context(nc.sbuf_tensor(f"m_{name}", shape, dt))

        def ring(name, shape, dt=F32):
            return [sb(f"{name}{b}", shape, dt) for b in range(R)]

        def sem(name):
            return used(s, ctx.enter_context(nc.semaphore(f"m_{name}")))

        def sems(name):
            return [sem(f"{name}{b}") for b in range(R)]

        def ps(name):
            return ctx.enter_context(nc.psum_tensor(f"mp_{name}", [P, 512], F32))

        S2, S3 = 2 * EH, 3 * EH
        xd, h0, h1, x1 = (ring(n, [P, EH, D]) for n in ("x", "h0_", "h1_", "x1_"))
        sq, sq2, hid = ring("squares", [P, EH, D]), ring("squares_b", [P, EH, D]), ring("base", [P, EH, D])
        hT1, a1 = sb("h0_turned", [P, W]), sb("mlp1", [P, W])
        hT2 = sb("h1_turned_and_ones", [D + 1, EH * P])
        tab, st = ring("table_rows", [P, EH, TW]), ring("stats", [P, 6, S3])
        ix = ring("dst_now", [P, EH], I32)
        pt1, pt2, pa, pb1 = ps("turned1"), ps("turned2"), ps("mlp1p"), ps("mlp2p")
        pb2 = [ps("vq0"), ps("vq1")]
        x_in, kept, scattered = (sems(n) for n in ("x_in", "kept", "scattered"))
        squared, squared2, varred = sem("squared"), sem("squared2"), sem("varred")
        rooted, scaled = sem("rooted"), sem("scaled")
        normed, normed2, summed = sem("normed"), sem("normed2"), sem("summed")
        turned1, turned2, mm1, mm2, mm3 = sem("turned1_"), sem("turned2_"), sem("mm1"), sem("mm2"), sem("mm3")
        copied1, copied2, relued = sem("copied1"), sem("copied2"), sem("relued")
        x1_done, tab_set, hid_done, q_done = sem("x1_done"), sem("tab_set"), sem("hid_done"), sem("q_done")
        v_fix, v_red, v_red2, v_norm, v_scale = (
            sem(f"steps_{k}") for k in ("fix", "red", "red2", "norm", "scale"))
        note_p, note_s, note_a, note_t = sem("note_p"), sem("note_s"), sem("note_a"), sem("note_t")
        extra, ones_set, ends_set = sem("extra"), sem("ones_set"), sem("ends_set")
        block = ctx.enter_context(nc.Block())

        @block.sync
        def _(sync):
            def load(n, b):
                passed(sync, x1_done, n - R + 1, note_s)
                sync.dma_start(xd[b][:, :, :], dram["xd"][:, edge_cols(n), :]).then_inc(x_in[b], 16)

            def body(n, b):
                if here(n + 1):
                    load(n + 1, (b + 1) % R)
                m, c = n - 5, (b - 5) % R
                if here(m):
                    passed(sync, hid_done, m + 1, note_s)
                    sync.dma_start(dram["base"][:, edge_cols(m), :], hid[c][:, :, :]).then_inc(kept[c], 16)

            load(0, 0)
            turns(sync, body, 5, R)
            for b in range(R):
                sync.wait_ge(kept[b], 16 * units_in(b))

        @block.gpsimd
        def _(pool):
            top = pool.to_reg(N - 1)

            def body(m, b):
                passed(pool, ends_set, 3 * m + 3, note_p)
                passed(pool, tab_set, m + 1, note_p)
                for k in range(EH):
                    pool.indirect_dma_start(
                        out=dram["table"],
                        out_offset=bass.IndirectOffsetOnAxis(ap=ix[b][0:EP, k:k + 1], axis=0),
                        in_=tab[b][0:EP, k, :], in_offset=None,
                        bounds_check=top, oob_is_err=False).then_inc(scattered[b], 16)

            turns(pool, body, 0, R)
            for b in range(R):
                pool.wait_ge(scattered[b], 16 * EH * units_in(b))

        @block.scalar
        def _(act):
            def body(n, b):
                if here(n):
                    act.wait_ge(x_in[b], with_unit(n, b, 16))
                    act.activation(sq[b][:, :, :], xd[b][:, :, :], ACT.Square).then_inc(squared, 1)
                m = n - 2
                if here(m):
                    act.wait_ge(turned1, m + 1)
                    act.activation(hT1[:, :], pt1[:, 0:W], ACT.Copy).then_inc(copied1, 1)
                m = n - 5
                if here(m):
                    act.wait_ge(turned2, m + 1)
                    act.activation(hT2[0:D, :], pt2[0:D, :], ACT.Copy).then_inc(copied2, 1)
                m = n - 2
                if here(m):
                    act.wait_ge(mm1, m + 1)
                    act.activation(a1[:, :], pa[:, 0:W], ACT.Relu, bias=s["b1"][:, 0:1]).then_inc(relued, 1)
                m, c = n - 4, (b - 4) % R
                if here(m):
                    q = st[(c + 3) % R]
                    act.wait_ge(scaled, m + 4)
                    for k in range(EH):
                        ins = act.activation(h1[c][:, k, :], x1[c][:, k, :], ACT.Relu,
                                             bias=q[:, 5, EH + k:EH + k + 1], scale=q[:, 4, EH + k:EH + k + 1])
                    ins.then_inc(normed2, 1)
                m, c = n - 1, (b - 1) % R
                if here(m):
                    act.wait_ge(scaled, m + 1)
                    for k in range(EH):
                        ins = act.activation(h0[c][:, k, :], xd[c][:, k, :], ACT.Relu,
                                             bias=st[c][:, 5, k:k + 1], scale=st[c][:, 4, k:k + 1])
                    ins.then_inc(normed, 1)
                if here(n) or here(n - 3):
                    act.wait_ge(varred, n + 1)
                    act.activation(st[b][:, 3, :], st[b][:, 2, :], ACT.Sqrt).then_inc(rooted, 1)
                m, c = n - 5, (b - 5) % R
                if here(m):
                    passed(act, ends_set, 3 * m + 3, note_a)
                    passed(act, mm3, m + 1, note_a)
                    for k in range(EH):
                        ins = act.activation(s["Q"][:, bass.ds(m * EH + k, 1), :],
                                             pb2[c % 2][:, k * 2 * D + D:(k + 1) * 2 * D].unsqueeze(1), ACT.Relu,
                                             scale=tab[c][:, k, D:D + 1])
                    ins.then_inc(q_done, 1)
                m, c = n - 2, (b - 2) % R
                if here(m):
                    act.wait_ge(x1_done, m + 1)
                    act.activation(sq2[c][:, :, :], x1[c][:, :, :], ACT.Square).then_inc(squared2, 1)

            act.wait_ge(ones_set, 1)
            turns(act, body, 5, R)

        @block.tensor
        def _(ten):
            def body(n, b):
                m = n - 2
                if here(m):
                    ten.wait_ge(copied1, m + 1)
                    wait(ten, relued, m)
                    ten.matmul(pa[:, 0:W], s["W1"][:, :], hT1[:, :], start=True, stop=True).then_inc(mm1, 1)
                m, c = n - 5, (b - 5) % R
                if here(m):
                    ten.wait_ge(copied2, m + 1)
                    wait(ten, hid_done, m - 1)
                    for k in range(EH):
                        ins = ten.matmul(pb2[c % 2][:, k * 2 * D:(k + 1) * 2 * D], hT2[:, k * P:(k + 1) * P],
                                         s["Wvq"][:, :], start=True, stop=True)
                    ins.then_inc(mm3, 1)
                m = n - 2
                if here(m):
                    ten.wait_ge(relued, m + 1)
                    wait(ten, x1_done, m)
                    ten.matmul(pb1[:, 0:W], s["ones3"][:, :], repeated(s["b23"], EH // 2), start=True, stop=False,
                               skip_group_check=True)
                    for k in range(EH // 2):
                        ins = ten.matmul(pb1[:, k * P:(k + 1) * P], a1[:, k * P:(k + 1) * P], s["W2"][:, :],
                                         start=False, stop=(k == EH // 2 - 1), skip_group_check=True)
                    ins.then_inc(mm2, 1)
                m, c = n - 4, (b - 4) % R
                if here(m):
                    passed(ten, normed2, m + 1, note_t)
                    passed(ten, copied2, m, note_t)
                    for k in range(EH):
                        ins = ten.transpose(pt2[0:D, k * P:(k + 1) * P], h1[c][:, k, :], s["ident"][:, :])
                    ins.then_inc(turned2, 1)
                m, c = n - 1, (b - 1) % R
                if here(m):
                    ten.wait_ge(summed, m + 1)
                    wait(ten, copied1, m)
                    for k in range(EH // 2):
                        ins = ten.transpose(pt1[:, k * P:(k + 1) * P], h0[c][:, 2 * k:2 * k + 2, :], s["ident"][:, :])
                    ins.then_inc(turned1, 1)

            ten.wait_ge(ones_set, 1)
            turns(ten, body, 5, R)

        @block.vector
        def _(vec):
            def flat(t):
                return t[:, :, :].rearrange("p j f -> p (j f)")

            def body(n, b):
                m, c = n - 3, (b - 3) % R
                waits = []
                if here(m):
                    vec.wait_ge(squared2, m + 1)
                    red2 = Chain(vec, v_red2, m, 2)
                    red2.step(vec.tensor_reduce(st[b][:, 0, EH:S2], x1[c][:, :, :], AX.X, ALU.add))
                    red2.step(vec.tensor_reduce(st[b][:, 1, EH:S2], sq2[c][:, :, :], AX.X, ALU.add))
                    waits.append(red2)
                if here(n):
                    vec.wait_ge(squared, n + 1)
                    vec.wait_ge(x_in[b], with_unit(n, b, 16))
                    red = Chain(vec, v_red, n, 3)
                    red.step(vec.tensor_reduce(st[b][:, 0, 0:EH], xd[b][:, :, :], AX.X, ALU.add))
                    red.step(vec.tensor_reduce(st[b][:, 1, 0:EH], sq[b][:, :, :], AX.X, ALU.add))
                    waits.append(red)
                    fix = Chain(vec, v_fix, n, 2 * EH)

                def complete(which, flags, tiles):
                    for k in tiles:
                        now = s["AG"][:, bass.ds(n * EH + k + 1, 1), :]
                        fix.step(vec.scalar_tensor_tensor(now, s["fix"][:, which:which + 1, :],
                                                          s[flags][:, bass.ds(n * EH + k, 1)], now,
                                                          ALU.mult, ALU.add))

                def meanwhile(k):
                    if here(n):
                        if k == 0:
                            complete(0, "first", range(EH))
                        elif k == 1:
                            fix.wait()
                            complete(1, "trail", range(0, 2))
                        elif k == 2:
                            complete(1, "trail", range(2, EH))
                        else:
                            fix.wait()
                            red.step(vec.tensor_copy(st[b][:, 2, S2:S3], s["AG"][:, bass.ds(n * EH + 1, EH), D]))
                    if here(m):
                        if k == 0:
                            wait(vec, scattered[c], before_unit(m, c, 16 * EH))
                            vec.tensor_copy(tab[c][:, :, D], st[c][:, 4, S2:S3]).then_inc(ends_set, 1)
                        elif k == 1:
                            vec.tensor_copy(tab[c][:, :, D + 1], s["slots"][:, edge_cols(m)]).then_inc(ends_set, 1)
                        elif k == 2:
                            vec.tensor_copy(ix[c][:, :], s["dst_end"][:, edge_cols(m)]).then_inc(ends_set, 1)

                if waits:
                    norm_stats(Chain(vec, v_norm, n, 3), waits, varred, st[b], S2, meanwhile)
                m, c = n - 4, (b - 4) % R
                if here(m):
                    vec.wait_ge(normed2, m + 1)
                    vec.tensor_copy(tab[c][:, :, 0:D], h1[c][:, :, :]).then_inc(tab_set, 1)
                m, c = n - 2, (b - 2) % R
                if here(m):
                    vec.wait_ge(mm2, m + 1)
                    vec.scalar_tensor_tensor(flat(x1[c]), pb1[:, 0:W], 0.0, flat(xd[c]),
                                             ALU.max, ALU.add).then_inc(x1_done, 1)
                m, c = n - 1, (b - 1) % R
                if here(m):
                    vec.wait_ge(normed, m + 1)
                    vec.tensor_tensor(h0[c][:, :, :], h0[c][:, :, :], s["AG"][:, bass.ds(m * EH + 1, EH), 0:D],
                                      ALU.add).then_inc(summed, 1)
                if here(n) or here(n - 3):
                    vec.wait_ge(rooted, n + 1)
                    norm_scales(Chain(vec, v_scale, n, 1), scaled, st[b], S2)
                m, c = n - 5, (b - 5) % R
                if here(m):
                    vec.wait_ge(q_done, m + 1)
                    wait(vec, kept[c], before_unit(m, c, 16))
                    value = pb2[c % 2][:, :].rearrange("p (j f) -> p j f", f=2 * D)[:, :, 0:D]
                    vec.tensor_tensor(hid[c][:, :, :], value, x1[c][:, :, :], ALU.add).then_inc(hid_done, 1)
                    if isinstance(m, int) and m == 0:
                        vec.wait_ge(hid_done, 1)
                        vec.tensor_copy(s["xbase"][:, :], hid[0][:, 0, :]).then_inc(extra, 1)

            for b in range(R):
                vec.memset(st[b][:, :, :], 1.0)
            vec.memset(hT2[D:D + 1, :], 1.0).then_inc(ones_set, 1)
            vec.wait_ge(ones_set, 1)
            turns(vec, body, 5, R)


def ihj(ap):
    return ap.rearrange("p (h i j) -> p h i j", h=HEADS, i=HD)


def over_j(ap):
    return ap.rearrange("p (h i) -> p h i", i=HD).unsqueeze(3).to_broadcast([P, HEADS, HD, HD])


def over_i(ap):
    return ap.rearrange("p (h j) -> p h j", j=HD).unsqueeze(2).to_broadcast([P, HEADS, HD, HD])


def state_rows(dram_t, m):
    return dram_t[bass.ds(m * (EH * P), EH * P), :].rearrange("(j p) f -> p j f", p=P)


def hop_zero(nc, s, dram, edge_attr, retired):
    with ExitStack() as ctx:
        def sb(name, shape, dt=F32):
            return ctx.enter_context(nc.sbuf_tensor(f"z_{name}", shape, dt))

        def two(name, shape, dt=F32):
            return [sb(f"{name}{b}", shape, dt) for b in range(2)]

        def sem(name):
            return ctx.enter_context(nc.semaphore(f"z_{name}"))

        tg, ef = two("table", [P, EH, TW]), two("edge", [P, EH, D])
        hT = sb("turned_and_ones", [D + 1, EH * P])
        kj, vs, kq, g = (two(n, [P, EH, D]) for n in ("kj", "v", "kq", "g"))
        sc, wn, ix = two("scores", [P, EH * HEADS]), two("wn", [P, EH]), two("src_now", [P, EH], I32)
        pr, acc = [sb(f"outer{k}", [P, MW]) for k in range(EH)], two("acc", [P, EH, MW])
        pt = ctx.enter_context(nc.psum_tensor("z_p_turned", [P, 512], F32))
        pk = [ctx.enter_context(nc.psum_tensor(f"z_p_kv{b}", [P, 512], F32)) for b in range(2)]
        row_in, ef_in, stored, g_kept = ([sem(f"{n}{b}") for b in range(2)]
                                         for n in ("row_in", "ef_in", "stored", "g_kept"))
        idx_set, turned, copied, kv = sem("idx_set"), sem("turned_"), sem("copied"), sem("kv")
        wn_set, v_done, k_done = sem("wn_set"), sem("v_done"), sem("k_done")
        acc_done, g_done, v, v2, zeroed = sem("acc_done"), sem("g_done"), sem("steps"), sem("steps2"), sem("zeroed")
        note_p, note_s, note_t = sem("note_p"), sem("note_s"), sem("note_t")
        ended = sem("ended")
        block = ctx.enter_context(nc.Block())
        ef_rows = edge_attr.rearrange("(p t) f -> p t f", t=T)

        @block.sync
        def _(sync):
            def body(n, b):
                if here(n):
                    passed(sync, kv, n - 1, note_s)
                    for p0, p1 in ((0, 112), (112, EP)):
                        sync.dma_start(ef[b][p0:p1, :, :], ef_rows[p0:p1, edge_cols(n), :]).then_inc(ef_in[b], 16)
                m, o = n - 2, b
                if here(m):
                    passed(sync, g_done, m + 1, note_s)
                    sync.dma_start(dram["g"][0][:, edge_cols(m), :], g[o][:, :, :]).then_inc(g_kept[o], 16)
                    passed(sync, acc_done, EH * (m + 1), note_s)
                    sync.dma_start(state_rows(dram["M0"], m), acc[o][:, :, :]).then_inc(stored[o], 16)

            sync.wait_ge(zeroed, 1)
            turns(sync, body, 2)
            for b in range(2):
                sync.wait_ge(stored[b], 16 * NG)
                sync.wait_ge(g_kept[b], 16 * NG)

        @block.gpsimd
        def _(pool):
            for old in retired:
                pool.sem_clear(old)
            top = pool.to_reg(N - 1)

            def body(n, b):
                passed(pool, idx_set, n + 1, note_p)
                for k in range(EH):
                    pool.indirect_dma_start(
                        out=tg[b][0:EP, k, :], out_offset=None, in_=dram["table"],
                        in_offset=bass.IndirectOffsetOnAxis(ap=ix[b][0:EP, k:k + 1], axis=0),
                        bounds_check=top, oob_is_err=False).then_inc(row_in[b], 16)

            turns(pool, body, 0)

        @block.tensor
        def _(ten):
            def body(n, b):
                passed(ten, row_in[b], 8 * EH * (n - b + 2), note_t)
                passed(ten, copied, n, note_t)
                for k in range(EH):
                    ins = ten.transpose(pt[0:D, k * P:(k + 1) * P], tg[b][:, k, 0:D], s["ident"][:, :])
                ins.then_inc(turned, 1)
                wait(ten, v_done, n - 1)
                ten.wait_ge(copied, n + 1)
                for k in range(EH):
                    ten.matmul(pk[b][:, k * P:(k + 1) * P], hT[:, k * P:(k + 1) * P],
                               s["Wkv"][:, :], start=(k == 0), stop=False, skip_group_check=True)
                ten.wait_ge(ef_in[b], 16 * (n - b + 2))
                ten.matmul(pk[b][:, :].rearrange("p (j f) -> p j f", f=2 * D)[:, :, 0:D], s["ident"][:, :],
                           ef[b][:, :, :], start=False, stop=True, skip_group_check=True).then_inc(kv, 1)

            ten.wait_ge(zeroed, 1)
            turns(ten, body, 0)

        @block.scalar
        def _(act):
            def body(n, b):
                act.wait_ge(turned, n + 1)
                act.activation(hT[0:D, :], pt[0:D, :], ACT.Copy).then_inc(copied, 1)
                act.wait_ge(kv, n + 1)
                wait(act, acc_done, EH * (n - 1))
                act.activation(kj[b][:, :, :], pk[b][:, :].rearrange("p (j f) -> p j f", f=2 * D)[:, :, 0:D],
                               ACT.Relu).then_inc(k_done, 1)
                act.wait_ge(wn_set, n + 1)
                for k in range(EH):
                    ins = act.activation(vs[b][:, k, :], pk[b][:, (2 * k + 1) * D:(2 * k + 2) * D], ACT.Copy,
                                         scale=wn[b][:, k:k + 1])
                ins.then_inc(v_done, 1)

            turns(act, body, 0)

        @block.vector
        def _(vec):
            def set_index(m, b):
                vec.tensor_copy(ix[b][:, :], s["src"][:, edge_cols(m)]).then_inc(idx_set, 1)

            def outer(m, o, ch, k):
                ch.step(vec.tensor_tensor(ihj(pr[k][:, :]), over_j(kj[o][:, k, :]), over_i(vs[o][:, k, :]), ALU.mult))

            def join(m, o, ch, k, steps_ago):
                before = acc[o][:, k - 1, :] if k else acc[1 - o][:, EH - 1, :]
                wait(vec, acc_done, EH * m + k)
                ch.wait(steps_ago)
                vec.scalar_tensor_tensor(acc[o][:, k, :], before, s["same"][:, bass.ds(m * EH + k, 1)], pr[k][:, :],
                                         ALU.mult, ALU.add).then_inc(acc_done, 1)

            def body(n, b):
                o = 1 - b
                m = n - 1
                if here(m):
                    ch = Chain(vec, v, m, 2 + EH)
                    vec.wait_ge(k_done, m + 1)
                    ch.step(vec.tensor_tensor(kq[o][:, :, :], kj[o][:, :, :], s["Q"][:, edge_cols(m), :], ALU.mult))
                    vec.wait_ge(v_done, m + 1)
                    outer(m, o, ch, 0)
                    outer(m, o, ch, 1)
                    ch.wait(2)
                    ch.step(vec.tensor_reduce(sc[o][:, :], kq[o][:, :, :].rearrange("p t (h i) -> p (t h) i", i=HD),
                                              AX.X, ALU.add))
                    wait(vec, stored[o], 8 * (m - o))
                    join(m, o, ch, 0, 2)
                    outer(m, o, ch, 2)
                if here(n):
                    ch2 = Chain(vec, v2, n, 2)
                    vec.wait_ge(row_in[b], 8 * EH * (n - b + 2))
                    vec.tensor_tensor(wn[b][:, :], s["w"][:, edge_cols(n)], tg[b][:, :, D],
                                      ALU.mult).then_inc(wn_set, 1)
                    ch2.step(vec.tensor_copy(s["sidx"][:, edge_cols(n)], tg[b][:, :, D + 1]))
                if here(m):
                    join(m, o, ch, 1, 2)
                    outer(m, o, ch, 3)
                if here(n):
                    vec.wait_ge(wn_set, n + 1)
                    ch2.step(vec.tensor_tensor(s["wn"][:, edge_cols(n)], wn[b][:, :], tg[b][:, :, D], ALU.mult))
                if here(m):
                    join(m, o, ch, 2, 1)
                    wait(vec, g_kept[o], 8 * (m - o))
                    vec.tensor_tensor(
                        g[o][:, :, :].rearrange("p t (h j) -> p t h j", j=HD),
                        vs[o][:, :, :].rearrange("p t (h j) -> p t h j", j=HD),
                        sc[o][:, :].rearrange("p (t h) -> p t h", h=HEADS).unsqueeze(3).to_broadcast(
                            [P, EH, HEADS, HD]),
                        ALU.mult).then_inc(g_done, 1)
                    join(m, o, ch, 3, 0)
                if here(n):
                    vec.wait_ge(kv, n + 1)
                    if here(n + 2):
                        ch2.wait()
                        set_index(n + 2, b)

            vec.memset(hT[D:D + 1, :], 1.0)
            vec.memset(acc[1][:, EH - 1, :], 0.0)
            for b in range(2):
                vec.memset(tg[b][:, :, :], 0.0)
                vec.memset(ef[b][:, :, :], 0.0)
                set_index(b, b)
            vec.drain().then_inc(zeroed, 1)
            vec.wait_ge(zeroed, 1)
            turns(vec, body, 1)
            vec.wait_ge(acc_done, T)
            vec.tensor_copy(s["acc_end"][:, :], acc[1][:, EH - 1, :]).then_inc(ended, 1)


def hop_next(nc, s, dram, hop):
    keep = hop < HOPS - 1
    with ExitStack() as ctx:
        def sb(name, shape, dt=F32):
            return ctx.enter_context(nc.sbuf_tensor(f"n{hop}_{name}", shape, dt))

        def two(name, shape, dt=F32):
            return [sb(f"{name}{b}", shape, dt) for b in range(2)]

        def sem(name):
            return ctx.enter_context(nc.semaphore(f"n{hop}_{name}"))

        mg = [sb(f"state{b}", [P, EH, MW]) for b in range(R)]
        pr = two("product", [P, EH, MW])
        acc = [sb(f"acc{b}", [P, EH, MW]) for b in range(R)] if keep else None
        g, ix = two("g", [P, EH, D]), [sb(f"slot_now{b}", [P, EH], I32) for b in range(R)]
        pg = [ctx.enter_context(nc.psum_tensor(f"n{hop}_heads{b}", [P, 512], F32)) for b in range(R)]
        row_in = s["row_in"]

        def rows_in(n, b):
            return 16 * EH * units_in(b) * hop + with_unit(n, b, 16 * EH)

        stored = [sem(f"stored{b}") for b in range(R)] if keep else None
        g_kept = [sem(f"g_kept{b}") for b in range(2)]
        idx_set, weighted, multiplied, headed = sem("idx_set"), sem("weighted"), sem("multiplied"), sem("headed")
        acc_done, g_done, zeroed = sem("acc_done"), sem("g_done"), sem("zeroed")
        note_p, note_s = sem("note_p"), sem("note_s")
        extra, ended = sem("extra"), sem("ended")
        block = ctx.enter_context(nc.Block())

        @block.sync
        def _(sync):
            def body(n, b):
                if keep and here(n):
                    passed(sync, acc_done, EH * (n + 1), note_s)
                    sync.dma_start(state_rows(dram[f"M{hop}"], n), acc[b][:, :, :]).then_inc(stored[b], 16)
                m, o = n - 2, b % 2
                if here(m):
                    passed(sync, g_done, m + 1, note_s)
                    sync.dma_start(dram["g"][hop][:, edge_cols(m), :], g[o][:, :, :]).then_inc(g_kept[o], 16)

            turns(sync, body, 2, R)
            for b in range(R if keep else 0):
                sync.wait_ge(stored[b], 16 * units_in(b))
            for b in range(2):
                sync.wait_ge(g_kept[b], 16 * NG)

        @block.gpsimd
        def _(pool):
            top = pool.to_reg(SLOTS - 1)

            def body(n, b):
                passed(pool, idx_set, n + 1, note_p)
                passed(pool, multiplied, EH * (n - R + 1), note_p)
                if keep:
                    passed(pool, acc_done, EH * (n - R + 1), note_p)
                for k in range(EH):
                    pool.indirect_dma_start(
                        out=mg[b][0:EP, k, :], out_offset=None, in_=dram[f"M{hop - 1}"],
                        in_offset=bass.IndirectOffsetOnAxis(ap=ix[b][0:EP, k:k + 1], axis=0),
                        bounds_check=top, oob_is_err=False).then_inc(row_in[b], 16)

            turns(pool, body, 0, R)

        @block.scalar
        def _(act):
            def body(n, b):
                if here(n):
                    act.wait_ge(row_in[b], rows_in(n, b))
                    for k in range(EH):
                        act.activation(mg[b][:, k:k + 1, :], mg[b][:, k:k + 1, :], ACT.Copy,
                                       scale=s["wn"][:, bass.ds(n * EH + k, 1)]).then_inc(weighted, 1)
                m, o, c = n - 2, b % 2, (b - 2) % R
                if here(m):
                    act.wait_ge(headed, m + 1)
                    wait(act, g_kept[o], 8 * (m - o))
                    if not keep:
                        act.wait_ge(extra, EH * (m + 1))
                    act.activation(g[o][:, :, :].rearrange("p t f -> p (t f)"), pg[c][:, 0:W],
                                   ACT.Copy).then_inc(g_done, 1)

            turns(act, body, 2, R)

        @block.tensor
        def _(ten):
            def body(n, b):
                ten.wait_ge(multiplied, EH * (n + 1))
                wait(ten, g_done, n - R + 1)
                for r in range(HD):
                    part = pr[b % 2][:, :, :].rearrange("p t (h i j) -> p (t h) i j", h=HEADS, i=HD)[:, :, r, :]
                    ins = ten.matmul(pg[b][:, 0:W].rearrange("p (c j) -> p c j", j=HD), s["ident"][:, :], part,
                                     start=(r == 0), stop=(r == HD - 1))
                ins.then_inc(headed, 1)

            turns(ten, body, 0, R)

        @block.vector
        def _(vec):
            def set_index(m, b):
                vec.tensor_copy(ix[b][:, :], s["sidx"][:, edge_cols(m)]).then_inc(idx_set, 1)

            def body(n, b):
                if here(n):
                    wait(vec, headed, n - 1)
                    h = b % 2
                    if keep:
                        wait(vec, stored[b], before_unit(n, b, 16))
                    for k in range(EH):
                        t = n * EH + k
                        vec.wait_ge(weighted, EH * n + k + 1)
                        if keep:
                            before = acc[b][:, k - 1, :] if k else acc[(b - 1) % R][:, EH - 1, :]
                            wait(vec, acc_done, EH * n + k)
                            vec.scalar_tensor_tensor(acc[b][:, k, :], before, s["same"][:, bass.ds(t, 1)],
                                                     mg[b][:, k, :], ALU.mult, ALU.add).then_inc(acc_done, 1)
                        vec.tensor_tensor(
                            ihj(pr[h][:, k, :]), ihj(mg[b][:, k, :]),
                            over_j(s["Q"][:, bass.ds(t, 1), :].rearrange("p t f -> p (t f)")),
                            ALU.mult).then_inc(multiplied, 1)
                        if k == 0 and here(n + 3):
                            set_index(n + 3, (b + 3) % R)
                m, o = n - 1, (b - 1) % R
                if not keep and here(m):
                    vec.wait_ge(headed, m + 1)
                    for k in range(EH):
                        wait(vec, extra, EH * m + k)
                        gx = s["gx"][:, hop, :]
                        vec.scalar_tensor_tensor(gx, pg[o][:, k * D:(k + 1) * D],
                                                 s["first"][:, bass.ds(m * EH + k, 1)], gx,
                                                 ALU.mult, ALU.add).then_inc(extra, 1)

            if keep:
                vec.memset(acc[R - 1][:, EH - 1, :], 0.0).then_inc(zeroed, 1)
            for b in range(R):
                vec.memset(mg[b][:, :, :], 0.0).then_inc(zeroed, 1)
                if b < R - 1:
                    set_index(b, b)
            vec.wait_ge(zeroed, R + keep)
            turns(vec, body, 1, R)
            if keep:
                vec.wait_ge(acc_done, T)
                vec.tensor_copy(s["acc_end"][:, :], acc[(UNITS - 1) % R][:, EH - 1, :]).then_inc(ended, 1)


def hop_end(nc, s, dram, hop):
    with ExitStack() as ctx:
        def sb(name, shape, dt=F32):
            return ctx.enter_context(nc.sbuf_tensor(f"e{hop}_{name}", shape, dt))

        def sem(name):
            return ctx.enter_context(nc.semaphore(f"e{hop}_{name}"))

        row, prod = sb("first_state", [P, MW]), sb("first_product", [P, MW])
        pc = ctx.enter_context(nc.psum_tensor(f"e{hop}_carry", [P, 512], F32))
        carried, got, fixed, put, v, zeroed = (sem("carried"), sem("got"), sem("fixed"), sem("put"), sem("steps"),
                                               sem("zeroed"))
        block = ctx.enter_context(nc.Block())

        @block.tensor
        def _(ten):
            ten.matmul(pc[:, :], s["carry"][:, :], s["acc_end"][:, :], start=True, stop=True).then_inc(carried, 1)

        @block.gpsimd
        def _(pool):
            top = pool.to_reg(SLOTS - 1)
            slot = bass.IndirectOffsetOnAxis(ap=s["slot_x"][0:EP, 0:1], axis=0)
            pool.wait_ge(zeroed, 1)
            pool.indirect_dma_start(out=row[0:EP, :], out_offset=None, in_=dram[f"M{hop}"], in_offset=slot,
                                    bounds_check=top, oob_is_err=False).then_inc(got, 16)
            pool.wait_ge(fixed, 1)
            pool.indirect_dma_start(out=dram[f"M{hop}"], out_offset=slot, in_=row[0:EP, :], in_offset=None,
                                    bounds_check=top, oob_is_err=False).then_inc(put, 16)
            pool.wait_ge(put, 16)

        @block.vector
        def _(vec):
            vec.memset(row[:, :], 0.0).then_inc(zeroed, 1)
            vec.wait_ge(carried, 1)
            vec.wait_ge(got, 16)
            vec.wait_ge(zeroed, 1)
            vec.tensor_tensor(row[:, :], row[:, :], pc[:, :], ALU.add).then_inc(fixed, 1)
            vec.wait_ge(fixed, 1)
            vec.tensor_tensor(ihj(prod[:, :]), ihj(row[:, :]), over_j(s["Q"][:, 0, :]), ALU.mult).then_inc(v, 1)
            vec.wait_ge(v, 1)
            vec.tensor_reduce(s["gx"][:, hop, :], prod[:, :].rearrange("p (h i j) -> p h j i", h=HEADS, i=HD),
                              AX.X, ALU.add).then_inc(v, 1)


def write_out(nc, s, dram, out):
    with ExitStack() as ctx:
        def sb(name, shape, dt=F32):
            return ctx.enter_context(nc.sbuf_tensor(f"o_{name}", shape, dt))

        def ring(name, shape, dt=F32):
            return [sb(f"{name}{b}", shape, dt) for b in range(R)]

        def sem(name):
            return ctx.enter_context(nc.semaphore(f"o_{name}"))

        NH = HOPS * EH * HEADS
        XH = HOPS * HEADS
        base, gg, sq = ring("base", [P, EH, D]), ring("g", [P, HOPS, EH, D]), ring("squares", [P, NH, HD])
        q, row, ix = ring("norms", [P, 4, NH]), ring("rows", [P, EH, D]), ring("dst", [P, EH], I32)
        fac = sb("factors", [P, NH])
        xs, xq, xf = sb("x_squares", [P, XH, HD]), sb("x_norms", [P, 4, XH]), sb("x_factors", [P, XH])
        psr = [ctx.enter_context(nc.psum_tensor(f"o_p_rows{b}", [P, 512], F32)) for b in range(2)]
        pc = ctx.enter_context(nc.psum_tensor("o_carry", [P, 512], F32))
        loaded, base_in, put = ([sem(f"{n}{b}") for b in range(R)] for n in ("loaded", "base_in", "put"))
        chained, squared, clamped, rooted, scaled, added = (sem("chained"), sem("squared"), sem("clamped"),
                                                            sem("rooted"), sem("scaled"), sem("added"))
        rows_set, idx_set, steps, reduced = sem("rows_set"), sem("idx_set"), sem("steps"), sem("reduced")
        note_p, note_s = sem("note_p"), sem("note_s")
        prep, x_steps, x_act, x_pe, x_put = sem("prep"), sem("x_steps"), sem("x_act"), sem("x_pe"), sem("x_put")
        block = ctx.enter_context(nc.Block())

        @block.sync
        def _(sync):
            def body(n, b):
                passed(sync, scaled, n - R + 1, note_s)
                passed(sync, chained, EH * (n - R + 1) + 1, note_s)
                for k in range(HOPS):
                    sync.dma_start(gg[b][:, k, :, :], dram["g"][k][:, edge_cols(n), :]).then_inc(loaded[b], 16)
                passed(sync, added, n - R + 1, note_s)
                sync.dma_start(base[b][:, :, :], dram["base"][:, edge_cols(n), :]).then_inc(base_in[b], 16)

            sync.wait_ge(prep, 1 + 2 * HOPS)
            turns(sync, body, 0, R)

        @block.gpsimd
        def _(pool):
            top = pool.to_reg(N - 1)

            def body(m, b):
                passed(pool, rows_set, m + 1, note_p)
                passed(pool, idx_set, m + 1, note_p)
                for k in range(EH):
                    pool.indirect_dma_start(
                        out=out, out_offset=bass.IndirectOffsetOnAxis(ap=ix[b][0:EP, k:k + 1], axis=0),
                        in_=row[b][0:EP, k, :], in_offset=None,
                        bounds_check=top, oob_is_err=False).then_inc(put[b], 16)

            turns(pool, body, 0, R)
            pool.wait_ge(x_steps, X_STEPS)
            pool.indirect_dma_start(out=out, out_offset=bass.IndirectOffsetOnAxis(ap=s["dst_x"][0:EP, 0:1], axis=0),
                                    in_=s["xbase"][0:EP, :], in_offset=None,
                                    bounds_check=top, oob_is_err=False).then_inc(x_put, 16)
            for b in range(R):
                pool.wait_ge(put[b], 16 * EH * units_in(b))
            pool.wait_ge(x_put, 16)

        @block.scalar
        def _(act):
            def body(n, b):
                m, c = n - 1, (b - 1) % R
                if here(m):
                    act.wait_ge(clamped, m + 1)
                    act.activation(q[c][:, 1, :], q[c][:, 0, :], ACT.Sqrt).then_inc(rooted, 1)
                m, c = n - 3, (b - 3) % R
                if here(m):
                    act.wait_ge(added, m + 1)
                    wait(act, put[c], before_unit(m, c, 16 * EH))
                    act.activation(row[c][:, :, :].rearrange("p t f -> p (t f)"), psr[c % 2][:, 0:W],
                                   ACT.Copy).then_inc(rows_set, 1)
                if here(n):
                    act.wait_ge(chained, EH * (n + 1))
                    act.activation(sq[b][:, :, :].rearrange("p c j -> p (c j)"),
                                   gg[b][:, :, :, :].rearrange("p c t f -> p (c t f)"), ACT.Square).then_inc(squared, 1)

            turns(act, body, 3, R)
            act.wait_ge(x_steps, 1)
            act.activation(xs[:, :, :], s["gx"][:, :, :].rearrange("p k (h j) -> p (k h) j", j=HD),
                           ACT.Square).then_inc(x_act, 1)
            act.wait_ge(x_steps, 3)
            act.activation(xq[:, 1, :], xq[:, 0, :], ACT.Sqrt).then_inc(x_act, 1)

        @block.tensor
        def _(ten):
            def body(m, b):
                ten.wait_ge(base_in[b], with_unit(m, b, 16))
                ten.wait_ge(scaled, m + 1)
                wait(ten, rows_set, m - 1)
                ten.matmul(psr[b % 2][:, 0:W], s["ident"][:, :], base[b][:, :, :].rearrange("p t f -> p (t f)"),
                           start=True, stop=False)
                for k in range(HOPS):
                    ins = ten.matmul(psr[b % 2][:, 0:W], s["ident"][:, :],
                                     sq[b][:, :, :].rearrange("p (k c) j -> p k (c j)", k=HOPS)[:, k, :],
                                     start=False, stop=(k == HOPS - 1))
                ins.then_inc(added, 1)

            turns(ten, body, 0, R)
            ten.wait_ge(chained, T)
            ten.matmul(pc[:, 0:D], s["carry"][:, :], gg[(UNITS - 1) % R][:, HOPS - 1, EH - 1, :],
                       start=True, stop=True).then_inc(x_pe, 1)

        @block.vector
        def _(vec):
            def body(n, b):
                if here(n):
                    vec.wait_ge(loaded[b], with_unit(n, b, 16 * HOPS))

                def chain(k):
                    if here(n):
                        before = gg[b][:, :, k - 1, :] if k else gg[(b - 1) % R][:, :, EH - 1, :]
                        wait(vec, chained, EH * n + k)
                        vec.scalar_tensor_tensor(gg[b][:, :, k, :], before, s["same"][:, bass.ds(n * EH + k, 1)],
                                                 gg[b][:, :, k, :], ALU.mult, ALU.add).then_inc(chained, 1)

                chain(0)
                m, c = n - 2, (b - 2) % R
                if here(m):
                    vec.wait_ge(rooted, m + 1)
                    old = Chain(vec, steps, m, 2)
                    old.step(vec.reciprocal(q[c][:, 2, :], q[c][:, 1, :]))
                chain(1)
                if here(m):
                    old.wait()
                    old.step(vec.tensor_tensor(q[c][:, 3, :], q[c][:, 2, :], fac[:, :], ALU.mult))
                m2, c2 = n - 1, (b - 1) % R
                if here(m2):
                    vec.wait_ge(squared, m2 + 1)
                    vec.tensor_reduce(q[c2][:, 2, :], sq[c2][:, :, :], AX.X, ALU.add).then_inc(reduced, 1)
                chain(2)
                if here(m):
                    old.wait()
                    vec.tensor_tensor(sq[c][:, :, :], gg[c][:, :, :, :].rearrange("p k t (h j) -> p (k t h) j", j=HD),
                                      q[c][:, 3, :].unsqueeze(2).to_broadcast([P, NH, HD]), ALU.mult).then_inc(scaled, 1)
                if here(m2):
                    vec.wait_ge(reduced, m2 + 1)
                    vec.tensor_scalar(q[c2][:, 0, :], q[c2][:, 2, :], 1.0 / HD, 1.0,
                                      ALU.mult, ALU.max).then_inc(clamped, 1)
                chain(3)
                if here(m):
                    wait(vec, put[c], before_unit(m, c, 16 * EH))
                    vec.tensor_copy(ix[c][:, :], s["dst_out"][:, edge_cols(m)]).then_inc(idx_set, 1)

            vec.memset(gg[R - 1][:, :, EH - 1, :], 0.0).then_inc(prep, 1)
            for k in range(HOPS):
                c = slice(k * EH * HEADS, (k + 1) * EH * HEADS)
                factor = s["hop"][:, k + 1:k + 2]
                vec.tensor_copy(fac[:, c], factor.to_broadcast([P, EH * HEADS])).then_inc(prep, 1)
                vec.tensor_copy(xf[:, k * HEADS:(k + 1) * HEADS], factor.to_broadcast([P, HEADS])).then_inc(prep, 1)
            vec.wait_ge(prep, 1 + 2 * HOPS)
            turns(vec, body, 2, R)
            n = [0]

            def step(ins):
                ins.then_inc(x_steps, 1)
                n[0] += 1
                vec.wait_ge(x_steps, n[0])

            gx = s["gx"][:, HOPS - 1, :]
            vec.wait_ge(x_pe, 1)
            step(vec.tensor_tensor(gx, gx, pc[:, 0:D], ALU.add))
            vec.wait_ge(x_act, 1)
            step(vec.tensor_reduce(xq[:, 2, :], xs[:, :, :], AX.X, ALU.add))
            step(vec.tensor_scalar(xq[:, 0, :], xq[:, 2, :], 1.0 / HD, 1.0, ALU.mult, ALU.max))
            vec.wait_ge(x_act, 2)
            step(vec.reciprocal(xq[:, 2, :], xq[:, 1, :]))
            step(vec.tensor_tensor(xq[:, 3, :], xq[:, 2, :], xf[:, :], ALU.mult))
            step(vec.tensor_tensor(xs[:, :, :], s["gx"][:, :, :].rearrange("p k (h j) -> p (k h) j", j=HD),
                                   xq[:, 3, :].unsqueeze(2).to_broadcast([P, XH, HD]), ALU.mult))
            for k in range(HOPS):
                step(vec.tensor_tensor(s["xbase"][:, :], s["xbase"][:, :],
                                       xs[:, k * HEADS:(k + 1) * HEADS, :].rearrange("p c j -> p (c j)"), ALU.add))
            assert n[0] == X_STEPS


INPUTS = ["x", "src", "dst", "edge_attr_64", "edge_weight", "L0_gnn_W1", "L0_gnn_b1", "L0_gnn_W2", "L0_gnn_b2",
          "L1_gnn_Wq", "L1_gnn_bq", "L1_gnn_Wk", "L1_gnn_bk", "L1_gnn_Wv", "L1_gnn_bv", "L1_gnn_hopwise"]


def kernel(**inputs):
    import concourse.bacc as bacc
    from concourse.bass_utils import run_bass_kernel_spmd

    nc = bacc.Bacc("TRN2", target_bir_lowering=False, num_devices=1)
    r, c = np.arange(P)[:, None], np.arange(P)[None, :]
    constants = {
        "mats": np.concatenate([r == c, c > r, r == c + 1], axis=1).astype(np.float32),
        "slots": (np.arange(T)[None, :] * P + r).astype(np.float32),
    }
    arrays, args = {}, []
    for name, a in [(n, inputs[n]) for n in INPUTS] + list(constants.items()):
        a = np.ascontiguousarray(a)
        arrays[f"in_{name}"] = a
        args.append(nc.dram_tensor(f"in_{name}", a.shape, mybir.dt.from_np(a.dtype), kind="ExternalInput").ap())
    args.append(nc.dram_tensor("out", (N, D), F32, kind="ExternalOutput").ap())
    gnn(nc, *args)
    r = run_bass_kernel_spmd(nc, [arrays], core_ids=[0])
    return r.results[0]["out"]
```
